# Optimizing a Trainium2 kernel written in Bass

```python
import numpy as np
import jax
import jax.numpy as jnp

def _softmax(x, axis=-1):
    return jax.nn.softmax(x, axis=axis)

def _gelu(x):
    return jax.nn.gelu(x, approximate=True)

def _silu(x):
    return jax.nn.silu(x)

def _sigmoid(x):
    return jax.nn.sigmoid(x)

def _layernorm(x, axis=-1, eps=1e-05):
    m = jnp.mean(x, axis=axis, keepdims=True)
    v = jnp.var(x, axis=axis, keepdims=True)
    return (x - m) / jnp.sqrt(v + eps)

def _scatter_add(tgt, idx, src, axis=0):
    return tgt.at[idx].add(src)

def _segment_sum(src, seg, n):
    return jax.ops.segment_sum(src, seg, n)
kernel_name = 'mk_seq_preln_d1_jaxref_r8_d9fec9'

def setup_inputs(seed: int=0):
    np.random.seed(seed)
    _w = jnp.asarray

    def _L0_attn_setup():
        import jax, jax.numpy as jnp
        import numpy as np
        import math
        B, L, F, N, EXP = (2, 128, 128, 16, 1)
        FI = int(F * EXP)
        ND = math.ceil(F / 16)
        EPS = 1e-05

        def _lin_init(k, o, i):
            s = 1.0 / np.sqrt(i)
            kw, kb = jax.random.split(k)
            W = jax.random.uniform(kw, (o, i), jnp.float32, -s, s)
            b = jax.random.uniform(kb, (o,), jnp.float32, -s, s)
            return (W, b)

        def _norm(x, axes):
            mu = x.mean(axes, keepdims=True)
            var = ((x - mu) ** 2).mean(axes, keepdims=True)
            return (x - mu) * jax.lax.rsqrt(var + EPS)
        key = jax.random.key(seed)
        ks = jax.random.split(key, 10)
        w_in, b_in = _lin_init(ks[0], FI, F)
        cs = 1.0 / np.sqrt(FI * 3)
        conv_w = jax.random.uniform(ks[1], (FI, FI, 3), jnp.float32, -cs, cs)
        conv_b = jax.random.uniform(ks[2], (FI,), jnp.float32, -cs, cs)
        A_log = jnp.log(jnp.tile(jnp.arange(1, N + 1, dtype=jnp.float32)[None, :], (FI, 1)))
        D = jnp.ones((FI,), jnp.float32)
        w_B, b_B = _lin_init(ks[3], N, FI)
        w_C, b_C = _lin_init(ks[4], N, FI)
        w_d1, b_d1 = _lin_init(ks[5], ND, FI)
        w_d2, b_d2 = _lin_init(ks[6], FI, ND)
        w_out, b_out = _lin_init(ks[7], F, FI)
        x = jax.random.normal(ks[8], (B, L, F), jnp.float32)
        return dict(x=x, w_in=w_in, b_in=b_in, conv_w=conv_w, conv_b=conv_b, A_log=A_log, D=D, w_B=w_B, b_B=b_B, w_C=w_C, b_C=b_C, w_d1=w_d1, b_d1=b_d1, w_d2=w_d2, b_d2=b_d2, w_out=w_out, b_out=b_out)
    _L0_attn_in = _L0_attn_setup()

    def _L0_ffn_setup():
        import jax, jax.numpy as jnp
        import numpy as np
        B, S, D = (2, 128, 128)
        H, HD = (16, 64)
        E_R = 31
        K_ACT = 3
        INTER = 128
        EPS = 1e-05
        BASE = 10000.0

        def _rmsnorm(x, gamma):
            rms = jnp.sqrt(jnp.mean(x * x, axis=-1, keepdims=True) + EPS)
            return x / rms * gamma

        def _rope(x, theta):
            seq = x.shape[2]
            angles = jnp.arange(seq, dtype=theta.dtype)[:, None] * theta
            cos = jnp.cos(angles)[None, None]
            sin = jnp.sin(angles)[None, None]
            x1, x2 = (x[..., 0::2], x[..., 1::2])
            return jnp.concatenate([x1 * cos - x2 * sin, x1 * sin + x2 * cos], axis=-1)

        def _forward(x, theta, gamma1, gamma2, q_w, q_b, k_w, k_b, v_w, v_b, o_w, o_b, router_w, router_b, sh_w1, sh_b1, sh_w2, sh_b2, re_w1, re_b1, re_w2, re_b2):
            b, s, d = x.shape
            xn = _rmsnorm(x, gamma1)
            q = (xn @ q_w + q_b).reshape(b, s, H, HD).transpose(0, 2, 1, 3)
            k = (xn @ k_w + k_b).reshape(b, s, H, HD).transpose(0, 2, 1, 3)
            v = (xn @ v_w + v_b).reshape(b, s, H, HD).transpose(0, 2, 1, 3)
            q = _rope(q, theta)
            k = _rope(k, theta)
            scale = 1.0 / np.sqrt(HD)
            scores = jnp.einsum('bhqd,bhkd->bhqk', q, k) * scale
            causal = jnp.tril(jnp.ones((s, s), dtype=bool))
            scores = jnp.where(causal, scores, -jnp.inf)
            attn = jax.nn.softmax(scores, axis=-1)
            ctx = jnp.einsum('bhqk,bhkd->bhqd', attn, v)
            ctx = ctx.transpose(0, 2, 1, 3).reshape(b, s, H * HD)
            attn_out = ctx @ o_w + o_b + xn
            an = _rmsnorm(attn_out, gamma2)
            shared = jax.nn.gelu(an @ sh_w1 + sh_b1, approximate=False) @ sh_w2 + sh_b2
            logits = an @ router_w + router_b
            aff = jax.nn.softmax(logits, axis=-1)
            topv, topi = jax.lax.top_k(aff, K_ACT)
            gates = jnp.sum(jax.nn.one_hot(topi, E_R, dtype=aff.dtype) * topv[..., None], axis=-2)
            h = jax.nn.gelu(jnp.einsum('bsd,edh->besh', an, re_w1) + re_b1[None, :, None, :], approximate=False)
            routed = jnp.einsum('bse,besh,ehd->bsd', gates, h, re_w2) + jnp.einsum('bse,ed->bsd', gates, re_b2)
            return shared + routed + an + attn_out
        key = jax.random.key(seed)
        ks = jax.random.split(key, 24)
        s = 0.02
        theta = BASE ** (-jnp.arange(HD // 2, dtype=jnp.float32) * 2.0 / HD)
        inp = {'x': jax.random.normal(ks[0], (B, S, D), jnp.float32), 'positions': jnp.arange(S, dtype=jnp.int32), 'theta': theta, 'gamma1': jnp.ones((D,), jnp.float32), 'gamma2': jnp.ones((D,), jnp.float32), 'q_w': jax.random.normal(ks[1], (D, H * HD), jnp.float32) * s, 'q_b': jnp.zeros((H * HD,), jnp.float32), 'k_w': jax.random.normal(ks[2], (D, H * HD), jnp.float32) * s, 'k_b': jnp.zeros((H * HD,), jnp.float32), 'v_w': jax.random.normal(ks[3], (D, H * HD), jnp.float32) * s, 'v_b': jnp.zeros((H * HD,), jnp.float32), 'o_w': jax.random.normal(ks[4], (H * HD, D), jnp.float32) * s, 'o_b': jnp.zeros((D,), jnp.float32), 'router_w': jax.random.normal(ks[5], (D, E_R), jnp.float32) * s, 'router_b': jnp.zeros((E_R,), jnp.float32), 'sh_w1': jax.random.normal(ks[6], (D, INTER), jnp.float32) * s, 'sh_b1': jnp.zeros((INTER,), jnp.float32), 'sh_w2': jax.random.normal(ks[7], (INTER, D), jnp.float32) * s, 'sh_b2': jnp.zeros((D,), jnp.float32), 're_w1': jax.random.normal(ks[8], (E_R, D, INTER), jnp.float32) * s, 're_b1': jnp.zeros((E_R, INTER), jnp.float32), 're_w2': jax.random.normal(ks[9], (E_R, INTER, D), jnp.float32) * s, 're_b2': jnp.zeros((E_R, D), jnp.float32)}
        return inp
    _L0_ffn_in = _L0_ffn_setup()
    _d = {'L0_attn_x': _L0_attn_in['x'], 'L0_attn_w_in': _L0_attn_in['w_in'], 'L0_attn_b_in': _L0_attn_in['b_in'], 'L0_attn_conv_w': _L0_attn_in['conv_w'], 'L0_attn_conv_b': _L0_attn_in['conv_b'], 'L0_attn_A_log': _L0_attn_in['A_log'], 'L0_attn_D': _L0_attn_in['D'], 'L0_attn_w_B': _L0_attn_in['w_B'], 'L0_attn_b_B': _L0_attn_in['b_B'], 'L0_attn_w_C': _L0_attn_in['w_C'], 'L0_attn_b_C': _L0_attn_in['b_C'], 'L0_attn_w_d1': _L0_attn_in['w_d1'], 'L0_attn_b_d1': _L0_attn_in['b_d1'], 'L0_attn_w_d2': _L0_attn_in['w_d2'], 'L0_attn_b_d2': _L0_attn_in['b_d2'], 'L0_attn_w_out': _L0_attn_in['w_out'], 'L0_attn_b_out': _L0_attn_in['b_out'], 'L0_ffn_positions': _L0_ffn_in['positions'], 'L0_ffn_theta': _L0_ffn_in['theta'], 'L0_ffn_gamma1': _L0_ffn_in['gamma1'], 'L0_ffn_gamma2': _L0_ffn_in['gamma2'], 'L0_ffn_q_w': _L0_ffn_in['q_w'], 'L0_ffn_q_b': _L0_ffn_in['q_b'], 'L0_ffn_k_w': _L0_ffn_in['k_w'], 'L0_ffn_k_b': _L0_ffn_in['k_b'], 'L0_ffn_v_w': _L0_ffn_in['v_w'], 'L0_ffn_v_b': _L0_ffn_in['v_b'], 'L0_ffn_o_w': _L0_ffn_in['o_w'], 'L0_ffn_o_b': _L0_ffn_in['o_b'], 'L0_ffn_router_w': _L0_ffn_in['router_w'], 'L0_ffn_router_b': _L0_ffn_in['router_b'], 'L0_ffn_sh_w1': _L0_ffn_in['sh_w1'], 'L0_ffn_sh_b1': _L0_ffn_in['sh_b1'], 'L0_ffn_sh_w2': _L0_ffn_in['sh_w2'], 'L0_ffn_sh_b2': _L0_ffn_in['sh_b2'], 'L0_ffn_re_w1': _L0_ffn_in['re_w1'], 'L0_ffn_re_b1': _L0_ffn_in['re_b1'], 'L0_ffn_re_w2': _L0_ffn_in['re_w2'], 'L0_ffn_re_b2': _L0_ffn_in['re_b2']}
    _x0 = _d['L0_attn_x']
    _d['L0_attn_x'] = jax.random.normal(jax.random.fold_in(jax.random.key(seed), 1), (4, 1024, 128), dtype=_x0.dtype)
    del _x0
    return _d

def reference(L0_attn_x, L0_attn_w_in, L0_attn_b_in, L0_attn_conv_w, L0_attn_conv_b, L0_attn_A_log, L0_attn_D, L0_attn_w_B, L0_attn_b_B, L0_attn_w_C, L0_attn_b_C, L0_attn_w_d1, L0_attn_b_d1, L0_attn_w_d2, L0_attn_b_d2, L0_attn_w_out, L0_attn_b_out, L0_ffn_positions, L0_ffn_theta, L0_ffn_gamma1, L0_ffn_gamma2, L0_ffn_q_w, L0_ffn_q_b, L0_ffn_k_w, L0_ffn_k_b, L0_ffn_v_w, L0_ffn_v_b, L0_ffn_o_w, L0_ffn_o_b, L0_ffn_router_w, L0_ffn_router_b, L0_ffn_sh_w1, L0_ffn_sh_b1, L0_ffn_sh_w2, L0_ffn_sh_b2, L0_ffn_re_w1, L0_ffn_re_b1, L0_ffn_re_w2, L0_ffn_re_b2):

    def _L0_attn_ref(x, w_in, b_in, conv_w, conv_b, A_log, D, w_B, b_B, w_C, b_C, w_d1, b_d1, w_d2, b_d2, w_out, b_out):
        import jax, jax.numpy as jnp
        import numpy as np
        import math
        B, L, F, N, EXP = (2, 128, 128, 16, 1)
        FI = int(F * EXP)
        ND = math.ceil(F / 16)
        EPS = 1e-05

        def _lin_init(k, o, i):
            s = 1.0 / np.sqrt(i)
            kw, kb = jax.random.split(k)
            W = jax.random.uniform(kw, (o, i), jnp.float32, -s, s)
            b = jax.random.uniform(kb, (o,), jnp.float32, -s, s)
            return (W, b)

        def _norm(x, axes):
            mu = x.mean(axes, keepdims=True)
            var = ((x - mu) ** 2).mean(axes, keepdims=True)
            return (x - mu) * jax.lax.rsqrt(var + EPS)
        x0 = x
        h = _norm(x, (1, 2)) @ w_in.T + b_in
        h0 = h
        hc = jnp.transpose(h, (0, 2, 1))
        hc = jax.lax.conv_general_dilated(hc, conv_w, (1,), [(1, 1)], dimension_numbers=('NCH', 'OIH', 'NCH'))
        hc = hc + conv_b[None, :, None]
        hc = jax.nn.silu(_norm(hc, (2,)))
        h = jnp.transpose(hc, (0, 2, 1))
        A = jnp.exp(A_log)
        Bm = h @ w_B.T + b_B
        Cm = h @ w_C.T + b_C
        Delta = jax.nn.softplus((h @ w_d1.T + b_d1) @ w_d2.T + b_d2)
        A_bar = jnp.exp(-Delta[..., None] * A)
        BX = (Delta * h)[..., None] * Bm[:, :, None, :]

        def comb(c1, c2):
            a1, b1 = c1
            a2, b2 = c2
            return (a1 * a2, a2 * b1 + b2)
        _, states = jax.lax.associative_scan(comb, (A_bar, BX), axis=1)
        y = jnp.einsum('blfn,bln->blf', states, Cm) + D * h
        g = y * jax.nn.silu(h0)
        out = _norm(g, (2,)) @ w_out.T + b_out + x0
        return out

    def _L0_ffn_ref(x, positions, theta, gamma1, gamma2, q_w, q_b, k_w, k_b, v_w, v_b, o_w, o_b, router_w, router_b, sh_w1, sh_b1, sh_w2, sh_b2, re_w1, re_b1, re_w2, re_b2):
        import jax, jax.numpy as jnp
        import numpy as np
        B, S, D = (2, 128, 128)
        H, HD = (16, 64)
        E_R = 31
        K_ACT = 3
        INTER = 128
        EPS = 1e-05
        BASE = 10000.0

        def _rmsnorm(x, gamma):
            rms = jnp.sqrt(jnp.mean(x * x, axis=-1, keepdims=True) + EPS)
            return x / rms * gamma

        def _rope(x, theta):
            seq = x.shape[2]
            angles = jnp.arange(seq, dtype=theta.dtype)[:, None] * theta
            cos = jnp.cos(angles)[None, None]
            sin = jnp.sin(angles)[None, None]
            x1, x2 = (x[..., 0::2], x[..., 1::2])
            return jnp.concatenate([x1 * cos - x2 * sin, x1 * sin + x2 * cos], axis=-1)

        def _forward(x, theta, gamma1, gamma2, q_w, q_b, k_w, k_b, v_w, v_b, o_w, o_b, router_w, router_b, sh_w1, sh_b1, sh_w2, sh_b2, re_w1, re_b1, re_w2, re_b2):
            b, s, d = x.shape
            xn = _rmsnorm(x, gamma1)
            q = (xn @ q_w + q_b).reshape(b, s, H, HD).transpose(0, 2, 1, 3)
            k = (xn @ k_w + k_b).reshape(b, s, H, HD).transpose(0, 2, 1, 3)
            v = (xn @ v_w + v_b).reshape(b, s, H, HD).transpose(0, 2, 1, 3)
            q = _rope(q, theta)
            k = _rope(k, theta)
            scale = 1.0 / np.sqrt(HD)
            scores = jnp.einsum('bhqd,bhkd->bhqk', q, k) * scale
            causal = jnp.tril(jnp.ones((s, s), dtype=bool))
            scores = jnp.where(causal, scores, -jnp.inf)
            attn = jax.nn.softmax(scores, axis=-1)
            ctx = jnp.einsum('bhqk,bhkd->bhqd', attn, v)
            ctx = ctx.transpose(0, 2, 1, 3).reshape(b, s, H * HD)
            attn_out = ctx @ o_w + o_b + xn
            an = _rmsnorm(attn_out, gamma2)
            shared = jax.nn.gelu(an @ sh_w1 + sh_b1, approximate=False) @ sh_w2 + sh_b2
            logits = an @ router_w + router_b
            aff = jax.nn.softmax(logits, axis=-1)
            topv, topi = jax.lax.top_k(aff, K_ACT)
            gates = jnp.sum(jax.nn.one_hot(topi, E_R, dtype=aff.dtype) * topv[..., None], axis=-2)
            h = jax.nn.gelu(jnp.einsum('bsd,edh->besh', an, re_w1) + re_b1[None, :, None, :], approximate=False)
            routed = jnp.einsum('bse,besh,ehd->bsd', gates, h, re_w2) + jnp.einsum('bse,ed->bsd', gates, re_b2)
            return shared + routed + an + attn_out
        del positions
        return _forward(x, theta, gamma1, gamma2, q_w, q_b, k_w, k_b, v_w, v_b, o_w, o_b, router_w, router_b, sh_w1, sh_b1, sh_w2, sh_b2, re_w1, re_b1, re_w2, re_b2)
    x = L0_attn_x
    x = x + _L0_attn_ref(_layernorm(x, axis=-1), L0_attn_w_in, L0_attn_b_in, L0_attn_conv_w, L0_attn_conv_b, L0_attn_A_log, L0_attn_D, L0_attn_w_B, L0_attn_b_B, L0_attn_w_C, L0_attn_b_C, L0_attn_w_d1, L0_attn_b_d1, L0_attn_w_d2, L0_attn_b_d2, L0_attn_w_out, L0_attn_b_out)
    x = x + _L0_ffn_ref(_layernorm(x, axis=-1), L0_ffn_positions, L0_ffn_theta, L0_ffn_gamma1, L0_ffn_gamma2, L0_ffn_q_w, L0_ffn_q_b, L0_ffn_k_w, L0_ffn_k_b, L0_ffn_v_w, L0_ffn_v_b, L0_ffn_o_w, L0_ffn_o_b, L0_ffn_router_w, L0_ffn_router_b, L0_ffn_sh_w1, L0_ffn_sh_b1, L0_ffn_sh_w2, L0_ffn_sh_b2, L0_ffn_re_w1, L0_ffn_re_b1, L0_ffn_re_w2, L0_ffn_re_b2)
    return x

_drawn_inputs = setup_inputs


def setup_inputs(seed=0):
    import zlib

    import numpy as np

    out = dict(_drawn_inputs(seed))
    spreads = {'L0_attn_D': (1.0, 0.2),
     'L0_ffn_gamma1': (1.0, 0.2),
     'L0_ffn_gamma2': (1.0, 0.2),
     'L0_ffn_q_b': (0.0, 0.8),
     'L0_ffn_k_b': (0.0, 0.8),
     'L0_ffn_v_b': (0.0, 0.273),
     'L0_ffn_o_b': (0.0, 0.1),
     'L0_ffn_router_b': (0.0, 0.8),
     'L0_ffn_sh_b1': (0.0, 0.8),
     'L0_ffn_sh_b2': (0.0, 0.316),
     'L0_ffn_re_b1': (0.0, 0.8),
     'L0_ffn_re_b2': (0.0, 0.8)}
    factors = {'L0_attn_conv_b': 8.0,
     'L0_attn_A_log': 3.046,
     'L0_attn_b_B': 4.878,
     'L0_attn_b_C': 7.009,
     'L0_attn_b_d1': 8.0,
     'L0_ffn_theta': 8.0,
     'L0_ffn_q_w': 8.0,
     'L0_ffn_k_w': 8.0,
     'L0_ffn_v_w': 8.0,
     'L0_ffn_router_w': 8.0,
     'L0_ffn_sh_w1': 8.0,
     'L0_ffn_sh_w2': 7.775,
     'L0_ffn_re_w1': 8.0,
     'L0_ffn_re_w2': 8.0}
    for name, (base, spread) in spreads.items():
        noise = np.random.default_rng([zlib.crc32(name.encode()), seed]).standard_normal(out[name].shape)
        drawn = base * np.exp(spread * noise) if base else spread * noise
        out[name] = jnp.asarray(drawn.astype(out[name].dtype))
    for name, factor in factors.items():
        out[name] = (out[name] * factor).astype(out[name].dtype)
    return out
```

```python
from contextlib import ExitStack

import numpy as np

import concourse.bass as bass
from concourse import mybir

ALU = mybir.AluOpType
ACT = mybir.ActivationFunctionType
AX_X = mybir.AxisListType.X
F32 = mybir.dt.float32
F32R = mybir.dt.float32r
BF16 = mybir.dt.bfloat16

P = 128
BATCH, SEQ, DM = 4, 1024, 128
TILES = SEQ // P
HALF = 512
HALVES = SEQ // HALF
TPH = HALF // P
STATES = 16
DT_RANK = 8
HEADS, HD = 16, 64
PAIRS = HEADS // 2
EXPERTS = 32
ROUTED = 31
TOP = 3
SLOTS = 4
EPS = 1e-5
SCALE = HD ** -0.5
MASKED = -1e30
ENGINES = 5

C_B_IN, C_CONV_B, C_B_B, C_B_C, C_B_D1, C_B_D2, C_D, C_THETA, C_TURN, C_PHASE, C_SIGN = range(11)
C_ALOG = 11
C_B1 = C_ALOG + STATES
C_QK = C_B1 + EXPERTS
NCOLS = C_QK + 4 * PAIRS

TWO_PI_A = 6.28125
TWO_PI_B = float(np.float32(np.round((2 * np.pi - TWO_PI_A) * 2.0 ** 17) / 2.0 ** 17))
TWO_PI_C = float(np.float32(2 * np.pi - TWO_PI_A - TWO_PI_B))
ROUNDER = float(1.5 * 2 ** 23)
PI_BELOW = 3.1415925


def st_units():
    return [(c, j, max(P * j, HALF * c)) for c in range(HALVES) for j in range(TPH * (c + 1))]


def max_units():
    out = []
    for i in range(TILES):
        end = P * (i + 1)
        out.append((i, 0, min(end, HALF)))
        if end > HALF:
            out.append((i, HALF, end - HALF))
    return out


ST = st_units()
MX = max_units()
NU = len(ST)


def slots(do_prev, do_this):
    prev = [("st", 0, u) for u in range(NU)] + [("pv", 0, i) for i in range(TILES)]
    prev += [("st", 1, u) for u in range(NU)]
    for i in range(TILES):
        prev.append(("pv", 1, i))
        prev += {3: [("ct", 0, 0)], 5: [("op", 0, 0)], 7: [("ct", 1, 0), ("op", 1, 0)]}.get(i, [])
    mx = [("mx", h, u) for h in range(2) for u in range(NU)]
    out = []
    for k, s in enumerate(prev if do_prev else []):
        out.append(s)
        if do_this and k >= NU and mx:
            out.append(mx.pop(0))
    return out + (mx if do_this else [])


def program(nc, ins, out):
    with ExitStack() as ctx:
        def sb(name, shape, dt=F32, where=None):
            return (where or ctx).enter_context(nc.sbuf_tensor(name, shape, dt))

        def sem(name):
            return ctx.enter_context(nc.semaphore(name))

        ident = sb("ident", [P, P])
        identr = sb("identr", [P, P], F32R)
        identb = sb("identb", [P, P], BF16)
        masks32 = sb("masks32", [P, 2, P])
        masks = sb("masks", [P, 2, P], BF16)
        fold32 = sb("fold32", [96, 32])
        fold = sb("fold", [96, 32], BF16)
        mean_of = sb("mean_of", [P, P])
        diag_d = sb("diag_d", [P, P])
        neg_a = sb("neg_a", [P, STATES])
        exp_a = sb("exp_a", [P, STATES])
        neg_half = sb("neg_half", [P, TILES])
        cols = sb("cols", [P, NCOLS])
        cos_t = sb("cos_t", [P, SEQ])
        sin_t = sb("sin_t", [P, SEQ])
        w_in = sb("w_in", [P, P])
        w_conv = sb("w_conv", [P, 3, P])
        w_b3 = sb("w_b3", [P, 96])
        w_c3 = sb("w_c3", [P, 96])
        w_d1 = sb("w_d1", [P, DT_RANK])
        w_d2 = sb("w_d2", [DT_RANK, P])
        w_out = sb("w_out", [P, P])
        w_router = sb("w_router", [P, EXPERTS])
        b2_all = sb("b2_all", [EXPERTS, P])
        rows = sb("rows", [P, 4, P])
        router_b = sb("router_b", [P, EXPERTS])
        v_b = sb("v_b", [P, HEADS * HD])
        v_w = sb("v_w", [P, HEADS * HD])
        o_w = sb("o_w", [P, PAIRS, P])
        resets = sb("resets", [P, TILES * EXPERTS])
        b_out_r, gamma1_r, gamma2_r, o_b_r = (rows[:, i, :] for i in range(4))

        xin = sb("xin", [P, TILES, P])
        resid = sb("resid", [P, TILES, P])
        partial = sb("partial", [P, 2])
        glob = sb("glob", [P, 3])
        stats = sb("stats", [P, TILES, 6])
        mv = sb("mv", [P, TILES, 2])
        ms = sb("ms", [P, TILES])
        rstd = sb("rstd", [P, TILES])
        nmb = sb("nmb", [P, TILES])

        hpad = sb("hpad", [P, SEQ + 2])
        acc = sb("acc", [P, TILES, P], F32)
        vals = [sb(f"vals{i}", [P, TILES, 2, HD + 1], F32) for i in range(2)]
        q_max = [[sb(f"q_max{i}{h}", [P, SEQ], F32R) for h in range(2)] for i in range(2)]
        k_low = [[sb(f"k_low{i}{h}", [P, SEQ], F32R) for h in range(2)] for i in range(2)]

        m_ctx = ExitStack()
        x0 = sb("x0", [P, TILES, P], F32, m_ctx)
        xnT_m = sb("xnT_m", [P, SEQ], F32, m_ctx)
        gate = sb("gate", [P, SEQ], F32, m_ctx)
        hc = sb("hc", [P, SEQ], F32, m_ctx)
        h_act = sb("h_act", [P, SEQ], F32, m_ctx)
        bc32 = sb("bc32", [96, 2, SEQ], F32, m_ctx)
        bc_rest = sb("bc_rest", [96, SEQ], F32, m_ctx)
        bc_mid = sb("bc_mid", [96, SEQ], BF16, m_ctx)
        bc3 = sb("bc3", [96, 2, SEQ], BF16, m_ctx)
        d1 = sb("d1", [DT_RANK, SEQ], F32, m_ctx)
        z_abs = sb("z_abs", [P, SEQ], F32, m_ctx)
        z = sb("z", [P, SEQ], F32, m_ctx)
        sp_log = sb("sp_log", [P, SEQ], F32, m_ctx)
        delta = sb("delta", [P, SEQ], F32, m_ctx)
        du = sb("du", [P, SEQ], F32, m_ctx)
        decay = sb("decay", [P, 2, SEQ], F32, m_ctx)
        b_rows = sb("b_rows", [P, 2, SEQ], F32, m_ctx)
        bx = sb("bx", [P, 2, SEQ], F32, m_ctx)
        state = sb("state", [P, 2, SEQ], F32, m_ctx)
        cs = sb("cs", [P, 2, SEQ], F32, m_ctx)
        g_tok = sb("g_tok", [P, TILES, P], F32, m_ctx)
        gT = sb("gT", [P, SEQ], F32, m_ctx)
        m_ctx.close()

        a_ctx = ExitStack()
        xa = sb("xa", [P, TILES, P], F32, a_ctx)
        xnT = sb("xnT", [P, SEQ], F32, a_ctx)
        w_pair = [sb(f"w_pair{i}", [P, 4, P], F32, a_ctx) for i in range(2)]
        turned = sb("turned", [P, 4, SEQ], F32, a_ctx)
        roped = sb("roped", [P, 2, SEQ], F32, a_ctx)
        q_split = [[sb(f"q_split{i}{h}", [P, SEQ], F32R, a_ctx) for h in range(2)] for i in range(2)]
        k_high = [[sb(f"k_high{i}{h}", [P, SEQ], F32R, a_ctx) for h in range(2)] for i in range(2)]
        probs = sb("probs", [P, TPH + TILES, HALF], F32, a_ctx)
        tops = sb("tops", [P, 2, NU], F32, a_ctx)
        top_r = sb("top_r", [P, 2, TILES], F32R, a_ctx)
        sums = sb("sums", [P, TPH], F32, a_ctx)
        ctx_t = sb("ctx_t", [P, TILES, P], F32, a_ctx)
        ctxT = sb("ctxT", [P, HALF], F32, a_ctx)
        a_ctx.close()

        e_ctx = ExitStack()
        an = sb("an", [P, TILES, P], F32, e_ctx)
        anT = sb("anT", [P, SEQ], F32, e_ctx)
        logits = sb("logits", [P, TILES, EXPERTS], F32, e_ctx)
        aff = sb("aff", [P, TILES, EXPERTS], F32, e_ctx)
        big8 = sb("big8", [P, TILES, 8], F32, e_ctx)
        above = sb("above", [P, TILES, EXPERTS], F32, e_ctx)
        equal = sb("equal", [P, TILES, EXPERTS], F32, e_ctx)
        struck = sb("struck", [P, TILES, EXPERTS], F32, e_ctx)
        gates = sb("gates", [P, TILES, 3, EXPERTS], F32, e_ctx)
        red = sb("red", [P, 2, TILES], F32, e_ctx)
        gT32 = sb("gT32", [96, SEQ], F32, e_ctx)
        g_rest = sb("g_rest", [96, SEQ], F32, e_ctx)
        g_mid = sb("g_mid", [96, SEQ], BF16, e_ctx)
        g3 = sb("g3", [96, SEQ], BF16, e_ctx)
        w12 = [sb(f"w12_{i}", [P, 2, P], F32, e_ctx) for i in range(SLOTS)]
        hid = sb("hid", [P, 2, HALF], F32, e_ctx)
        hg = sb("hg", [P, 2, HALF], F32, e_ctx)
        moeT = sb("moeT", [P, SEQ], F32, e_ctx)
        y_out = sb("y_out", [P, TILES, P], F32, e_ctx)
        e_ctx.close()

        s_ctx = ExitStack()
        pos = sb("pos", [P, SEQ], F32, s_ctx)
        ang = sb("ang", [P, SEQ], F32, s_ctx)
        turns = sb("turns", [P, 2, SEQ], F32, s_ctx)
        whole = sb("whole", [P, SEQ], F32, s_ctx)
        sin_raw = sb("sin_raw", [P, SEQ], F32, s_ctx)
        s_ctx.close()

        ps = ctx.enter_context(nc.psum_tensor("ps", [P, 8, HALF], F32))

        def banks(a, n=2):
            return ps[:, a:a + n, :].rearrange("p a n -> p (a n)")

        passed, part_done, weights_in = sem("passed"), sem("part_done"), sem("weights_in")
        p_setup, v_setup, a_setup = sem("p_setup"), sem("v_setup"), sem("a_setup")
        x_in = sem("x_in")
        v_step = sem("v_step")
        p_step = sem("p_step")
        a_step = sem("a_step")
        ms_ready, ms_plus, rstd_ready = sem("ms_ready"), sem("ms_plus"), sem("rstd_ready")
        partial_ready, global_sum = sem("partial_ready"), sem("global_sum")
        a_out, a_taken = sem("a_out"), sem("a_taken")
        v_out, v_taken = sem("v_out"), sem("v_taken")
        tok_ready, v_norm, yg_ready = sem("tok_ready"), sem("v_norm"), sem("yg_ready")
        split_ready, delta_ready = sem("split_ready"), sem("delta_ready")
        y_begun = sem("y_begun")
        b_bcast, b_taken, c_bcast = sem("b_bcast"), sem("b_taken"), sem("c_bcast")
        decay_ready, bx_ready, scanned, cs_ready, cs_used = (
            sem("decay_ready"), sem("bx_ready"), sem("scanned"), sem("cs_ready"), sem("cs_used"))
        w_pair_in = [sem(f"w_pair_in{i}") for i in range(2)]
        proj_out, proj_taken = sem("proj_out"), sem("proj_taken")
        roped_ready, high_a, high_p, low_ready = sem("roped_ready"), sem("high_a"), sem("high_p"), sem("low_ready")
        scores_out, scores_taken = sem("scores_out"), sem("scores_taken")
        blocks_out, blocks_taken = sem("blocks_out"), sem("blocks_taken")
        tops_ready, misc_out, misc_taken = sem("tops_ready"), sem("misc_out"), sem("misc_taken")
        pv_out, pv_taken = sem("pv_out"), sem("pv_taken")
        acc_ready, resid_ready = sem("acc_ready"), sem("resid_ready")
        w12_in = [sem(f"w12_in{i}") for i in range(SLOTS)]
        router_out, aff_asked, aff_ready = sem("router_out"), sem("aff_asked"), sem("aff_ready")
        hid_out, hid_ready, gate_out, hg_ready, down_done = (
            sem("hid_out"), sem("hid_ready"), sem("gate_out"), sem("hg_ready"), sem("down_done"))
        gates_ready, g3_ready, sums_ready = sem("gates_ready"), sem("g3_ready"), sem("sums_ready")
        moe_taken, y_stored = sem("moe_taken"), sem("y_stored")

        CREDITS = [(a_taken, 2), (v_taken, 2), (scanned, 2), (bx_ready, 2), (cs_used, 2), (b_taken, 1), (cs_ready, 1),
                   (proj_taken, 2), (scores_taken, 2), (blocks_taken, 2), (pv_taken, 1), (pv_out, 2),
                   (hid_ready, 2), (hg_ready, 2), (down_done, 2)]

        block = ctx.enter_context(nc.Block())

        class Steps:

            def __init__(self, eng, s, base=0):
                self.eng, self.s, self.base, self.n = eng, s, base, 0

            def did(self, made):
                made.then_inc(self.s, 1)
                self.n += 1

            def wait(self):
                self.eng.wait_ge(self.s, self.base + self.n)

            def link(self, made):
                self.did(made)
                self.wait()

        PARTS, V_ANGLES, V_STEPS, V_OUTS, A_OUTS, A_STEPS = 3, 14, 136, 6, 22, 5

        def part_end(eng, k):
            eng.sem_inc(passed, 1)
            eng.drain().then_inc(part_done, 1)
            eng.wait_ge(part_done, ENGINES * k)
            eng.sem_inc(passed, 1)

        def both(t):
            return t.rearrange("p i d -> p (i d)")

        loads = [(ident[:, :], ins["c_ident"]), (masks32[:, :, :], ins["c_masks"]), (fold32[:, :], ins["c_fold"]),
                 (pos[:, :], ins["c_pos"].broadcast_to((P, SEQ))), (cols[:, :], ins["cols"]),
                 (resets[:, :], ins["c_resets"].broadcast_to((P, TILES * EXPERTS))),
                 (w_in[:, :], ins["w_in"]), (w_conv[:, :, :], ins["conv_w"]), (w_b3[:, :], ins["w_b3"]),
                 (w_c3[:, :], ins["w_c3"]), (w_d1[:, :], ins["w_d1"]), (w_d2[:, :], ins["w_d2"]),
                 (w_out[:, :], ins["w_out"]), (w_router[:, :], ins["router_w"]), (b2_all[:, :], ins["b2"]),
                 (v_w[:, :], ins["v_w"]), (o_w[:, :, :], ins["o_w"]),
                 (router_b[:, :], ins["router_b"].broadcast_to((P, EXPERTS))),
                 (v_b[:, :], ins["v_b"].broadcast_to((P, HEADS * HD)))]
        loads += [(rows[:, i, :], ins["rows"][i:i + 1, :].broadcast_to((P, P))) for i in range(4)]
        ALL_IN = 16 * len(loads)

        @block.sync
        def _(sp):
            for dst, src in loads:
                sp.dma_start(dst, src).then_inc(weights_in, 16)
            part_end(sp, 1)
            with sp.Fori(0, BATCH) as b:
                sp.dma_start(xin[:, :, :], ins["x"][bass.ds(b, 1), :, :].rearrange("o (i p) d -> p (o i) d", p=P)
                             ).then_inc(x_in, 16)
                part_end(sp, PARTS * b + 2)

                def load_pair(pair, buf):
                    sp.dma_start(w_pair[buf][:, :, :], ins["w_pairs"][bass.ds(pair, 1), :, :, :].rearrange(
                        "o p s n -> p (o s) n")).then_inc(w_pair_in[buf], 16)

                load_pair(0, 0)
                load_pair(1, 1)
                with sp.Fori(0, PAIRS // 2 - 1) as r:
                    for k in range(2):
                        sp.wait_ge(proj_out, 10 * (b * PAIRS + 2 * r + k) + 8)
                        sp.sem_inc(passed, 1)
                        load_pair(2 * r + 2 + k, k)
                part_end(sp, PARTS * b + 3)
                for k in range(SLOTS):
                    sp.dma_start(w12[k][:, :, :], ins["w12"][k, :, :, :]).then_inc(w12_in[k], 16)
                with sp.Fori(1, EXPERTS // SLOTS) as r:
                    for k in range(SLOTS):
                        sp.wait_ge(down_done, 2 + HALVES * (b * EXPERTS + (r - 1) * SLOTS + k + 1))
                        sp.sem_inc(passed, 1)
                        sp.dma_start(w12[k][:, :, :], ins["w12"][bass.ds(r * SLOTS + k, 1), :, :, :].rearrange(
                            "o p s n -> p (o s) n")).then_inc(w12_in[k], 16)
                sp.wait_ge(v_taken, V_OUTS * (b + 1) + 2)
                sp.dma_start(out[bass.ds(b, 1), :, :].rearrange("o (i p) d -> p (o i) d", p=P), y_out[:, :, :]
                             ).then_inc(y_stored, 16)
                sp.wait_ge(y_stored, 16 * b + 16)
                part_end(sp, PARTS * b + 4)
            sp.wait_ge(y_stored, 16 * BATCH)

        def pool_copy(pool, dst, src):
            return pool.tensor_scalar(dst, src, 1.0, 0.0, ALU.mult, ALU.add)

        RSTDS = 7
        P_STEPS = 3

        @block.gpsimd
        def _(pool):
            for s, c in CREDITS:
                pool.sem_inc(s, c)
            pool.memset(nmb[:, :], 0.0)
            pool.memset(neg_half[:, :], -0.5)
            pool.memset(mean_of[:, :], 1.0 / P)
            pool.memset(hpad[:, 0:1], 0.0)
            pool.memset(hpad[:, SEQ + 1:SEQ + 2], 0.0).then_inc(p_setup, 1)
            pool.wait_ge(p_setup, 1)
            part_end(pool, 1)
            with pool.Fori(0, BATCH) as b:
                steps = Steps(pool, p_step, b * P_STEPS)

                def inverse_root(k, n):
                    pool.wait_ge(ms_ready, b * RSTDS + k)
                    pool.sem_inc(passed, 1)
                    pool.tensor_scalar(ms[:, 0:n], ms[:, 0:n], EPS, None, ALU.add).then_inc(ms_plus, 1)
                    pool.wait_ge(ms_plus, b * RSTDS + k)
                    pool.tensor_tensor(rstd[:, 0:n], ms[:, 0:n], neg_half[:, 0:n], ALU.pow).then_inc(rstd_ready, 1)

                inverse_root(1, TILES)
                pool.wait_ge(tok_ready, 3 * b + 1)
                steps.link(pool.tensor_tensor(both(resid[:, :, :]), both(xin[:, :, :]), both(x0[:, :, :]), ALU.add))
                steps.link(pool.tensor_tensor(resid[:, :, :], resid[:, :, :],
                                              b_out_r.unsqueeze(1).broadcast_to((P, TILES, P)), ALU.add))
                inverse_root(2, 1)
                inverse_root(3, 1)
                pool.wait_ge(delta_ready, b + 1)
                pool.sem_inc(passed, 1)
                with pool.Fori(0, STATES // 2) as r:
                    for k in range(2):
                        n = b * STATES + 2 * r + k
                        pool.wait_ge(b_taken, n + 2)
                        pool.wait_ge(scanned, n + 1)
                        pool.tensor_tensor(bx[:, k, :], du[:, :], b_rows[:, k, :], ALU.mult).then_inc(bx_ready, 1)
                inverse_root(4, TILES)
                part_end(pool, PARTS * b + 2)
                inverse_root(5, TILES)
                inverse_root(6, TILES)
                pool.wait_ge(tok_ready, 3 * b + 2)
                pool.tensor_tensor(acc[:, :, :], xa[:, :, :], o_b_r.unsqueeze(1).broadcast_to((P, TILES, P)),
                                   ALU.add).then_inc(acc_ready, 1)

                def step(s, par):
                    n = b * PAIRS + s
                    for k in range(2):
                        pool.wait_ge(proj_taken, 10 * n + 4 * k + 4 + 2)
                        pool.wait_ge(high_a, 4 * n)
                        pool.wait_ge(low_ready, 4 * n)
                        pool.wait_ge(high_p, 4 * n)
                        pool.tensor_tensor(roped[:, k, :], turned[:, 2 * k, :], turned[:, 2 * k + 1, :], ALU.add
                                           ).then_inc(roped_ready, 1)
                        pool.wait_ge(roped_ready, 2 * n + k + 1)
                    copies = [(q_max[par][0][0:HD, :], roped[0:HD, 0, :]), (q_max[par][1][HD:P, :], roped[HD:P, 0, :]),
                              (k_high[par][0][HD:P, :], roped[0:HD, 1, :]), (k_high[par][1][HD:P, :], roped[HD:P, 1, :])]
                    for k, (dst, src) in enumerate(copies):
                        pool.sem_inc(passed, 1)
                        pool_copy(pool, dst, src).then_inc(high_p, 1)
                        pool.wait_ge(high_p, 4 * n + k + 1)
                        pool.sem_inc(passed, 1)

                step(0, 0)
                with pool.Fori(0, PAIRS // 2 - 1) as r:
                    for k in range(2):
                        step(2 * r + 1 + k, 1 - k)
                step(PAIRS - 1, 1)
                part_end(pool, PARTS * b + 3)
                inverse_root(7, TILES)
                pool.wait_ge(ms_ready, b * RSTDS + RSTDS)
                steps.link(pool.tensor_tensor(both(resid[:, :, :]), both(resid[:, :, :]), both(acc[:, :, :]), ALU.add))
                pool.wait_ge(tok_ready, 3 * b + 3)
                pool.tensor_tensor(both(resid[:, :, :]), both(resid[:, :, :]), both(an[:, :, :]), ALU.add
                                   ).then_inc(resid_ready, 1)
                part_end(pool, PARTS * b + 4)


        @block.scalar
        def _(act):
            act.wait_ge(weights_in, ALL_IN)
            act.activation(exp_a[:, :], cols[:, C_ALOG:C_ALOG + STATES], ACT.Exp).then_inc(a_setup, 1)
            act.wait_ge(v_setup, V_ANGLES)
            act.activation(sin_raw[:, :], turns[:, 0, :], ACT.Sin).then_inc(a_setup, 1)
            act.activation(cos_t[:, :], turns[:, 1, :], ACT.Sin).then_inc(a_setup, 1)
            part_end(act, 1)
            with act.Fori(0, BATCH) as b:
                def take(k, n, dst, func, bias=0.0, scale=1.0):
                    act.wait_ge(a_out, b * A_OUTS + k + 1)
                    act.activation(dst, ps[0:n, k % 2, :], func, bias=bias, scale=scale).then_inc(a_taken, 1)

                def col(c, n=P):
                    return cols[0:n, c:c + 1]

                act.wait_ge(v_norm, 2 * b + 1)
                for c in range(2):
                    take(c, P, xnT_m[:, c * HALF:(c + 1) * HALF], ACT.Identity, nmb[:, 0:1], rstd[:, 0:1])
                for c in range(2):
                    take(2 + c, P, hpad[:, 1 + c * HALF:1 + (c + 1) * HALF], ACT.Identity, col(C_B_IN))
                act.wait_ge(a_taken, b * A_OUTS + 4 + 2)
                act.activation(gate[:, :], hpad[:, 1:1 + SEQ], ACT.Silu).then_inc(a_step, 1)
                for c in range(2):
                    take(4 + c, P, hc[:, c * HALF:(c + 1) * HALF], ACT.Identity, col(C_CONV_B))
                act.wait_ge(v_norm, 2 * b + 2)
                act.wait_ge(a_taken, b * A_OUTS + 6 + 2)
                act.activation(h_act[:, :], hc[:, :], ACT.Silu, bias=nmb[:, 0:1], scale=rstd[:, 0:1]).then_inc(a_step, 1)
                for j in range(2):
                    for c in range(2):
                        take(6 + 2 * j + c, 96, bc32[:, j, c * HALF:(c + 1) * HALF], ACT.Identity,
                             col((C_B_B, C_B_C)[j], 96))
                for c in range(2):
                    take(10 + c, DT_RANK, d1[:, c * HALF:(c + 1) * HALF], ACT.Identity, col(C_B_D1, DT_RANK))
                for c in range(2):
                    take(12 + c, P, z[:, c * HALF:(c + 1) * HALF], ACT.Identity, col(C_B_D2))
                act.wait_ge(a_taken, b * A_OUTS + 14 + 2)
                act.activation(z_abs[:, :], z[:, :], ACT.Abs).then_inc(a_step, 1)
                act.wait_ge(a_step, A_STEPS * b + 3)
                act.activation(z_abs[:, :], z_abs[:, :], ACT.Exp, scale=-1.0).then_inc(a_step, 1)
                act.wait_ge(a_step, A_STEPS * b + 4)
                act.activation(sp_log[:, :], z_abs[:, :], ACT.Ln, bias=1.0).then_inc(a_step, 1)
                act.wait_ge(delta_ready, b + 1)
                with act.Fori(0, STATES // 2) as r:
                    for k in range(2):
                        n = b * STATES + 2 * r + k
                        act.wait_ge(scanned, n + 1)
                        act.sem_inc(passed, 1)
                        act.activation(decay[:, k, :], delta[:, :], ACT.Exp,
                                       scale=neg_a[:, bass.ds(2 * r + k, 1)]).then_inc(decay_ready, 1)
                        act.wait_ge(b_bcast, n + 1)
                        act.wait_ge(bx_ready, n + 1)
                        act.activation(b_rows[:, k, :], banks(2), ACT.Copy).then_inc(b_taken, 1)
                for c in range(2):
                    take(14 + c, P, gT[:, c * HALF:(c + 1) * HALF], ACT.Identity)
                part_end(act, PARTS * b + 2)
                for c in range(2):
                    take(16 + c, P, xnT[:, c * HALF:(c + 1) * HALF], ACT.Identity)

                def misc(m, k, dst, src, scale=1.0):
                    act.wait_ge(misc_out, 8 * m + k + 1)
                    act.activation(dst, src, ACT.Copy, scale=scale).then_inc(misc_taken, 1)

                def step(s, par, this, prev):
                    n = b * PAIRS + s
                    m = n - 1
                    if prev:
                        for h in range(2):
                            at = HD if h == 0 else 0
                            for c in range(HALVES):
                                misc(m, 2 * h + c, q_max[1 - par][h][at:at + 1, c * HALF:(c + 1) * HALF],
                                     ps[at:at + 1, 7, :], -1.0)

                    def high(k):
                        dst = (q_split, k_high)[k][par]
                        act.wait_ge(roped_ready, 2 * n + k + 1)
                        for h in range(2):
                            act.activation(dst[h][0:HD, :], roped[HD * h:HD * h + HD, k, :], ACT.Copy
                                           ).then_inc(high_a, 1)

                    seen = 0
                    if this and not prev:
                        high(0)
                        high(1)
                    for kind, h, u in slots(prev, this):
                        if kind == "st":
                            c, j, q0 = ST[u]
                            w = HALF * (c + 1) - q0
                            act.wait_ge(blocks_out, 2 * NU * m + NU * h + u + 1)
                            if j == 0:
                                act.wait_ge(pv_out, 4 * m + 2 * h + c + 1)
                            act.activation(probs[:, TPH * c + j, q0 - HALF * c:HALF], ps[:, 4 + u % 2, 0:w], ACT.Exp,
                                           scale=SCALE).then_inc(blocks_taken, 1)
                            if this and h == 0 and u in (3, 7):
                                high(0 if u == 3 else 1)
                        elif kind == "ct":
                            misc(m, 4 + 2 * h, ctxT[:, :], ps[:, 7, :])

                step(0, 0, True, False)
                with act.Fori(0, PAIRS // 2 - 1) as r:
                    for k in range(2):
                        step(2 * r + 1 + k, 1 - k, True, True)
                step(PAIRS - 1, 1, True, True)
                step(PAIRS, 0, False, True)
                part_end(act, PARTS * b + 3)
                for c in range(2):
                    take(18 + c, P, anT[:, c * HALF:(c + 1) * HALF], ACT.Identity)
                act.wait_ge(aff_asked, b + 1)
                act.activation(aff[:, :, 0:ROUTED], logits[:, :, 0:ROUTED], ACT.Exp).then_inc(aff_ready, 1)
                for c in range(2):
                    take(20 + c, 96, gT32[:, c * HALF:(c + 1) * HALF], ACT.Identity)
                with act.Fori(0, EXPERTS) as e:
                    for c in range(HALVES):
                        k = HALVES * (b * EXPERTS + e) + c
                        act.wait_ge(hid_out, k + 1)
                        act.wait_ge(hg_ready, k + 1)
                        act.sem_inc(passed, 1)
                        act.activation(hid[:, c, :], ps[:, c, :], ACT.Gelu,
                                       bias=cols[:, bass.ds(C_B1 + e, 1)]).then_inc(hid_ready, 1)
                act.wait_ge(down_done, HALVES * EXPERTS * (b + 1) + 2)
                for c in range(2):
                    act.activation(moeT[:, c * HALF:(c + 1) * HALF], ps[:, 4 + c, :], ACT.Identity).then_inc(moe_taken, 1)
                part_end(act, PARTS * b + 4)

        @block.vector
        def _(dve):
            dve.wait_ge(weights_in, ALL_IN)
            su = Steps(dve, v_setup)

            def slink(made):
                su.did(made)
                dve.wait_ge(v_setup, su.n)

            slink(dve.tensor_scalar(ang[:, :], pos[:, :], cols[:, C_THETA:C_THETA + 1], None, ALU.mult))
            for k in range(2):
                slink(dve.tensor_scalar(whole[:, :], ang[:, :], float(1 / (2 * np.pi)), 0.25 * k, ALU.mult, ALU.add))
                slink(dve.tensor_scalar(whole[:, :], whole[:, :], ROUNDER, ROUNDER, ALU.add, ALU.subtract))
                slink(dve.scalar_tensor_tensor(turns[:, k, :], whole[:, :], -TWO_PI_A, ang[:, :], ALU.mult, ALU.add))
                slink(dve.scalar_tensor_tensor(turns[:, k, :], whole[:, :], -TWO_PI_B, turns[:, k, :], ALU.mult, ALU.add))
                slink(dve.scalar_tensor_tensor(turns[:, k, :], whole[:, :], -TWO_PI_C, turns[:, k, :], ALU.mult, ALU.add))
                if k:
                    slink(dve.tensor_scalar(turns[:, k, :], turns[:, k, :], float(np.pi / 2), None, ALU.add))
                slink(dve.tensor_scalar(turns[:, k, :], turns[:, k, :], PI_BELOW, -PI_BELOW, ALU.min, ALU.max))
            assert su.n == V_ANGLES, su.n
            for i in range(2):
                dve.memset(vals[i][:, :, :, HD:HD + 1], 1.0)
                dve.memset(k_low[i][0][HD:HD + 1, :].bitcast(F32), 1.0)
                dve.memset(q_max[i][1][0:HD, :].bitcast(F32), 0.0)
                made = dve.memset(k_low[i][1][0:HD, :].bitcast(F32), 0.0)
            slink(made)
            for i in range(2):
                dve.memset(k_low[i][1][0:1, :].bitcast(F32), 1.0)
            dve.tensor_copy(identr[:, :], ident[:, :])
            dve.tensor_copy(identb[:, :], ident[:, :])
            dve.tensor_copy(masks[:, :, :], masks32[:, :, :])
            dve.tensor_copy(fold[:, :], fold32[:, :])
            dve.tensor_scalar(diag_d[:, :], ident[:, :], cols[:, C_D:C_D + 1], None, ALU.mult)
            dve.wait_ge(a_setup, 1)
            dve.tensor_scalar(neg_a[:, :], exp_a[:, :], -1.0, None, ALU.mult)
            dve.wait_ge(a_setup, 2)
            dve.tensor_scalar(sin_t[:, :], sin_raw[:, :], cols[:, C_SIGN:C_SIGN + 1], None, ALU.mult)
            part_end(dve, 1)
            with dve.Fori(0, BATCH) as b:
                st = Steps(dve, v_step, b * V_STEPS)

                def root(k, made):
                    made.then_inc(ms_ready, 1)
                    dve.wait_ge(rstd_ready, b * RSTDS + k)

                def moments(src, n):
                    for i in range(n):
                        st.did(dve.bn_stats(stats[:, i, :], src(i)))
                    st.wait()
                    dve.sem_inc(passed, 1)
                    for i in range(n):
                        st.did(dve.bn_aggr(mv[:, i, :], stats[:, i, :]))
                    st.wait()

                def mean_squares(k):
                    st.link(dve.tensor_tensor(ms[:, :], mv[:, :, 0], mv[:, :, 0], ALU.mult))
                    root(k, dve.tensor_tensor(ms[:, :], ms[:, :], mv[:, :, 1], ALU.add))

                def normed(dst, src, k, last):
                    for i in range(TILES):
                        made = dve.tensor_scalar(dst[:, i, :], src(i), mv[:, i, 0:1], rstd[:, i:i + 1],
                                                 ALU.subtract, ALU.mult)
                        last(i, made)

                def signal_last(s):
                    return lambda i, made: made.then_inc(s, 1) if i == TILES - 1 else None

                dve.wait_ge(x_in, 16 * b + 16)
                moments(lambda i: xin[:, i, :], TILES)
                root(1, dve.tensor_copy(ms[:, :], mv[:, :, 1]))
                normed(x0, lambda i: xin[:, i, :], 1, signal_last(tok_ready))
                dve.wait_ge(tok_ready, 3 * b + 1)
                for c in range(2):
                    st.did(dve.bn_stats(stats[:, c, :], both(x0[:, TPH * c:TPH * (c + 1), :])))
                st.wait()
                dve.sem_inc(passed, 1)
                st.link(dve.bn_aggr(mv[:, 0, :], stats[:, 0:2, :].rearrange("p a b -> p (a b)")))
                st.link(dve.tensor_copy(partial[:, 0:1], mv[:, 0, 0:1]))
                dve.scalar_tensor_tensor(partial[:, 1:2], mv[:, 0, 0:1], mv[:, 0, 0:1], mv[:, 0, 1:2], ALU.mult, ALU.add
                                         ).then_inc(partial_ready, 1)
                dve.wait_ge(global_sum, b + 1)
                st.link(dve.tensor_copy(glob[:, 0:2], ps[:, 6, 0:2]))
                st.link(dve.tensor_scalar(glob[:, 2:3], glob[:, 0:1], glob[:, 0:1], -1.0, ALU.mult, ALU.mult))
                root(2, dve.tensor_tensor(ms[:, 0:1], glob[:, 1:2], glob[:, 2:3], ALU.add))
                dve.tensor_scalar(nmb[:, 0:1], glob[:, 0:1], rstd[:, 0:1], -1.0, ALU.mult, ALU.mult).then_inc(v_norm, 1)
                dve.wait_ge(a_taken, b * A_OUTS + 6 + 2)
                for c in range(2):
                    st.did(dve.bn_stats(stats[:, c, :], hc[:, c * HALF:(c + 1) * HALF]))
                st.wait()
                dve.sem_inc(passed, 1)
                st.link(dve.bn_aggr(mv[:, 0, :], stats[:, 0:2, :].rearrange("p a b -> p (a b)")))
                root(3, dve.tensor_copy(ms[:, 0:1], mv[:, 0, 1:2]))
                dve.tensor_scalar(nmb[:, 0:1], mv[:, 0, 0:1], rstd[:, 0:1], -1.0, ALU.mult, ALU.mult).then_inc(v_norm, 1)

                def three_parts(dst, src, rest, mid, last):
                    st.link(dve.tensor_copy(dst[0:96, :], src[0:96, :]))
                    st.did(dve.tensor_tensor(dst[32:64, :], src[32:64, :], dst[32:64, :], ALU.subtract))
                    st.link(dve.tensor_tensor(rest[64:96, :], src[64:96, :], dst[64:96, :], ALU.subtract))
                    st.link(dve.tensor_copy(mid[64:96, :], rest[64:96, :]))
                    last(dve.tensor_tensor(dst[64:96, :], rest[64:96, :], mid[64:96, :], ALU.subtract))

                for j in range(2):
                    dve.wait_ge(a_taken, b * A_OUTS + 8 + 2 * j + 2)
                    three_parts(bc3[:, j, :], bc32[:, j, :], bc_rest, bc_mid,
                                (st.link if j == 0 else lambda made: made.then_inc(split_ready, 1)))
                dve.wait_ge(a_step, A_STEPS * b + 5)
                st.link(dve.scalar_tensor_tensor(delta[:, :], z[:, :], 0.0, sp_log[:, :], ALU.max, ALU.add))
                dve.tensor_tensor(du[:, :], delta[:, :], h_act[:, :], ALU.mult).then_inc(delta_ready, 1)
                with dve.Fori(0, STATES // 2) as r:
                    for k in range(2):
                        n = b * STATES + 2 * r + k
                        dve.wait_ge(decay_ready, n + 1)
                        dve.wait_ge(bx_ready, n + 3)
                        dve.wait_ge(cs_ready, n)
                        dve.tensor_tensor_scan(state[:, k, :], decay[:, k, :], bx[:, k, :], 0.0, ALU.mult, ALU.add
                                               ).then_inc(scanned, 1)
                        dve.wait_ge(scanned, n + 3)
                        dve.wait_ge(c_bcast, n + 1)
                        dve.wait_ge(cs_used, n + 1)
                        dve.tensor_tensor(cs[:, k, :], state[:, k, :], banks(4), ALU.mult).then_inc(cs_ready, 1)
                dve.wait_ge(cs_used, STATES * b + STATES + 2)
                dve.tensor_tensor(hc[:, :], banks(6), gate[:, :], ALU.mult).then_inc(yg_ready, 1)
                dve.wait_ge(v_out, V_OUTS * b + 2)
                g_ps = lambda i: ps[:, 2 + i // TPH, (i % TPH) * P:(i % TPH + 1) * P]
                moments(g_ps, TILES)
                root(4, dve.tensor_copy(ms[:, :], mv[:, :, 1]))
                normed(g_tok, g_ps, 4, lambda i, made: made.then_inc(v_taken, 1) if i % TPH == TPH - 1 else None)
                for c in range(2):
                    dve.wait_ge(v_out, V_OUTS * b + 3 + c)
                    dve.wait_ge(p_step, P_STEPS * b + 2)
                    part = both(resid[:, TPH * c:TPH * (c + 1), :])
                    dve.tensor_tensor(part, part, ps[:, 2 + c, :], ALU.add).then_inc(v_taken, 1)
                part_end(dve, PARTS * b + 2)

                moments(lambda i: resid[:, i, :], TILES)
                root(5, dve.tensor_copy(ms[:, :], mv[:, :, 1]))
                normed(xa, lambda i: resid[:, i, :], 5, lambda i, made: st.did(made))
                st.wait()
                moments(lambda i: xa[:, i, :], TILES)
                mean_squares(6)
                for i in range(TILES):
                    made = dve.scalar_tensor_tensor(xa[:, i, :], xa[:, i, :], rstd[:, i:i + 1], gamma1_r, ALU.mult, ALU.mult)
                made.then_inc(tok_ready, 1)

                def step(s, par, this, prev):
                    n = b * PAIRS + s
                    m = n - 1
                    if this:
                        for j in range(4):
                            for c in range(HALVES):
                                k = HALVES * j + c
                                dve.wait_ge(proj_out, 10 * n + k + 1)
                                if c == 0 and j % 2 == 0:
                                    dve.wait_ge(roped_ready, 2 * n + 0)
                                sl = slice(c * HALF, (c + 1) * HALF)
                                dve.scalar_tensor_tensor(
                                    turned[:, j, sl], ps[:, c, :], cols[:, bass.ds(C_QK + 4 * s + j, 1)],
                                    (cos_t, sin_t)[j % 2][:, sl], ALU.add, ALU.mult).then_inc(proj_taken, 1)
                        for c in range(HALVES):
                            dve.wait_ge(proj_out, 10 * n + 8 + c + 1)
                            dve.tensor_tensor(
                                vals[par][:, TPH * c:TPH * (c + 1), :, 0:HD],
                                ps[:, c, :].rearrange("p (i h d) -> p i h d", i=TPH, h=2),
                                v_b[:, bass.ds(P * s, P)].rearrange("p (h d) -> p h d", h=2).unsqueeze(1).broadcast_to(
                                    (P, TPH, 2, HD)), ALU.add).then_inc(proj_taken, 1)
                        for k in range(2):
                            dve.wait_ge(high_a, 4 * n + 2 * k + 2)
                            dve.wait_ge(high_p, 4 * n + 2 * k + 2)
                            dst = (q_split, k_low)[k][par]
                            high0 = (q_split, k_high)[k][par][0]
                            high1 = (q_max, k_high)[k][par][1]
                            at0 = (HD, 0)[k]
                            dve.tensor_tensor(dst[0][at0:at0 + HD, :], roped[0:HD, k, :], high0[0:HD, :].bitcast(F32),
                                              ALU.subtract).then_inc(low_ready, 1)
                            dve.tensor_tensor(dst[1][HD:P, :], roped[HD:P, k, :], high1[HD:P, :].bitcast(F32),
                                              ALU.subtract).then_inc(low_ready, 1)
                    for kind, h, u in slots(prev, this):
                        if kind == "mx":
                            i, k0, w = MX[u]
                            dve.wait_ge(scores_out, 2 * NU * n + NU * h + u + 1)
                            dve.tensor_reduce(tops[:, h, u:u + 1], ps[:, 2 + u % 2, 0:w], AX_X, ALU.max
                                              ).then_inc(scores_taken, 1)
                            if u == NU - 1:
                                dve.wait_ge(scores_taken, 2 * NU * n + NU * h + NU + 2)
                                dve.tensor_copy(top_r[:, h, 0:TPH], tops[:, h, 0:TPH])
                                dve.tensor_tensor(top_r[:, h, TPH:TILES], tops[:, h, TPH:NU:2], tops[:, h, TPH + 1:NU:2],
                                                  ALU.max).then_inc(tops_ready, 1)
                        elif kind == "pv" and u % TPH == TPH - 1:
                            c = u // TPH
                            g = 4 * m + 2 * h + c
                            dve.wait_ge(pv_out, g + 1 + 2)
                            out4 = ps[:, 6, 0:TPH * (HD + 1)].rearrange("p (i d) -> p i d", i=TPH)
                            dve.reciprocal(sums[:, :], out4[:, :, HD]).then_inc(sums_ready, 1)
                            dve.wait_ge(sums_ready, g + 1)
                            dve.tensor_tensor(ctx_t[:, TPH * c:TPH * (c + 1), HD * h:HD * (h + 1)], out4[:, :, 0:HD],
                                              sums[:, :].unsqueeze(2).broadcast_to((P, TPH, HD)), ALU.mult
                                              ).then_inc(pv_taken, 1)
                        elif kind == "op":
                            dve.wait_ge(misc_out, 8 * m + 4 + 2 * h + 2)
                            dve.wait_ge(acc_ready, b + 1)
                            dve.wait_ge(misc_taken, 8 * m + 4 + 2 * h + 1)
                            part = both(acc[:, TPH * h:TPH * (h + 1), :])
                            dve.tensor_tensor(part, part, ps[:, 7, :], ALU.add).then_inc(misc_taken, 1)

                step(0, 0, True, False)
                with dve.Fori(0, PAIRS // 2 - 1) as r:
                    for k in range(2):
                        step(2 * r + 1 + k, 1 - k, True, True)
                step(PAIRS - 1, 1, True, True)
                step(PAIRS, 0, False, True)
                dve.wait_ge(misc_taken, 8 * PAIRS * (b + 1))
                part_end(dve, PARTS * b + 3)

                moments(lambda i: acc[:, i, :], TILES)
                mean_squares(7)
                for i in range(TILES):
                    made = dve.scalar_tensor_tensor(an[:, i, :], acc[:, i, :], rstd[:, i:i + 1], gamma2_r, ALU.mult, ALU.mult)
                made.then_inc(tok_ready, 1)
                wide = (P, TILES, ROUTED)
                dve.wait_ge(router_out, b + 1)
                st.link(dve.tensor_tensor(logits[:, :, :], ps[:, 6, 0:TILES * EXPERTS].rearrange("p (i e) -> p i e", i=TILES),
                                          router_b[:, :].unsqueeze(1).broadcast_to((P, TILES, EXPERTS)), ALU.add))
                st.did(dve.memset(aff[:, :, ROUTED:EXPERTS], 0.0))
                st.link(dve.tensor_reduce(red[:, 0, :], logits[:, :, 0:ROUTED], AX_X, ALU.max))
                dve.tensor_tensor(logits[:, :, 0:ROUTED], logits[:, :, 0:ROUTED],
                                  red[:, 0, :].unsqueeze(2).broadcast_to(wide), ALU.subtract).then_inc(aff_asked, 1)
                dve.wait_ge(aff_ready, b + 1)
                st.link(dve.tensor_reduce(red[:, 1, :], aff[:, :, 0:ROUTED], AX_X, ALU.add))
                st.link(dve.reciprocal(red[:, 0, :], red[:, 1, :]))
                st.link(dve.tensor_tensor(aff[:, :, 0:ROUTED], aff[:, :, 0:ROUTED],
                                          red[:, 0, :].unsqueeze(2).broadcast_to(wide), ALU.mult))
                full = (P, TILES, EXPERTS)
                dve.sem_inc(passed, 1)
                for i in range(TILES):
                    st.did(dve.max(big8[:, i, :], aff[:, i, 0:ROUTED]))
                st.wait()
                third = big8[:, :, TOP - 1:TOP].broadcast_to(full)
                st.did(dve.tensor_tensor(above[:, :, :], aff[:, :, :], third, ALU.is_gt))
                st.link(dve.tensor_tensor(equal[:, :, :], aff[:, :, :], third, ALU.is_equal))
                st.did(dve.tensor_reduce(red[:, 1, :], above[:, :, :], AX_X, ALU.add))
                st.link(dve.tensor_tensor_scan(both(struck[:, :, :]), resets[:, :], both(equal[:, :, :]), 0.0,
                                               ALU.mult, ALU.add))
                st.link(dve.tensor_tensor(struck[:, :, :], struck[:, :, :], red[:, 1, :].unsqueeze(2).broadcast_to(full),
                                          ALU.add))
                st.link(dve.scalar_tensor_tensor(both(struck[:, :, :]), both(struck[:, :, :]), TOP + 0.5,
                                                 both(equal[:, :, :]), ALU.is_lt, ALU.mult))
                st.link(dve.tensor_tensor(struck[:, :, :], struck[:, :, :], above[:, :, :], ALU.add))
                st.link(dve.tensor_tensor(struck[:, :, :], struck[:, :, :], aff[:, :, :], ALU.mult))
                st.link(dve.memset(struck[:, :, ROUTED:EXPERTS], 1.0))
                dve.tensor_copy(gates[:, :, :, :], struck[:, :, :].unsqueeze(2).broadcast_to((P, TILES, 3, EXPERTS))
                                ).then_inc(gates_ready, 1)
                dve.wait_ge(a_taken, b * A_OUTS + 22 + 2)
                three_parts(g3[:, :], gT32[:, :], g_rest, g_mid, lambda made: made.then_inc(g3_ready, 1))
                assert st.n == V_STEPS, st.n
                with dve.Fori(0, EXPERTS) as e:
                    for c in range(HALVES):
                        k = HALVES * (b * EXPERTS + e) + c
                        dve.wait_ge(hid_ready, k + 3)
                        dve.wait_ge(gate_out, k + 1)
                        dve.wait_ge(down_done, k + 1)
                        dve.tensor_tensor(hg[:, c, :], hid[:, c, :], ps[:, 2 + c, :], ALU.mult).then_inc(hg_ready, 1)
                for c in range(2):
                    dve.wait_ge(v_out, V_OUTS * b + 5 + c)
                    dve.wait_ge(resid_ready, b + 1)
                    sl = slice(TPH * c, TPH * (c + 1))
                    dve.tensor_tensor(both(y_out[:, sl, :]), both(resid[:, sl, :]), ps[:, 2 + c, :], ALU.add
                                      ).then_inc(v_taken, 1)
                part_end(dve, PARTS * b + 4)

        @block.tensor
        def _(pe):
            part_end(pe, 1)
            with pe.Fori(0, BATCH) as b:
                def a_bank(k):
                    pe.wait_ge(a_taken, b * A_OUTS + k + 1)

                def v_bank(k):
                    pe.wait_ge(v_taken, b * V_OUTS + k + 1)

                def halves(k, n, lhs, rhs, taps=1):
                    for c in range(2):
                        a_bank(k + c)
                        for t in range(taps):
                            made = pe.matmul(ps[0:n, c, :], lhs(t), rhs(c, t), start=(t == 0), stop=(t == taps - 1))
                        made.then_inc(a_out, 1)

                def turn(src, bank, n=P):
                    for i in range(TPH):
                        made = pe.transpose(ps[0:n, bank, i * P:(i + 1) * P], src(i), ident[:, :])
                    return made

                def cut(t, c, shift=0):
                    return t[:, c * HALF + shift:(c + 1) * HALF + shift]

                pe.wait_ge(tok_ready, 3 * b + 1)
                for c in range(2):
                    a_bank(c)
                    turn(lambda i: x0[:, TPH * c + i, :], c).then_inc(a_out, 1)
                pe.wait_ge(partial_ready, b + 1)
                pe.matmul(ps[:, 6, 0:2], mean_of[:, :], partial[:, :], start=True, stop=True).then_inc(global_sum, 1)
                pe.wait_ge(a_taken, b * A_OUTS + 2 + 2)
                halves(2, P, lambda t: w_in[:, :], lambda c, t: cut(xnT_m, c))
                pe.wait_ge(a_taken, b * A_OUTS + 4 + 2)
                halves(4, P, lambda t: w_conv[:, t, :], lambda c, t: cut(hpad, c, t), 3)
                pe.wait_ge(a_step, A_STEPS * b + 2)
                halves(6, 96, lambda t: w_b3[:, :], lambda c, t: cut(h_act, c))
                halves(8, 96, lambda t: w_c3[:, :], lambda c, t: cut(h_act, c))
                halves(10, DT_RANK, lambda t: w_d1[:, :], lambda c, t: cut(h_act, c))
                pe.wait_ge(a_taken, b * A_OUTS + 12 + 2)
                halves(12, P, lambda t: w_d2[:, :], lambda c, t: cut(d1, c))
                for c in range(2):
                    pe.matmul(ps[:, 6 + c, :], diag_d[:, :], cut(h_act, c), start=True, stop=False, skip_group_check=True)
                pe.wait_ge(split_ready, b + 1)
                pe.sem_inc(passed, 1)
                with pe.Fori(0, STATES // 2) as r:
                    for k in range(2):
                        n = b * STATES + 2 * r + k
                        pick = fold[:, bass.ds(2 * r + k, 1)].broadcast_to((96, P))
                        pe.wait_ge(b_taken, n + 1)
                        for c in range(2):
                            made = pe.matmul(ps[:, 2 + c, :], pick, cut(bc3[:, 0, :], c), start=True, stop=True)
                        made.then_inc(b_bcast, 1)
                        pe.wait_ge(cs_ready, n + 1)
                        for c in range(2):
                            made = pe.matmul(ps[:, 4 + c, :], pick, cut(bc3[:, 1, :], c), start=True, stop=True)
                        made.then_inc(c_bcast, 1)
                        pe.wait_ge(cs_ready, n + 2)
                        for c in range(2):
                            made = pe.matmul(ps[:, 6 + c, :], ident[:, :], cut(cs[:, k, :], c), start=False, stop=False,
                                             skip_group_check=True)
                        made.then_inc(cs_used, 1)
                pe.wait_ge(yg_ready, b + 1)
                for c in range(2):
                    v_bank(c)
                    turn(lambda i: hc[:, (TPH * c + i) * P:(TPH * c + i + 1) * P], 2 + c).then_inc(v_out, 1)
                for c in range(2):
                    pe.wait_ge(v_taken, b * V_OUTS + c + 1 + 2)
                    a_bank(14 + c)
                    turn(lambda i: g_tok[:, TPH * c + i, :], c).then_inc(a_out, 1)
                for c in range(2):
                    pe.wait_ge(a_taken, b * A_OUTS + 14 + c + 1 + 2)
                    v_bank(2 + c)
                    for i in range(TPH):
                        made = pe.matmul(ps[:, 2 + c, i * P:(i + 1) * P], gT[:, (TPH * c + i) * P:(TPH * c + i + 1) * P],
                                         w_out[:, :], start=True, stop=True)
                    made.then_inc(v_out, 1)
                part_end(pe, PARTS * b + 2)

                pe.wait_ge(tok_ready, 3 * b + 2)
                for c in range(2):
                    a_bank(16 + c)
                    turn(lambda i: xa[:, TPH * c + i, :], c).then_inc(a_out, 1)
                pe.wait_ge(a_taken, b * A_OUTS + 18 + 2)

                def step(s, turn_of, par, this, prev):
                    n = b * PAIRS + s
                    m = n - 1
                    rows_left = [(h, c) for h in range(2) for c in range(HALVES)] if prev else []

                    def max_row(h, c):
                        if c == 0:
                            pe.wait_ge(tops_ready, 2 * m + h + 1)
                        pe.wait_ge(misc_taken, 8 * m + 2 * h + c)
                        for i in range(TPH):
                            at = TPH * c + i
                            made = pe.matmul(ps[:, 7, i * P:(i + 1) * P], top_r[:, h, at:at + 1].broadcast_to((P, P)),
                                             identr[:, :], start=True, stop=True)
                        made.then_inc(misc_out, 1)

                    if this:
                        pe.wait_ge(w_pair_in[par], 16 * (b * (PAIRS // 2) + turn_of + 1))
                        for j in range(4):
                            for c in range(HALVES):
                                pe.wait_ge(proj_taken, 10 * n + 2 * j + c + 1)
                                pe.matmul(ps[:, c, :], w_pair[par][:, j, :], cut(xnT, c), start=True, stop=True
                                          ).then_inc(proj_out, 1)
                            if rows_left and j > 0:
                                max_row(*rows_left.pop(0))
                        for c in range(HALVES):
                            pe.wait_ge(proj_taken, 10 * n + 8 + c + 1)
                            for i in range(TPH):
                                at = TPH * c + i
                                made = pe.matmul(ps[:, c, i * P:(i + 1) * P], xnT[:, at * P:(at + 1) * P],
                                                 v_w[:, bass.ds(P * s, P)], start=True, stop=True)
                            made.then_inc(proj_out, 1)
                    while rows_left:
                        max_row(*rows_left.pop(0))
                    for kind, h, u in slots(prev, this):
                        if kind == "st":
                            c, j, q0 = ST[u]
                            w = HALF * (c + 1) - q0
                            if u == 0:
                                pe.wait_ge(misc_taken, 8 * m + 4)
                            pe.wait_ge(blocks_taken, 2 * NU * m + NU * h + u + 1)
                            o = ps[:, 4 + u % 2, 0:w]
                            own = q0 == P * j
                            rows_k = slice(0, HD + 1) if h == 0 else slice(0, P)
                            pe.matmul(o, k_high[1 - par][h][:, j * P:(j + 1) * P], q_split[1 - par][h][:, q0:q0 + w],
                                      start=True, stop=False)
                            made = pe.matmul(o, k_low[1 - par][h][rows_k, j * P:(j + 1) * P],
                                             q_max[1 - par][h][rows_k, q0:q0 + w], start=False, stop=not own)
                            if own:
                                made = pe.matmul(o[:, 0:P], identb[:, :], masks[:, 1, :], start=False, stop=True)
                            made.then_inc(blocks_out, 1)
                        elif kind == "pv":
                            c, i = u // TPH, u
                            if i % TPH == 0:
                                pe.wait_ge(pv_taken, 4 * m + 2 * h + c + 1)
                                pe.wait_ge(blocks_taken, 2 * NU * m + NU * h + (TPH, NU)[c] + 2)
                            at = (i % TPH) * (HD + 1)
                            for j in range(i + 1):
                                made = pe.matmul(ps[:, 6, at:at + HD + 1],
                                                 probs[:, TPH * c + j, (i % TPH) * P:(i % TPH + 1) * P],
                                                 vals[1 - par][:, j, h, :], start=(j == 0), stop=(j == i))
                            if i % TPH == TPH - 1:
                                made.then_inc(pv_out, 1)
                        elif kind == "mx":
                            i, k0, w = MX[u]
                            if u == 0:
                                pe.wait_ge(high_a, 4 * n + 4)
                                pe.wait_ge(high_p, 4 * n + 4)
                                pe.wait_ge(low_ready, 4 * n + 4)
                            pe.wait_ge(scores_taken, 2 * NU * n + NU * h + u + 1)
                            o = ps[:, 2 + u % 2, 0:w]
                            own = k0 + w == P * (i + 1)
                            made = pe.matmul(o, q_split[par][h][:, i * P:(i + 1) * P], k_high[par][h][:, k0:k0 + w],
                                             start=True, stop=not own)
                            if own:
                                made = pe.matmul(o[:, w - P:w], identb[:, :], masks[:, 0, :], start=False, stop=True)
                            made.then_inc(scores_out, 1)
                        elif kind == "ct":
                            pe.wait_ge(pv_taken, 4 * m + 2 + h + 2)
                            pe.wait_ge(misc_taken, 8 * m + 4 + 2 * h)
                            turn(lambda i: ctx_t[:, TPH * h + i, :], 7).then_inc(misc_out, 1)
                        elif kind == "op":
                            pe.wait_ge(misc_taken, 8 * m + 4 + 2 * h + 1)
                            for i in range(TPH):
                                made = pe.matmul(ps[:, 7, i * P:(i + 1) * P], ctxT[:, i * P:(i + 1) * P],
                                                 o_w[:, bass.ds(s - 1, 1), :].rearrange("p o n -> p (o n)"),
                                                 start=True, stop=True)
                            made.then_inc(misc_out, 1)

                step(0, 0, 0, True, False)
                with pe.Fori(0, PAIRS // 2 - 1) as r:
                    for k in range(2):
                        step(2 * r + 1 + k, r + k, 1 - k, True, True)
                step(PAIRS - 1, PAIRS // 2 - 1, 1, True, True)
                step(PAIRS, 0, 0, False, True)
                part_end(pe, PARTS * b + 3)

                pe.wait_ge(tok_ready, 3 * b + 3)
                for c in range(2):
                    a_bank(18 + c)
                    turn(lambda i: an[:, TPH * c + i, :], c).then_inc(a_out, 1)
                pe.wait_ge(a_taken, b * A_OUTS + 20 + 2)
                for i in range(TILES):
                    made = pe.matmul(ps[:, 6, i * EXPERTS:(i + 1) * EXPERTS], anT[:, i * P:(i + 1) * P], w_router[:, :],
                                     start=True, stop=True)
                made.then_inc(router_out, 1)
                pe.wait_ge(gates_ready, b + 1)
                for c in range(2):
                    a_bank(20 + c)
                    turn(lambda i: gates[:, TPH * c + i, :, :].rearrange("p a e -> p (a e)"), c, 96).then_inc(a_out, 1)
                pe.wait_ge(a_taken, b * A_OUTS + 22 + 2)
                for c in range(2):
                    pe.matmul(ps[:, 4 + c, :], b2_all[:, :], gT32[0:EXPERTS, c * HALF:(c + 1) * HALF], start=True,
                              stop=False, skip_group_check=True)
                pe.wait_ge(g3_ready, b + 1)

                def up(e, turn_of, slot, c):
                    k = HALVES * (b * EXPERTS + e) + c
                    if c == 0:
                        pe.wait_ge(w12_in[slot], 16 * (b * (EXPERTS // SLOTS) + turn_of + 1))
                    pe.wait_ge(hid_ready, k + 1)
                    pe.matmul(ps[:, c, :], w12[slot][:, 0, :], cut(anT, c), start=True, stop=True).then_inc(hid_out, 1)
                    pe.wait_ge(hg_ready, k + 1)
                    pe.matmul(ps[:, 2 + c, :], fold[:, bass.ds(e, 1)].broadcast_to((96, P)), cut(g3, c), start=True,
                              stop=True).then_inc(gate_out, 1)

                def down(e, slot, c):
                    k = HALVES * (b * EXPERTS + e) + c
                    pe.wait_ge(hg_ready, k + 3)
                    pe.matmul(ps[:, 4 + c, :], w12[slot][:, 1, :], hg[:, c, :], start=False, stop=False,
                              skip_group_check=True).then_inc(down_done, 1)

                for c in range(2):
                    up(0, 0, 0, c)
                with pe.Fori(0, EXPERTS // SLOTS - 1) as r:
                    for i in range(SLOTS):
                        for c in range(2):
                            down(SLOTS * r + i, i, c)
                            up(SLOTS * r + i + 1, r + (i + 1) // SLOTS, (i + 1) % SLOTS, c)
                for i in range(SLOTS):
                    for c in range(2):
                        down(EXPERTS - SLOTS + i, i, c)
                        if i < SLOTS - 1:
                            up(EXPERTS - SLOTS + i + 1, EXPERTS // SLOTS - 1, i + 1, c)
                for c in range(2):
                    pe.wait_ge(moe_taken, 2 * b + c + 1)
                    v_bank(4 + c)
                    turn(lambda i: moeT[:, (TPH * c + i) * P:(TPH * c + i + 1) * P], 2 + c).then_inc(v_out, 1)
                part_end(pe, PARTS * b + 4)


def constants():
    eye = np.eye(P, dtype=np.float32)
    q, k = np.arange(P)[:, None], np.arange(P)[None, :]
    masks = np.stack([np.where(k > q, MASKED, 0.0), np.where(k < q, MASKED, 0.0)], 1).astype(np.float32)
    fold = (np.arange(96)[:, None] % 32 == np.arange(32)[None, :]).astype(np.float32)
    resets = (np.arange(TILES * EXPERTS) % EXPERTS != 0).astype(np.float32)[None]
    return dict(c_ident=eye, c_masks=masks, c_fold=fold, c_pos=np.arange(SEQ, dtype=np.float32)[None], c_resets=resets)


def kernel(**inputs):
    import concourse.bacc as bacc
    from concourse.bass_utils import run_bass_kernel_spmd

    x = {k: np.asarray(v) for k, v in inputs.items()}
    m = {k[len("L0_attn_"):]: v for k, v in x.items() if k.startswith("L0_attn_")}
    f = {k[len("L0_ffn_"):]: v for k, v in x.items() if k.startswith("L0_ffn_")}
    f32 = np.float32

    def thrice(w):
        out = np.zeros((w.shape[0], 96), f32)
        for i in range(3):
            out[:, 32 * i:32 * i + w.shape[1]] = w
        return out

    cols = np.zeros((P, NCOLS), f32)
    cols[:, C_B_IN], cols[:, C_CONV_B], cols[:, C_B_D2], cols[:, C_D] = m["b_in"], m["conv_b"], m["b_d2"], m["D"]
    cols[:96, C_B_B], cols[:96, C_B_C] = thrice(m["b_B"][None])[0], thrice(m["b_C"][None])[0]
    cols[:DT_RANK, C_B_D1] = m["b_d1"]
    cols[:, C_THETA] = np.tile(f["theta"], P // f["theta"].shape[0])
    cols[:, C_SIGN] = np.where(np.arange(P) % HD < HD // 2, -1.0, 1.0)
    cols[:, C_ALOG:C_ALOG + STATES] = m["A_log"]
    cols[:, C_B1:C_B1 + ROUTED], cols[:, C_B1 + ROUTED] = f["re_b1"].T, f["sh_b1"]
    order = np.concatenate([np.arange(0, HD, 2), np.arange(1, HD, 2)])
    swapped = np.concatenate([np.arange(1, HD, 2), np.arange(0, HD, 2)])
    pick = [np.concatenate([HD * h + o for h in range(HEADS)]) for o in (order, swapped)]
    w_pairs = np.zeros((PAIRS, P, 4, P), f32)
    for j, name in enumerate("qk"):
        for i in range(2):
            w = f[name + "_w"][:, pick[i]].reshape(DM, PAIRS, P)
            w_pairs[:, :, 2 * j + i, :] = w.transpose(1, 0, 2)
            cols[:, C_QK + 2 * j + i::4] = f[name + "_b"][pick[i]].reshape(PAIRS, P).T
    rows = np.stack([m["b_out"], f["gamma1"], f["gamma2"], f["o_b"]])
    w12 = np.zeros((EXPERTS, P, 2, P), f32)
    w12[:ROUTED, :, 0], w12[ROUTED, :, 0] = f["re_w1"], f["sh_w1"]
    w12[:ROUTED, :, 1], w12[ROUTED, :, 1] = f["re_w2"], f["sh_w2"]
    router_w = np.zeros((DM, EXPERTS), f32)
    router_w[:, :ROUTED] = f["router_w"]
    router_b = np.zeros((1, EXPERTS), f32)
    router_b[0, :ROUTED] = f["router_b"]
    arrays = dict(
        x=m["x"], w_in=m["w_in"].T, conv_w=m["conv_w"].transpose(1, 2, 0), w_b3=thrice(m["w_B"].T),
        w_c3=thrice(m["w_C"].T), w_d1=m["w_d1"].T, w_d2=m["w_d2"].T, w_out=m["w_out"].T, cols=cols, rows=rows,
        w_pairs=w_pairs, v_w=f["v_w"], v_b=f["v_b"][None], o_w=f["o_w"].reshape(PAIRS, P, DM).transpose(1, 0, 2),
        w12=w12, b2=np.concatenate([f["re_b2"], f["sh_b2"][None]]), router_w=router_w, router_b=router_b,
        **constants())
    nc = bacc.Bacc("TRN2", target_bir_lowering=False, num_devices=1)
    arrays = {"in_" + k: np.ascontiguousarray(v) for k, v in arrays.items()}
    ins = {k[3:]: nc.dram_tensor(k, v.shape, mybir.dt.from_np(v.dtype), kind="ExternalInput").ap()
           for k, v in arrays.items()}
    out = nc.dram_tensor("out_0", (BATCH, SEQ, DM), F32, kind="ExternalOutput").ap()
    program(nc, ins, out)
    r = run_bass_kernel_spmd(nc, [arrays], core_ids=[0])
    return r.results[0]["out_0"]
```

```python
from contextlib import ExitStack

import numpy as np

import concourse.bass as bass
from concourse import mybir

ALU = mybir.AluOpType
ACT = mybir.ActivationFunctionType
AX_X = mybir.AxisListType.X
F32 = mybir.dt.float32
F32R = mybir.dt.float32r
BF16 = mybir.dt.bfloat16

P = 128
BATCH, SEQ, DM = 4, 1024, 128
TILES = SEQ // P
HALF = 512
HALVES = SEQ // HALF
TPH = HALF // P
STATES = 16
DT_RANK = 8
HEADS, HD = 16, 64
PAIRS = HEADS // 2
EXPERTS = 32
ROUTED = 31
TOP = 3
SLOTS = 4
EPS = 1e-5
SCALE = HD ** -0.5
MASKED = -1e30
ENGINES = 5

C_B_IN, C_CONV_B, C_B_B, C_B_C, C_B_D1, C_B_D2, C_D, C_THETA, C_TURN, C_PHASE, C_SIGN = range(11)
C_ALOG = 11
C_B1 = C_ALOG + STATES
C_QK = C_B1 + EXPERTS
NCOLS = C_QK + 4 * PAIRS

TWO_PI_A = 6.28125
TWO_PI_B = float(np.float32(np.round((2 * np.pi - TWO_PI_A) * 2.0 ** 17) / 2.0 ** 17))
TWO_PI_C = float(np.float32(2 * np.pi - TWO_PI_A - TWO_PI_B))
ROUNDER = float(1.5 * 2 ** 23)
PI_BELOW = 3.1415925


def st_units():
    return [(c, j, max(P * j, HALF * c)) for c in range(HALVES) for j in range(TPH * (c + 1))]


def max_units():
    out = []
    for i in range(TILES):
        end = P * (i + 1)
        out.append((i, 0, min(end, HALF)))
        if end > HALF:
            out.append((i, HALF, end - HALF))
    return out


ST = st_units()
MX = max_units()
NU = len(ST)


RING = 6
PV_LAG = 2
HALF_START = (0, TPH)
HALF_END = (TPH, NU)


def adds_with(u):
    c, j, _ = ST[u]
    return (1, TPH)[c] + max(j, 1)


ADDS = adds_with(NU - 1)


def slots(do_prev, do_this):
    mx = [("mx", h, u) for h in range(2) for u in range(NU)]
    out = []
    for u in range(NU + PV_LAG):
        def rows():
            return [mx.pop(0)] if do_this and u >= MX_FROM and mx else []

        if do_prev and u < NU:
            out.append(("st", 0, u))
            out += rows()
            out.append(("st", 1, u))
        out += rows()
        if do_prev and u >= PV_LAG:
            out.append(("pv", 0, u - PV_LAG))
        out += rows()
        if do_prev and 1 <= u <= NU:
            out.append(("add", 0, u - 1))
        if do_this and u == MX_FROM - 1:
            out.append(("low", 0, 0))
        if do_prev and u == OLD_OP_AT:
            out.append(("op", 1, 0))
        if do_prev and u == SUM_AT:
            out.append(("sum", 0, 0))
        if do_prev and SUM_AT < u <= SUM_AT + INV_PARTS:
            out.append(("inv", 0, u - SUM_AT - 1))
        if do_prev and u == OP_AT:
            out.append(("op", 0, 0))
    return out + (mx if do_this else [])


MX_FROM = 4
OLD_OP_AT = 2
SUM_AT = 6
OP_AT = 12
INV_PARTS = 4
PART = HALF // INV_PARTS


def row_at(m, k, first):
    return 8 * m + k - (0 if first else 1)


def sum_at(m, c):
    return 8 * m + 4 + 2 * c


def op_at(m, c, last):
    return 8 * m + (5 if c == 0 else 7 if last else 11)


def program(nc, ins, out):
    with ExitStack() as ctx:
        def sb(name, shape, dt=F32, where=None):
            return (where or ctx).enter_context(nc.sbuf_tensor(name, shape, dt))

        def sem(name):
            return ctx.enter_context(nc.semaphore(name))

        ident = sb("ident", [P, P])
        identr = sb("identr", [P, P], F32R)
        identb = sb("identb", [P, P], BF16)
        masks32 = sb("masks32", [P, 2, P])
        masks = sb("masks", [P, 2, P], BF16)
        fold32 = sb("fold32", [96, 32])
        fold = sb("fold", [96, 32], BF16)
        mean_of = sb("mean_of", [P, P])
        diag_d = sb("diag_d", [P, P])
        neg_a = sb("neg_a", [P, STATES])
        exp_a = sb("exp_a", [P, STATES])
        neg_half = sb("neg_half", [P, TILES])
        cols = sb("cols", [P, NCOLS])
        cos_t = sb("cos_t", [P, SEQ])
        sin_t = sb("sin_t", [P, SEQ])
        w_in = sb("w_in", [P, P])
        w_conv = sb("w_conv", [P, 3, P])
        w_b3 = sb("w_b3", [P, 96])
        w_c3 = sb("w_c3", [P, 96])
        w_d1 = sb("w_d1", [P, DT_RANK])
        w_d2 = sb("w_d2", [DT_RANK, P])
        w_out = sb("w_out", [P, P])
        w_router = sb("w_router", [P, EXPERTS])
        b2_all = sb("b2_all", [EXPERTS, P])
        rows = sb("rows", [P, 4, P])
        router_b = sb("router_b", [P, EXPERTS])
        v_b = sb("v_b", [P, HEADS * HD])
        v_w = sb("v_w", [P, HEADS * HD])
        o_w = sb("o_w", [P, PAIRS, P])
        resets = sb("resets", [P, TILES * EXPERTS])
        b_out_r, gamma1_r, gamma2_r, o_b_r = (rows[:, i, :] for i in range(4))

        xin = sb("xin", [P, TILES, P])
        resid = sb("resid", [P, TILES, P])
        partial = sb("partial", [P, 2])
        glob = sb("glob", [P, 3])
        stats = sb("stats", [P, TILES, 6])
        mv = sb("mv", [P, TILES, 2])
        ms = sb("ms", [P, TILES])
        rstd = sb("rstd", [P, TILES])
        nmb = sb("nmb", [P, TILES])

        hpad = sb("hpad", [P, SEQ + 2])
        acc = sb("acc", [P, TILES, P], F32)
        vals = [sb(f"vals{i}", [P, TILES, 2, HD], F32) for i in range(2)]
        ones = sb("ones", [P, HD])
        q_max = [[sb(f"q_max{i}{h}", [P, SEQ], F32R) for h in range(2)] for i in range(2)]
        k_low = [[sb(f"k_low{i}{h}", [P, SEQ], F32R) for h in range(2)] for i in range(2)]

        m_ctx = ExitStack()
        x0 = sb("x0", [P, TILES, P], F32, m_ctx)
        xnT_m = sb("xnT_m", [P, SEQ], F32, m_ctx)
        gate = sb("gate", [P, SEQ], F32, m_ctx)
        hc = sb("hc", [P, SEQ], F32, m_ctx)
        h_act = sb("h_act", [P, SEQ], F32, m_ctx)
        bc32 = sb("bc32", [96, 2, SEQ], F32, m_ctx)
        bc_rest = sb("bc_rest", [96, SEQ], F32, m_ctx)
        bc_mid = sb("bc_mid", [96, SEQ], BF16, m_ctx)
        bc3 = sb("bc3", [96, 2, SEQ], BF16, m_ctx)
        d1 = sb("d1", [DT_RANK, SEQ], F32, m_ctx)
        z_abs = sb("z_abs", [P, SEQ], F32, m_ctx)
        z = sb("z", [P, SEQ], F32, m_ctx)
        sp_log = sb("sp_log", [P, SEQ], F32, m_ctx)
        delta = sb("delta", [P, SEQ], F32, m_ctx)
        du = sb("du", [P, SEQ], F32, m_ctx)
        decay = sb("decay", [P, 2, SEQ], F32, m_ctx)
        b_rows = sb("b_rows", [P, 2, SEQ], F32, m_ctx)
        bx = sb("bx", [P, 2, SEQ], F32, m_ctx)
        state = sb("state", [P, 2, SEQ], F32, m_ctx)
        cs = sb("cs", [P, 2, SEQ], F32, m_ctx)
        g_tok = sb("g_tok", [P, TILES, P], F32, m_ctx)
        gT = sb("gT", [P, SEQ], F32, m_ctx)
        m_ctx.close()

        a_ctx = ExitStack()
        xa = sb("xa", [P, TILES, P], F32, a_ctx)
        xnT = sb("xnT", [P, SEQ], F32, a_ctx)
        w_pair = [sb(f"w_pair{i}", [P, 4, P], F32, a_ctx) for i in range(2)]
        turned = sb("turned", [P, 4, SEQ], F32, a_ctx)
        roped = sb("roped", [P, 2, SEQ], F32, a_ctx)
        q_split = [[sb(f"q_split{i}{h}", [P, SEQ], F32R, a_ctx) for h in range(2)] for i in range(2)]
        k_high = [[sb(f"k_high{i}{h}", [P, SEQ], F32R, a_ctx) for h in range(2)] for i in range(2)]
        probs = sb("probs", [P, RING, 2, HALF], F32, a_ctx)
        prob_sums = sb("prob_sums", [P, 2, HALVES, HALF], F32, a_ctx)
        tops = sb("tops", [P, 2, NU], F32, a_ctx)
        top_r = sb("top_r", [P, 2, TILES], F32R, a_ctx)
        sums = sb("sums", [P, HALF], F32, a_ctx)
        inverse = sb("inverse", [P, HALF], F32, a_ctx)
        ctxT = sb("ctxT", [P, HALVES, HALF], F32, a_ctx)
        a_ctx.close()

        e_ctx = ExitStack()
        an = sb("an", [P, TILES, P], F32, e_ctx)
        anT = sb("anT", [P, SEQ], F32, e_ctx)
        logits = sb("logits", [P, TILES, EXPERTS], F32, e_ctx)
        aff = sb("aff", [P, TILES, EXPERTS], F32, e_ctx)
        big8 = sb("big8", [P, TILES, 8], F32, e_ctx)
        above = sb("above", [P, TILES, EXPERTS], F32, e_ctx)
        equal = sb("equal", [P, TILES, EXPERTS], F32, e_ctx)
        struck = sb("struck", [P, TILES, EXPERTS], F32, e_ctx)
        gates = sb("gates", [P, TILES, 3, EXPERTS], F32, e_ctx)
        red = sb("red", [P, 2, TILES], F32, e_ctx)
        gT32 = sb("gT32", [96, SEQ], F32, e_ctx)
        g_rest = sb("g_rest", [96, SEQ], F32, e_ctx)
        g_mid = sb("g_mid", [96, SEQ], BF16, e_ctx)
        g3 = sb("g3", [96, SEQ], BF16, e_ctx)
        w12 = [sb(f"w12_{i}", [P, 2, P], F32, e_ctx) for i in range(SLOTS)]
        hid = sb("hid", [P, 2, HALF], F32, e_ctx)
        hg = sb("hg", [P, 2, HALF], F32, e_ctx)
        moeT = sb("moeT", [P, SEQ], F32, e_ctx)
        y_out = sb("y_out", [P, TILES, P], F32, e_ctx)
        e_ctx.close()

        s_ctx = ExitStack()
        pos = sb("pos", [P, SEQ], F32, s_ctx)
        ang = sb("ang", [P, SEQ], F32, s_ctx)
        turns = sb("turns", [P, 2, SEQ], F32, s_ctx)
        whole = sb("whole", [P, SEQ], F32, s_ctx)
        sin_raw = sb("sin_raw", [P, SEQ], F32, s_ctx)
        s_ctx.close()

        ps = ctx.enter_context(nc.psum_tensor("ps", [P, 8, HALF], F32))

        def banks(a, n=2):
            return ps[:, a:a + n, :].rearrange("p a n -> p (a n)")

        passed, part_done, weights_in = sem("passed"), sem("part_done"), sem("weights_in")
        p_setup, v_setup, a_setup = sem("p_setup"), sem("v_setup"), sem("a_setup")
        x_in = sem("x_in")
        v_step = sem("v_step")
        p_step = sem("p_step")
        a_step = sem("a_step")
        ms_ready, ms_plus, rstd_ready = sem("ms_ready"), sem("ms_plus"), sem("rstd_ready")
        partial_ready, global_sum = sem("partial_ready"), sem("global_sum")
        a_out, a_taken = sem("a_out"), sem("a_taken")
        v_out, v_taken = sem("v_out"), sem("v_taken")
        tok_ready, v_norm, yg_ready = sem("tok_ready"), sem("v_norm"), sem("yg_ready")
        split_ready, delta_ready = sem("split_ready"), sem("delta_ready")
        b_bcast, b_taken, c_bcast = sem("b_bcast"), sem("b_taken"), sem("c_bcast")
        decay_ready, bx_ready, scanned, cs_ready, cs_used = (
            sem("decay_ready"), sem("bx_ready"), sem("scanned"), sem("cs_ready"), sem("cs_used"))
        w_pair_in = [sem(f"w_pair_in{i}") for i in range(2)]
        proj_out, proj_taken = sem("proj_out"), sem("proj_taken")
        roped_ready, high_a, high_p, low_ready = sem("roped_ready"), sem("high_a"), sem("high_p"), sem("low_ready")
        scores_out, scores_taken = sem("scores_out"), sem("scores_taken")
        blocks_out, blocks_taken = sem("blocks_out"), sem("blocks_taken")
        tops_ready, misc_out, misc_taken = sem("tops_ready"), sem("misc_out"), sem("misc_taken")
        pv_out, v_added, p_added, ctx_ready = sem("pv_out"), sem("v_added"), sem("p_added"), sem("ctx_ready")
        acc_ready, resid_ready = sem("acc_ready"), sem("resid_ready")
        w12_in = [sem(f"w12_in{i}") for i in range(SLOTS)]
        router_out, aff_asked, aff_ready = sem("router_out"), sem("aff_asked"), sem("aff_ready")
        hid_out, hid_ready, gate_out, hg_ready, down_done = (
            sem("hid_out"), sem("hid_ready"), sem("gate_out"), sem("hg_ready"), sem("down_done"))
        inverted = sem("inverted")
        low_p = sem("low_p")
        gates_ready, g3_ready = sem("gates_ready"), sem("g3_ready")
        moe_taken, y_stored = sem("moe_taken"), sem("y_stored")

        CREDITS = [(a_taken, 2), (v_taken, 2), (scanned, 2), (bx_ready, 2), (cs_used, 2), (b_taken, 1), (cs_ready, 2),
                   (proj_taken, 2), (scores_taken, 2), (blocks_taken, 2), (pv_out, NU), (v_added, ADDS), (p_added, ADDS),
                   (ctx_ready, 4),
                   (high_a, 1), (high_p, 1), (low_ready, 1), (roped_ready, 1), (inverted, 1), (misc_taken, 1),
                   (hid_ready, 2), (hg_ready, 2), (down_done, 2)]

        block = ctx.enter_context(nc.Block())

        class Steps:

            def __init__(self, eng, s, base=0):
                self.eng, self.s, self.base, self.n = eng, s, base, 0

            def did(self, made):
                made.then_inc(self.s, 1)
                self.n += 1

            def wait(self):
                self.eng.wait_ge(self.s, self.base + self.n)

            def link(self, made):
                self.did(made)
                self.wait()

        PARTS, V_ANGLES, V_STEPS, V_OUTS, A_OUTS, A_STEPS = 3, 14, 136, 6, 22, 5

        CTX_BANK = (0, 6)

        def part_end(eng, k):
            eng.sem_inc(passed, 1)
            eng.drain().then_inc(part_done, 1)
            eng.wait_ge(part_done, ENGINES * k)
            eng.sem_inc(passed, 1)

        def both(t):
            return t.rearrange("p i d -> p (i d)")

        loads = [(ident[:, :], ins["c_ident"]), (masks32[:, :, :], ins["c_masks"]), (fold32[:, :], ins["c_fold"]),
                 (pos[:, :], ins["c_pos"].broadcast_to((P, SEQ))), (cols[:, :], ins["cols"]),
                 (resets[:, :], ins["c_resets"].broadcast_to((P, TILES * EXPERTS))),
                 (w_in[:, :], ins["w_in"]), (w_conv[:, :, :], ins["conv_w"]), (w_b3[:, :], ins["w_b3"]),
                 (w_c3[:, :], ins["w_c3"]), (w_d1[:, :], ins["w_d1"]), (w_d2[:, :], ins["w_d2"]),
                 (w_out[:, :], ins["w_out"]), (w_router[:, :], ins["router_w"]), (b2_all[:, :], ins["b2"]),
                 (v_w[:, :], ins["v_w"]), (o_w[:, :, :], ins["o_w"]),
                 (router_b[:, :], ins["router_b"].broadcast_to((P, EXPERTS))),
                 (v_b[:, :], ins["v_b"].broadcast_to((P, HEADS * HD)))]
        loads += [(rows[:, i, :], ins["rows"][i:i + 1, :].broadcast_to((P, P))) for i in range(4)]
        ALL_IN = 16 * len(loads)

        @block.sync
        def _(sp):
            for dst, src in loads:
                sp.dma_start(dst, src).then_inc(weights_in, 16)
            part_end(sp, 1)
            with sp.Fori(0, BATCH) as b:
                sp.dma_start(xin[:, :, :], ins["x"][bass.ds(b, 1), :, :].rearrange("o (i p) d -> p (o i) d", p=P)
                             ).then_inc(x_in, 16)
                part_end(sp, PARTS * b + 2)

                def load_pair(pair, buf):
                    sp.dma_start(w_pair[buf][:, :, :], ins["w_pairs"][bass.ds(pair, 1), :, :, :].rearrange(
                        "o p s n -> p (o s) n")).then_inc(w_pair_in[buf], 16)

                load_pair(0, 0)
                load_pair(1, 1)
                with sp.Fori(0, PAIRS // 2 - 1) as r:
                    for k in range(2):
                        sp.wait_ge(proj_out, 10 * (b * PAIRS + 2 * r + k) + 8)
                        sp.sem_inc(passed, 1)
                        load_pair(2 * r + 2 + k, k)
                part_end(sp, PARTS * b + 3)
                for k in range(SLOTS):
                    sp.dma_start(w12[k][:, :, :], ins["w12"][k, :, :, :]).then_inc(w12_in[k], 16)
                with sp.Fori(1, EXPERTS // SLOTS) as r:
                    for k in range(SLOTS):
                        sp.wait_ge(down_done, 2 + HALVES * (b * EXPERTS + (r - 1) * SLOTS + k + 1))
                        sp.sem_inc(passed, 1)
                        sp.dma_start(w12[k][:, :, :], ins["w12"][bass.ds(r * SLOTS + k, 1), :, :, :].rearrange(
                            "o p s n -> p (o s) n")).then_inc(w12_in[k], 16)
                sp.wait_ge(v_taken, V_OUTS * (b + 1) + 2)
                sp.dma_start(out[bass.ds(b, 1), :, :].rearrange("o (i p) d -> p (o i) d", p=P), y_out[:, :, :]
                             ).then_inc(y_stored, 16)
                sp.wait_ge(y_stored, 16 * b + 16)
                part_end(sp, PARTS * b + 4)
            sp.wait_ge(y_stored, 16 * BATCH)

        def pool_copy(pool, dst, src):
            return pool.tensor_scalar(dst, src, 1.0, 0.0, ALU.mult, ALU.add)

        RSTDS = 7
        P_STEPS = 3

        @block.gpsimd
        def _(pool):
            for s, c in CREDITS:
                pool.sem_inc(s, c)
            pool.memset(nmb[:, :], 0.0)
            pool.memset(neg_half[:, :], -0.5)
            pool.memset(mean_of[:, :], 1.0 / P)
            pool.memset(ones[:, :], 1.0)
            pool.memset(hpad[:, 0:1], 0.0)
            pool.memset(hpad[:, SEQ + 1:SEQ + 2], 0.0).then_inc(p_setup, 1)
            pool.wait_ge(p_setup, 1)
            part_end(pool, 1)
            with pool.Fori(0, BATCH) as b:
                steps = Steps(pool, p_step, b * P_STEPS)

                def inverse_root(k, n):
                    pool.wait_ge(ms_ready, b * RSTDS + k)
                    pool.sem_inc(passed, 1)
                    pool.tensor_scalar(ms[:, 0:n], ms[:, 0:n], EPS, None, ALU.add).then_inc(ms_plus, 1)
                    pool.wait_ge(ms_plus, b * RSTDS + k)
                    pool.tensor_tensor(rstd[:, 0:n], ms[:, 0:n], neg_half[:, 0:n], ALU.pow).then_inc(rstd_ready, 1)

                inverse_root(1, TILES)
                pool.wait_ge(tok_ready, 3 * b + 1)
                steps.link(pool.tensor_tensor(both(resid[:, :, :]), both(xin[:, :, :]), both(x0[:, :, :]), ALU.add))
                steps.link(pool.tensor_tensor(resid[:, :, :], resid[:, :, :],
                                              b_out_r.unsqueeze(1).broadcast_to((P, TILES, P)), ALU.add))
                inverse_root(2, 1)
                inverse_root(3, 1)
                pool.wait_ge(delta_ready, b + 1)
                pool.sem_inc(passed, 1)
                with pool.Fori(0, STATES // 2) as r:
                    for k in range(2):
                        n = b * STATES + 2 * r + k
                        pool.wait_ge(b_taken, n + 2)
                        pool.wait_ge(scanned, n + 1)
                        pool.tensor_tensor(bx[:, k, :], du[:, :], b_rows[:, k, :], ALU.mult).then_inc(bx_ready, 1)
                inverse_root(4, TILES)
                part_end(pool, PARTS * b + 2)
                inverse_root(5, TILES)
                inverse_root(6, TILES)
                pool.wait_ge(tok_ready, 3 * b + 2)
                pool.tensor_tensor(acc[:, :, :], xa[:, :, :], o_b_r.unsqueeze(1).broadcast_to((P, TILES, P)),
                                   ALU.add).then_inc(acc_ready, 1)

                def step(s, par, this, prev, prev2):
                    n = b * PAIRS + s
                    m = n - 1
                    copies = [(q_max[par][0][0:HD, :], roped[0:HD, 0, :]), (q_max[par][1][HD:P, :], roped[HD:P, 0, :]),
                              (k_high[par][0][HD:P, :], roped[0:HD, 1, :]), (k_high[par][1][HD:P, :], roped[HD:P, 1, :])]
                    for k in range(2 if this else 0):
                        pool.wait_ge(proj_taken, 10 * n + 4 * k + 4 + 2)
                        pool.wait_ge(high_a, 4 * n + 1)
                        pool.wait_ge(low_ready, 3 * n + 1)
                        pool.wait_ge(high_p, 4 * n + 1)
                        pool.tensor_tensor(roped[:, k, :], turned[:, 2 * k, :], turned[:, 2 * k + 1, :], ALU.add
                                           ).then_inc(roped_ready, 1)
                        pool.wait_ge(roped_ready, 2 * n + k + 2)
                        for i in (2 * k, 2 * k + 1):
                            pool.sem_inc(passed, 1)
                            pool_copy(pool, *copies[i]).then_inc(high_p, 1)
                            pool.wait_ge(high_p, 4 * n + i + 2)
                            pool.sem_inc(passed, 1)
                    for kind, _, u in slots(prev, this):
                        if kind == "low":
                            if prev:
                                pool.wait_ge(p_added, ADDS * (m + 1) + adds_with(MX_FROM - 2))
                            pool.tensor_tensor(k_low[par][1][HD:P, :], roped[HD:P, 1, :],
                                               k_high[par][1][HD:P, :].bitcast(F32), ALU.subtract).then_inc(low_p, 1)
                            pool.wait_ge(low_p, n + 1)
                        if kind != "add":
                            continue
                        c, j, q0 = ST[u]
                        at = q0 - HALF * c
                        if u == 0:
                            pool.wait_ge(blocks_taken, 2 * NU * m + 2 + 2)
                            pool.wait_ge(misc_taken, row_at(m, 4, not prev2) + 1)
                            pool.sem_inc(passed, 1)
                            pool_copy(pool, prob_sums[:, 1, 0, 0:P], probs[:, 0, 1, 0:P]).then_inc(p_added, 1)
                        if j > 0:
                            pool.wait_ge(blocks_taken, 2 * (NU * m + u + 1) + 2)
                            pool.wait_ge(p_added, ADDS * (m + 1) + adds_with(u) - 1)
                            total = prob_sums[:, 1, c, at:HALF]
                            before = probs[:, (u - 1) % RING, 1, at:HALF] if j == 1 else total
                            pool.tensor_tensor(total, before, probs[:, u % RING, 1, at:HALF], ALU.add).then_inc(p_added, 1)

                step(0, 0, True, False, False)
                step(1, 1, True, True, False)
                with pool.Fori(0, PAIRS // 2 - 1) as r:
                    for k in range(2):
                        step(2 * r + 2 + k, k, True, True, True)
                step(PAIRS, 0, False, True, True)
                part_end(pool, PARTS * b + 3)
                inverse_root(7, TILES)
                pool.wait_ge(ms_ready, b * RSTDS + RSTDS)
                steps.link(pool.tensor_tensor(both(resid[:, :, :]), both(resid[:, :, :]), both(acc[:, :, :]), ALU.add))
                pool.wait_ge(tok_ready, 3 * b + 3)
                pool.tensor_tensor(both(resid[:, :, :]), both(resid[:, :, :]), both(an[:, :, :]), ALU.add
                                   ).then_inc(resid_ready, 1)
                part_end(pool, PARTS * b + 4)


        @block.scalar
        def _(act):
            act.wait_ge(weights_in, ALL_IN)
            act.activation(exp_a[:, :], cols[:, C_ALOG:C_ALOG + STATES], ACT.Exp).then_inc(a_setup, 1)
            act.wait_ge(v_setup, V_ANGLES)
            act.activation(sin_raw[:, :], turns[:, 0, :], ACT.Sin).then_inc(a_setup, 1)
            act.activation(cos_t[:, :], turns[:, 1, :], ACT.Sin).then_inc(a_setup, 1)
            part_end(act, 1)
            with act.Fori(0, BATCH) as b:
                def take(k, n, dst, func, bias=0.0, scale=1.0):
                    act.wait_ge(a_out, b * A_OUTS + k + 1)
                    act.activation(dst, ps[0:n, k % 2, :], func, bias=bias, scale=scale).then_inc(a_taken, 1)

                def col(c, n=P):
                    return cols[0:n, c:c + 1]

                act.wait_ge(v_norm, 2 * b + 1)
                for c in range(2):
                    take(c, P, xnT_m[:, c * HALF:(c + 1) * HALF], ACT.Identity, nmb[:, 0:1], rstd[:, 0:1])
                for c in range(2):
                    take(2 + c, P, hpad[:, 1 + c * HALF:1 + (c + 1) * HALF], ACT.Identity, col(C_B_IN))
                act.wait_ge(a_taken, b * A_OUTS + 4 + 2)
                act.activation(gate[:, :], hpad[:, 1:1 + SEQ], ACT.Silu).then_inc(a_step, 1)
                for c in range(2):
                    take(4 + c, P, hc[:, c * HALF:(c + 1) * HALF], ACT.Identity, col(C_CONV_B))
                act.wait_ge(v_norm, 2 * b + 2)
                act.wait_ge(a_taken, b * A_OUTS + 6 + 2)
                act.activation(h_act[:, :], hc[:, :], ACT.Silu, bias=nmb[:, 0:1], scale=rstd[:, 0:1]).then_inc(a_step, 1)
                for j in range(2):
                    for c in range(2):
                        take(6 + 2 * j + c, 96, bc32[:, j, c * HALF:(c + 1) * HALF], ACT.Identity,
                             col((C_B_B, C_B_C)[j], 96))
                for c in range(2):
                    take(10 + c, DT_RANK, d1[:, c * HALF:(c + 1) * HALF], ACT.Identity, col(C_B_D1, DT_RANK))
                for c in range(2):
                    take(12 + c, P, z[:, c * HALF:(c + 1) * HALF], ACT.Identity, col(C_B_D2))
                act.wait_ge(a_taken, b * A_OUTS + 14 + 2)
                act.activation(z_abs[:, :], z[:, :], ACT.Abs).then_inc(a_step, 1)
                act.wait_ge(a_step, A_STEPS * b + 3)
                act.activation(z_abs[:, :], z_abs[:, :], ACT.Exp, scale=-1.0).then_inc(a_step, 1)
                act.wait_ge(a_step, A_STEPS * b + 4)
                act.activation(sp_log[:, :], z_abs[:, :], ACT.Ln, bias=1.0).then_inc(a_step, 1)
                act.wait_ge(delta_ready, b + 1)
                act.sem_inc(passed, 1)
                act.sem_inc(passed, 1)
                act.preload_act_table(ACT.Exp)
                with act.Fori(0, STATES // 2) as r:
                    for k in range(2):
                        n = b * STATES + 2 * r + k
                        act.wait_ge(scanned, n + 1)
                        act.sem_inc(passed, 1)
                        act.activation(decay[:, k, :], delta[:, :], ACT.Exp,
                                       scale=neg_a[:, bass.ds(2 * r + k, 1)]).then_inc(decay_ready, 1)
                        act.wait_ge(b_bcast, n + 1)
                        act.wait_ge(bx_ready, n + 1)
                        act.activation(b_rows[:, k, :], banks(2), ACT.Copy).then_inc(b_taken, 1)
                for c in range(2):
                    take(14 + c, P, gT[:, c * HALF:(c + 1) * HALF], ACT.Identity)
                part_end(act, PARTS * b + 2)
                for c in range(2):
                    take(16 + c, P, xnT[:, c * HALF:(c + 1) * HALF], ACT.Identity)

                def keep_sums(m, c):
                    act.wait_ge(misc_out, sum_at(m, c) + 1)
                    act.wait_ge(inverted, INV_PARTS * (2 * m + c) + 1)
                    act.activation(sums[:, :], ps[:, 7, :], ACT.Copy).then_inc(misc_taken, 1)

                def step(s, par, this, prev, prev2):
                    n = b * PAIRS + s
                    m = n - 1
                    if prev2:
                        keep_sums(n - 2, 1)
                    if prev:
                        for h in range(2):
                            at = HD if h == 0 else 0
                            for c in range(HALVES):
                                act.wait_ge(misc_out, row_at(m, 2 * h + c, not prev2) + 1)
                                act.activation(q_max[1 - par][h][at:at + 1, c * HALF:(c + 1) * HALF],
                                               ps[at:at + 1, 7, :], ACT.Copy, scale=-1.0).then_inc(misc_taken, 1)

                    def high(k):
                        dst = (q_split, k_high)[k][par]
                        act.wait_ge(roped_ready, 2 * n + k + 2)
                        for h in range(2):
                            act.activation(dst[h][0:HD, :], roped[HD * h:HD * h + HD, k, :], ACT.Copy
                                           ).then_inc(high_a, 1)

                    if this:
                        high(0)
                    if this and not prev:
                        high(1)
                    for kind, h, u in slots(prev, this):
                        if kind == "st":
                            c, j, q0 = ST[u]
                            w = HALF * (c + 1) - q0
                            act.wait_ge(blocks_out, 2 * (NU * m + u) + h + 1)
                            used = u + NU - RING
                            behind = u < RING
                            act.wait_ge(pv_out, NU * (m + 1 - behind) + used % NU + 1)
                            act.wait_ge((v_added, p_added)[h], ADDS * (m + 1 - behind) + adds_with(used % NU))
                            act.activation(probs[:, u % RING, h, q0 - HALF * c:HALF], ps[:, 4 + h, 0:w], ACT.Exp,
                                           scale=SCALE).then_inc(blocks_taken, 1)
                            if this and h == 1 and u == 1:
                                high(1)
                        elif kind == "sum":
                            keep_sums(m, 0)

                step(0, 0, True, False, False)
                step(1, 1, True, True, False)
                with act.Fori(0, PAIRS // 2 - 1) as r:
                    for k in range(2):
                        step(2 * r + 2 + k, k, True, True, True)
                step(PAIRS, 0, False, True, True)
                step(PAIRS + 1, 1, False, False, True)
                part_end(act, PARTS * b + 3)
                for c in range(2):
                    take(18 + c, P, anT[:, c * HALF:(c + 1) * HALF], ACT.Identity)
                act.wait_ge(aff_asked, b + 1)
                act.activation(aff[:, :, 0:ROUTED], logits[:, :, 0:ROUTED], ACT.Exp).then_inc(aff_ready, 1)
                for c in range(2):
                    take(20 + c, 96, gT32[:, c * HALF:(c + 1) * HALF], ACT.Identity)
                act.sem_inc(passed, 1)
                act.sem_inc(passed, 1)
                act.preload_act_table(ACT.Gelu)
                with act.Fori(0, EXPERTS) as e:
                    for c in range(HALVES):
                        k = HALVES * (b * EXPERTS + e) + c
                        act.wait_ge(hid_out, k + 1)
                        act.wait_ge(hg_ready, k + 1)
                        act.sem_inc(passed, 1)
                        act.activation(hid[:, c, :], ps[:, c, :], ACT.Gelu,
                                       bias=cols[:, bass.ds(C_B1 + e, 1)]).then_inc(hid_ready, 1)
                act.wait_ge(down_done, HALVES * EXPERTS * (b + 1) + 2)
                for c in range(2):
                    act.activation(moeT[:, c * HALF:(c + 1) * HALF], ps[:, 4 + c, :], ACT.Identity).then_inc(moe_taken, 1)
                part_end(act, PARTS * b + 4)

        @block.vector
        def _(dve):
            dve.wait_ge(weights_in, ALL_IN)
            su = Steps(dve, v_setup)

            def slink(made):
                su.did(made)
                dve.wait_ge(v_setup, su.n)

            slink(dve.tensor_scalar(ang[:, :], pos[:, :], cols[:, C_THETA:C_THETA + 1], None, ALU.mult))
            for k in range(2):
                slink(dve.tensor_scalar(whole[:, :], ang[:, :], float(1 / (2 * np.pi)), 0.25 * k, ALU.mult, ALU.add))
                slink(dve.tensor_scalar(whole[:, :], whole[:, :], ROUNDER, ROUNDER, ALU.add, ALU.subtract))
                slink(dve.scalar_tensor_tensor(turns[:, k, :], whole[:, :], -TWO_PI_A, ang[:, :], ALU.mult, ALU.add))
                slink(dve.scalar_tensor_tensor(turns[:, k, :], whole[:, :], -TWO_PI_B, turns[:, k, :], ALU.mult, ALU.add))
                slink(dve.scalar_tensor_tensor(turns[:, k, :], whole[:, :], -TWO_PI_C, turns[:, k, :], ALU.mult, ALU.add))
                if k:
                    slink(dve.tensor_scalar(turns[:, k, :], turns[:, k, :], float(np.pi / 2), None, ALU.add))
                slink(dve.tensor_scalar(turns[:, k, :], turns[:, k, :], PI_BELOW, -PI_BELOW, ALU.min, ALU.max))
            assert su.n == V_ANGLES, su.n
            for i in range(2):
                dve.memset(k_low[i][0][HD:HD + 1, :].bitcast(F32), 1.0)
                dve.memset(q_max[i][1][0:HD, :].bitcast(F32), 0.0)
                made = dve.memset(k_low[i][1][0:HD, :].bitcast(F32), 0.0)
            slink(made)
            for i in range(2):
                dve.memset(k_low[i][1][0:1, :].bitcast(F32), 1.0)
            dve.tensor_copy(identr[:, :], ident[:, :])
            dve.tensor_copy(identb[:, :], ident[:, :])
            dve.tensor_copy(masks[:, :, :], masks32[:, :, :])
            dve.tensor_copy(fold[:, :], fold32[:, :])
            dve.tensor_scalar(diag_d[:, :], ident[:, :], cols[:, C_D:C_D + 1], None, ALU.mult)
            dve.wait_ge(a_setup, 1)
            dve.tensor_scalar(neg_a[:, :], exp_a[:, :], -1.0, None, ALU.mult)
            dve.wait_ge(a_setup, 2)
            dve.tensor_scalar(sin_t[:, :], sin_raw[:, :], cols[:, C_SIGN:C_SIGN + 1], None, ALU.mult)
            part_end(dve, 1)
            with dve.Fori(0, BATCH) as b:
                st = Steps(dve, v_step, b * V_STEPS)

                def root(k, made):
                    made.then_inc(ms_ready, 1)
                    dve.wait_ge(rstd_ready, b * RSTDS + k)

                def moments(src, n):
                    for i in range(n):
                        st.did(dve.bn_stats(stats[:, i, :], src(i)))
                    st.wait()
                    dve.sem_inc(passed, 1)
                    for i in range(n):
                        st.did(dve.bn_aggr(mv[:, i, :], stats[:, i, :]))
                    st.wait()

                def mean_squares(k):
                    st.link(dve.tensor_tensor(ms[:, :], mv[:, :, 0], mv[:, :, 0], ALU.mult))
                    root(k, dve.tensor_tensor(ms[:, :], ms[:, :], mv[:, :, 1], ALU.add))

                def normed(dst, src, k, last):
                    for i in range(TILES):
                        made = dve.tensor_scalar(dst[:, i, :], src(i), mv[:, i, 0:1], rstd[:, i:i + 1],
                                                 ALU.subtract, ALU.mult)
                        last(i, made)

                def signal_last(s):
                    return lambda i, made: made.then_inc(s, 1) if i == TILES - 1 else None

                dve.wait_ge(x_in, 16 * b + 16)
                moments(lambda i: xin[:, i, :], TILES)
                root(1, dve.tensor_copy(ms[:, :], mv[:, :, 1]))
                normed(x0, lambda i: xin[:, i, :], 1, signal_last(tok_ready))
                dve.wait_ge(tok_ready, 3 * b + 1)
                for c in range(2):
                    st.did(dve.bn_stats(stats[:, c, :], both(x0[:, TPH * c:TPH * (c + 1), :])))
                st.wait()
                dve.sem_inc(passed, 1)
                st.link(dve.bn_aggr(mv[:, 0, :], stats[:, 0:2, :].rearrange("p a b -> p (a b)")))
                st.link(dve.tensor_copy(partial[:, 0:1], mv[:, 0, 0:1]))
                dve.scalar_tensor_tensor(partial[:, 1:2], mv[:, 0, 0:1], mv[:, 0, 0:1], mv[:, 0, 1:2], ALU.mult, ALU.add
                                         ).then_inc(partial_ready, 1)
                dve.wait_ge(global_sum, b + 1)
                st.link(dve.tensor_copy(glob[:, 0:2], ps[:, 6, 0:2]))
                st.link(dve.tensor_scalar(glob[:, 2:3], glob[:, 0:1], glob[:, 0:1], -1.0, ALU.mult, ALU.mult))
                root(2, dve.tensor_tensor(ms[:, 0:1], glob[:, 1:2], glob[:, 2:3], ALU.add))
                dve.tensor_scalar(nmb[:, 0:1], glob[:, 0:1], rstd[:, 0:1], -1.0, ALU.mult, ALU.mult).then_inc(v_norm, 1)
                dve.wait_ge(a_taken, b * A_OUTS + 6 + 2)
                for c in range(2):
                    st.did(dve.bn_stats(stats[:, c, :], hc[:, c * HALF:(c + 1) * HALF]))
                st.wait()
                dve.sem_inc(passed, 1)
                st.link(dve.bn_aggr(mv[:, 0, :], stats[:, 0:2, :].rearrange("p a b -> p (a b)")))
                root(3, dve.tensor_copy(ms[:, 0:1], mv[:, 0, 1:2]))
                dve.tensor_scalar(nmb[:, 0:1], mv[:, 0, 0:1], rstd[:, 0:1], -1.0, ALU.mult, ALU.mult).then_inc(v_norm, 1)

                def three_parts(dst, src, rest, mid, last):
                    st.link(dve.tensor_copy(dst[0:96, :], src[0:96, :]))
                    st.did(dve.tensor_tensor(dst[32:64, :], src[32:64, :], dst[32:64, :], ALU.subtract))
                    st.link(dve.tensor_tensor(rest[64:96, :], src[64:96, :], dst[64:96, :], ALU.subtract))
                    st.link(dve.tensor_copy(mid[64:96, :], rest[64:96, :]))
                    last(dve.tensor_tensor(dst[64:96, :], rest[64:96, :], mid[64:96, :], ALU.subtract))

                for j in range(2):
                    dve.wait_ge(a_taken, b * A_OUTS + 8 + 2 * j + 2)
                    three_parts(bc3[:, j, :], bc32[:, j, :], bc_rest, bc_mid,
                                (st.link if j == 0 else lambda made: made.then_inc(split_ready, 1)))
                dve.wait_ge(a_step, A_STEPS * b + 5)
                st.link(dve.scalar_tensor_tensor(delta[:, :], z[:, :], 0.0, sp_log[:, :], ALU.max, ALU.add))
                dve.tensor_tensor(du[:, :], delta[:, :], h_act[:, :], ALU.mult).then_inc(delta_ready, 1)
                with dve.Fori(0, STATES // 2) as r:
                    for k in range(2):
                        n = b * STATES + 2 * r + k
                        dve.wait_ge(decay_ready, n + 1)
                        dve.wait_ge(bx_ready, n + 3)
                        dve.wait_ge(cs_ready, n + 1)
                        dve.tensor_tensor_scan(state[:, k, :], decay[:, k, :], bx[:, k, :], 0.0, ALU.mult, ALU.add
                                               ).then_inc(scanned, 1)
                        dve.wait_ge(scanned, n + 3)
                        dve.wait_ge(c_bcast, n + 1)
                        dve.wait_ge(cs_used, n + 1)
                        dve.tensor_tensor(cs[:, k, :], state[:, k, :], banks(4), ALU.mult).then_inc(cs_ready, 1)
                dve.wait_ge(cs_used, STATES * b + STATES + 2)
                dve.tensor_tensor(hc[:, :], banks(6), gate[:, :], ALU.mult).then_inc(yg_ready, 1)
                dve.wait_ge(v_out, V_OUTS * b + 2)
                g_ps = lambda i: ps[:, 2 + i // TPH, (i % TPH) * P:(i % TPH + 1) * P]
                moments(g_ps, TILES)
                root(4, dve.tensor_copy(ms[:, :], mv[:, :, 1]))
                normed(g_tok, g_ps, 4, lambda i, made: made.then_inc(v_taken, 1) if i % TPH == TPH - 1 else None)
                for c in range(2):
                    dve.wait_ge(v_out, V_OUTS * b + 3 + c)
                    dve.wait_ge(p_step, P_STEPS * b + 2)
                    part = both(resid[:, TPH * c:TPH * (c + 1), :])
                    dve.tensor_tensor(part, part, ps[:, 2 + c, :], ALU.add).then_inc(v_taken, 1)
                part_end(dve, PARTS * b + 2)

                moments(lambda i: resid[:, i, :], TILES)
                root(5, dve.tensor_copy(ms[:, :], mv[:, :, 1]))
                normed(xa, lambda i: resid[:, i, :], 5, lambda i, made: st.did(made))
                st.wait()
                moments(lambda i: xa[:, i, :], TILES)
                mean_squares(6)
                for i in range(TILES):
                    made = dve.scalar_tensor_tensor(xa[:, i, :], xa[:, i, :], rstd[:, i:i + 1], gamma1_r, ALU.mult, ALU.mult)
                made.then_inc(tok_ready, 1)

                def invert(m, c, i):
                    if i == 0:
                        dve.wait_ge(misc_taken, sum_at(m, c) + 2)
                        dve.wait_ge(ctx_ready, 2 * m + c + 4)
                    dve.reciprocal(inverse[:, i * PART:(i + 1) * PART], sums[:, i * PART:(i + 1) * PART]
                                   ).then_inc(inverted, 1)
                    if i == INV_PARTS - 1:
                        dve.wait_ge(inverted, INV_PARTS * (2 * m + c + 1) + 1)
                        dve.wait_ge(pv_out, NU * (m + 1) + HALF_END[c])
                        dve.tensor_tensor(ctxT[:, c, :], ps[:, CTX_BANK[c], :], inverse[:, :], ALU.mult
                                          ).then_inc(ctx_ready, 1)

                def add_output(m, c, last):
                    dve.wait_ge(misc_out, op_at(m, c, last) + 1)
                    dve.wait_ge(acc_ready, b + 1)
                    dve.wait_ge(misc_taken, op_at(m, c, last) + 1)
                    part = both(acc[:, TPH * c:TPH * (c + 1), :])
                    dve.tensor_tensor(part, part, ps[:, 7, :], ALU.add).then_inc(misc_taken, 1)

                def low(k, n, par):
                    dve.wait_ge(high_a, 4 * n + 2 * k + 3)
                    dve.wait_ge(high_p, 4 * n + 2 * k + 3)
                    dst = (q_split, k_low)[k][par]
                    high0 = (q_split, k_high)[k][par][0]
                    high1 = (q_max, k_high)[k][par][1]
                    at0 = (HD, 0)[k]
                    dve.tensor_tensor(dst[0][at0:at0 + HD, :], roped[0:HD, k, :], high0[0:HD, :].bitcast(F32),
                                      ALU.subtract).then_inc(low_ready, 1)
                    if k == 0:
                        dve.tensor_tensor(dst[1][HD:P, :], roped[HD:P, k, :], high1[HD:P, :].bitcast(F32),
                                          ALU.subtract).then_inc(low_ready, 1)

                def step(s, par, this, prev, prev2):
                    n = b * PAIRS + s
                    m = n - 1
                    for k in range(8 if this else 0):
                        j, c = divmod(k, HALVES)
                        dve.wait_ge(proj_out, 10 * n + k + 1)
                        if c == 0 and j % 2 == 0:
                            dve.wait_ge(roped_ready, 2 * n + 1)
                        sl = slice(c * HALF, (c + 1) * HALF)
                        dve.scalar_tensor_tensor(
                            turned[:, j, sl], ps[:, c, :], cols[:, bass.ds(C_QK + 4 * s + j, 1)],
                            (cos_t, sin_t)[j % 2][:, sl], ALU.add, ALU.mult).then_inc(proj_taken, 1)
                        if prev2 and k in (3, 5, 7):
                            invert(n - 2, 1, k // 2 - 1)
                    for i in range(INV_PARTS if prev2 and not this else 0):
                        invert(n - 2, 1, i)
                    if prev2 and not prev:
                        add_output(n - 2, 1, True)
                    for c in range(HALVES if this else 0):
                        dve.wait_ge(proj_out, 10 * n + 8 + c + 1)
                        dve.tensor_tensor(
                            vals[par][:, TPH * c:TPH * (c + 1), :, :].rearrange("p i h d -> p i (h d)"),
                            ps[:, c, :].rearrange("p (i n) -> p i n", i=TPH),
                            v_b[:, bass.ds(P * s, P)].unsqueeze(1).broadcast_to((P, TPH, P)), ALU.add
                            ).then_inc(proj_taken, 1)
                    if prev2 and this:
                        invert(n - 2, 1, INV_PARTS - 1)
                    if this:
                        low(0, n, par)
                    for kind, h, u in slots(prev, this):
                        if kind == "mx":
                            i, k0, w = MX[u]
                            dve.wait_ge(scores_out, 2 * NU * n + NU * h + u + 1)
                            dve.tensor_reduce(tops[:, h, u:u + 1], ps[:, 2 + u % 2, 0:w], AX_X, ALU.max
                                              ).then_inc(scores_taken, 1)
                            if u == NU - 1:
                                dve.wait_ge(scores_taken, 2 * NU * n + NU * h + NU + 2)
                                dve.tensor_copy(top_r[:, h, 0:TPH], tops[:, h, 0:TPH])
                                dve.tensor_tensor(top_r[:, h, TPH:TILES], tops[:, h, TPH:NU:2], tops[:, h, TPH + 1:NU:2],
                                                  ALU.max).then_inc(tops_ready, 1)
                        elif kind == "low":
                            low(1, n, par)
                        elif kind == "add":
                            c, j, q0 = ST[u]
                            at = q0 - HALF * c
                            if u == 0:
                                dve.wait_ge(blocks_taken, 2 * NU * m + 1 + 2)
                                dve.wait_ge(misc_taken, row_at(m, 4, not prev2) + 1)
                                dve.tensor_copy(prob_sums[:, 0, 0, 0:P], probs[:, 0, 0, 0:P]).then_inc(v_added, 1)
                            if j == 0:
                                continue
                            dve.wait_ge(blocks_taken, 2 * (NU * m + u) + 1 + 2)
                            dve.wait_ge(v_added, ADDS * (m + 1) + adds_with(u) - 1)
                            total = prob_sums[:, 0, c, at:HALF]
                            before = probs[:, (u - 1) % RING, 0, at:HALF] if j == 1 else total
                            dve.tensor_tensor(total, before, probs[:, u % RING, 0, at:HALF], ALU.add).then_inc(v_added, 1)
                        elif kind == "inv":
                            invert(m, 0, u)
                        elif kind == "op" and (h == 0 or prev2):
                            add_output(m - h, h, False)

                step(0, 0, True, False, False)
                step(1, 1, True, True, False)
                with dve.Fori(0, PAIRS // 2 - 1) as r:
                    for k in range(2):
                        step(2 * r + 2 + k, k, True, True, True)
                step(PAIRS, 0, False, True, True)
                step(PAIRS + 1, 1, False, False, True)
                dve.wait_ge(misc_taken, 8 * PAIRS * (b + 1) + 1)
                part_end(dve, PARTS * b + 3)

                moments(lambda i: acc[:, i, :], TILES)
                mean_squares(7)
                for i in range(TILES):
                    made = dve.scalar_tensor_tensor(an[:, i, :], acc[:, i, :], rstd[:, i:i + 1], gamma2_r, ALU.mult, ALU.mult)
                made.then_inc(tok_ready, 1)
                wide = (P, TILES, ROUTED)
                dve.wait_ge(router_out, b + 1)
                st.link(dve.tensor_tensor(logits[:, :, :], ps[:, 6, 0:TILES * EXPERTS].rearrange("p (i e) -> p i e", i=TILES),
                                          router_b[:, :].unsqueeze(1).broadcast_to((P, TILES, EXPERTS)), ALU.add))
                st.did(dve.memset(aff[:, :, ROUTED:EXPERTS], 0.0))
                st.link(dve.tensor_reduce(red[:, 0, :], logits[:, :, 0:ROUTED], AX_X, ALU.max))
                dve.tensor_tensor(logits[:, :, 0:ROUTED], logits[:, :, 0:ROUTED],
                                  red[:, 0, :].unsqueeze(2).broadcast_to(wide), ALU.subtract).then_inc(aff_asked, 1)
                dve.wait_ge(aff_ready, b + 1)
                st.link(dve.tensor_reduce(red[:, 1, :], aff[:, :, 0:ROUTED], AX_X, ALU.add))
                st.link(dve.reciprocal(red[:, 0, :], red[:, 1, :]))
                st.link(dve.tensor_tensor(aff[:, :, 0:ROUTED], aff[:, :, 0:ROUTED],
                                          red[:, 0, :].unsqueeze(2).broadcast_to(wide), ALU.mult))
                full = (P, TILES, EXPERTS)
                dve.sem_inc(passed, 1)
                for i in range(TILES):
                    st.did(dve.max(big8[:, i, :], aff[:, i, 0:ROUTED]))
                st.wait()
                third = big8[:, :, TOP - 1:TOP].broadcast_to(full)
                st.did(dve.tensor_tensor(above[:, :, :], aff[:, :, :], third, ALU.is_gt))
                st.link(dve.tensor_tensor(equal[:, :, :], aff[:, :, :], third, ALU.is_equal))
                st.did(dve.tensor_reduce(red[:, 1, :], above[:, :, :], AX_X, ALU.add))
                st.link(dve.tensor_tensor_scan(both(struck[:, :, :]), resets[:, :], both(equal[:, :, :]), 0.0,
                                               ALU.mult, ALU.add))
                st.link(dve.tensor_tensor(struck[:, :, :], struck[:, :, :], red[:, 1, :].unsqueeze(2).broadcast_to(full),
                                          ALU.add))
                st.link(dve.scalar_tensor_tensor(both(struck[:, :, :]), both(struck[:, :, :]), TOP + 0.5,
                                                 both(equal[:, :, :]), ALU.is_lt, ALU.mult))
                st.link(dve.tensor_tensor(struck[:, :, :], struck[:, :, :], above[:, :, :], ALU.add))
                st.link(dve.tensor_tensor(struck[:, :, :], struck[:, :, :], aff[:, :, :], ALU.mult))
                st.link(dve.memset(struck[:, :, ROUTED:EXPERTS], 1.0))
                dve.tensor_copy(gates[:, :, :, :], struck[:, :, :].unsqueeze(2).broadcast_to((P, TILES, 3, EXPERTS))
                                ).then_inc(gates_ready, 1)
                dve.wait_ge(a_taken, b * A_OUTS + 22 + 2)
                three_parts(g3[:, :], gT32[:, :], g_rest, g_mid, lambda made: made.then_inc(g3_ready, 1))
                assert st.n == V_STEPS, st.n
                with dve.Fori(0, EXPERTS) as e:
                    for c in range(HALVES):
                        k = HALVES * (b * EXPERTS + e) + c
                        dve.wait_ge(hid_ready, k + 3)
                        dve.wait_ge(gate_out, k + 1)
                        dve.wait_ge(down_done, k + 1)
                        dve.tensor_tensor(hg[:, c, :], hid[:, c, :], ps[:, 2 + c, :], ALU.mult).then_inc(hg_ready, 1)
                for c in range(2):
                    dve.wait_ge(v_out, V_OUTS * b + 5 + c)
                    dve.wait_ge(resid_ready, b + 1)
                    sl = slice(TPH * c, TPH * (c + 1))
                    dve.tensor_tensor(both(y_out[:, sl, :]), both(resid[:, sl, :]), ps[:, 2 + c, :], ALU.add
                                      ).then_inc(v_taken, 1)
                part_end(dve, PARTS * b + 4)

        @block.tensor
        def _(pe):
            part_end(pe, 1)
            with pe.Fori(0, BATCH) as b:
                def a_bank(k):
                    pe.wait_ge(a_taken, b * A_OUTS + k + 1)

                def v_bank(k):
                    pe.wait_ge(v_taken, b * V_OUTS + k + 1)

                def halves(k, n, lhs, rhs, taps=1):
                    for c in range(2):
                        a_bank(k + c)
                        for t in range(taps):
                            made = pe.matmul(ps[0:n, c, :], lhs(t), rhs(c, t), start=(t == 0), stop=(t == taps - 1))
                        made.then_inc(a_out, 1)

                def turn(src, bank, n=P):
                    for i in range(TPH):
                        made = pe.transpose(ps[0:n, bank, i * P:(i + 1) * P], src(i), ident[:, :])
                    return made

                def cut(t, c, shift=0):
                    return t[:, c * HALF + shift:(c + 1) * HALF + shift]

                pe.wait_ge(tok_ready, 3 * b + 1)
                for c in range(2):
                    a_bank(c)
                    turn(lambda i: x0[:, TPH * c + i, :], c).then_inc(a_out, 1)
                pe.wait_ge(partial_ready, b + 1)
                pe.matmul(ps[:, 6, 0:2], mean_of[:, :], partial[:, :], start=True, stop=True).then_inc(global_sum, 1)
                pe.wait_ge(a_taken, b * A_OUTS + 2 + 2)
                halves(2, P, lambda t: w_in[:, :], lambda c, t: cut(xnT_m, c))
                pe.wait_ge(a_taken, b * A_OUTS + 4 + 2)
                halves(4, P, lambda t: w_conv[:, t, :], lambda c, t: cut(hpad, c, t), 3)
                pe.wait_ge(a_step, A_STEPS * b + 2)
                halves(6, 96, lambda t: w_b3[:, :], lambda c, t: cut(h_act, c))
                halves(8, 96, lambda t: w_c3[:, :], lambda c, t: cut(h_act, c))
                halves(10, DT_RANK, lambda t: w_d1[:, :], lambda c, t: cut(h_act, c))
                pe.wait_ge(a_taken, b * A_OUTS + 12 + 2)
                halves(12, P, lambda t: w_d2[:, :], lambda c, t: cut(d1, c))
                for c in range(2):
                    pe.matmul(ps[:, 6 + c, :], diag_d[:, :], cut(h_act, c), start=True, stop=False, skip_group_check=True)
                pe.wait_ge(split_ready, b + 1)
                pe.sem_inc(passed, 1)

                def broadcast_b(i):
                    pe.wait_ge(b_taken, b * STATES + i + 1)
                    for c in range(2):
                        made = pe.matmul(ps[:, 2 + c, :], fold[:, bass.ds(i, 1)].broadcast_to((96, P)),
                                         cut(bc3[:, 0, :], c), start=True, stop=True)
                    made.then_inc(b_bcast, 1)

                def broadcast_c(i):
                    pe.wait_ge(cs_ready, b * STATES + i + 2)
                    for c in range(2):
                        made = pe.matmul(ps[:, 4 + c, :], fold[:, bass.ds(i, 1)].broadcast_to((96, P)),
                                         cut(bc3[:, 1, :], c), start=True, stop=True)
                    made.then_inc(c_bcast, 1)

                def add_state(i, k):
                    pe.wait_ge(cs_ready, b * STATES + i + 3)
                    for c in range(2):
                        made = pe.matmul(ps[:, 6 + c, :], ident[:, :], cut(cs[:, k, :], c), start=False, stop=False,
                                         skip_group_check=True)
                    made.then_inc(cs_used, 1)

                broadcast_b(0)
                broadcast_b(1)
                broadcast_c(0)
                with pe.Fori(0, STATES // 2 - 1) as r:
                    for k in range(2):
                        broadcast_b(2 * r + k + 2)
                        broadcast_c(2 * r + k + 1)
                        add_state(2 * r + k, k)
                broadcast_c(STATES - 1)
                add_state(STATES - 2, 0)
                add_state(STATES - 1, 1)
                pe.wait_ge(yg_ready, b + 1)
                for c in range(2):
                    v_bank(c)
                    turn(lambda i: hc[:, (TPH * c + i) * P:(TPH * c + i + 1) * P], 2 + c).then_inc(v_out, 1)
                for c in range(2):
                    pe.wait_ge(v_taken, b * V_OUTS + c + 1 + 2)
                    a_bank(14 + c)
                    turn(lambda i: g_tok[:, TPH * c + i, :], c).then_inc(a_out, 1)
                for c in range(2):
                    pe.wait_ge(a_taken, b * A_OUTS + 14 + c + 1 + 2)
                    v_bank(2 + c)
                    for i in range(TPH):
                        made = pe.matmul(ps[:, 2 + c, i * P:(i + 1) * P], gT[:, (TPH * c + i) * P:(TPH * c + i + 1) * P],
                                         w_out[:, :], start=True, stop=True)
                    made.then_inc(v_out, 1)
                part_end(pe, PARTS * b + 2)

                pe.wait_ge(tok_ready, 3 * b + 2)
                for c in range(2):
                    a_bank(16 + c)
                    turn(lambda i: xa[:, TPH * c + i, :], c).then_inc(a_out, 1)
                pe.wait_ge(a_taken, b * A_OUTS + 18 + 2)

                def max_row(m, h, c, first):
                    if c == 0:
                        pe.wait_ge(tops_ready, 2 * m + h + 1)
                    pe.wait_ge(misc_taken, row_at(m, 2 * h + c, first) + 1)
                    for i in range(TPH):
                        at = TPH * c + i
                        made = pe.matmul(ps[:, 7, i * P:(i + 1) * P], top_r[:, h, at:at + 1].broadcast_to((P, P)),
                                         identr[:, :], start=True, stop=True)
                    made.then_inc(misc_out, 1)

                def prob_sum(m, c):
                    done = ADDS * (m + 1) + adds_with(HALF_END[c] - 1)
                    pe.wait_ge(v_added, done)
                    pe.wait_ge(p_added, done)
                    pe.wait_ge(misc_taken, sum_at(m, c) + 1)
                    for h in range(2):
                        made = pe.matmul(ps[HD * h:HD * (h + 1), 7, :], ones[:, :], prob_sums[:, h, c, :],
                                         start=True, stop=True)
                    made.then_inc(misc_out, 1)

                def output(m, pair, c, last):
                    pe.wait_ge(ctx_ready, 2 * m + 4 + c + 1)
                    pe.wait_ge(misc_taken, op_at(m, c, last) + 1)
                    for i in range(TPH):
                        made = pe.matmul(ps[:, 7, i * P:(i + 1) * P], ctxT[:, c, i * P:(i + 1) * P],
                                         o_w[:, bass.ds(pair, 1), :].rearrange("p o n -> p (o n)"), start=True, stop=True)
                    made.then_inc(misc_out, 1)

                def step(s, turn_of, par, this, prev, prev2):
                    n = b * PAIRS + s
                    m = n - 1
                    if this:
                        pe.wait_ge(w_pair_in[par], 16 * (b * (PAIRS // 2) + turn_of + 1))
                    for k in range(8):
                        j, c = divmod(k, HALVES)
                        if this:
                            pe.wait_ge(proj_taken, 10 * n + k + 1)
                            if k == 0:
                                pe.wait_ge(ctx_ready, 2 * n + 1)
                            pe.matmul(ps[:, c, :], w_pair[par][:, j, :], cut(xnT, c), start=True, stop=True
                                      ).then_inc(proj_out, 1)
                        if prev2 and k == 1:
                            prob_sum(n - 2, 1)
                        if prev and k >= 4:
                            max_row(m, (k - 4) // 2, k % 2, not prev2)
                    if prev2 and not prev:
                        output(n - 2, s - 2, 1, True)
                    if this:
                        for c in range(HALVES):
                            pe.wait_ge(proj_taken, 10 * n + 8 + c + 1)
                            for i in range(TPH):
                                at = TPH * c + i
                                made = pe.matmul(ps[:, c, i * P:(i + 1) * P], xnT[:, at * P:(at + 1) * P],
                                                 v_w[:, bass.ds(P * s, P)], start=True, stop=True)
                            made.then_inc(proj_out, 1)
                    for kind, h, u in slots(prev, this):
                        if kind == "st":
                            c, j, q0 = ST[u]
                            w = HALF * (c + 1) - q0
                            if u == 0:
                                pe.wait_ge(misc_taken, row_at(m, 4, not prev2) + 1)
                                pe.wait_ge(low_ready, 3 * m + 4)
                                pe.wait_ge(low_p, m + 1)
                            pe.wait_ge(blocks_taken, 2 * (NU * m + u) + h + 1)
                            o = ps[:, 4 + h, 0:w]
                            own = q0 == P * j
                            rows_k = slice(0, HD + 1) if h == 0 else slice(0, P)
                            pe.matmul(o, k_high[1 - par][h][:, j * P:(j + 1) * P], q_split[1 - par][h][:, q0:q0 + w],
                                      start=True, stop=False)
                            made = pe.matmul(o, k_low[1 - par][h][rows_k, j * P:(j + 1) * P],
                                             q_max[1 - par][h][rows_k, q0:q0 + w], start=False, stop=not own)
                            if own:
                                made = pe.matmul(o[:, 0:P], identb[:, :], masks[:, 1, :], start=False, stop=True)
                            made.then_inc(blocks_out, 1)
                        elif kind == "pv":
                            c, j, q0 = ST[u]
                            at = q0 - HALF * c
                            if u == 0:
                                pe.wait_ge(proj_taken, 10 * n + (9 if this else 0) + 2)
                            if u == HALF_START[1]:
                                pe.wait_ge(ctx_ready, 2 * m + 4)
                            pe.wait_ge(blocks_taken, 2 * (NU * m + u + 1) + 2)
                            for g in range(2):
                                made = pe.matmul(ps[HD * g:HD * (g + 1), CTX_BANK[c], at:HALF], vals[1 - par][:, j, g, :],
                                                 probs[:, u % RING, g, at:HALF], start=(j == 0),
                                                 stop=(u == HALF_END[c] - 1), skip_group_check=True)
                            made.then_inc(pv_out, 1)
                        elif kind == "mx":
                            i, k0, w = MX[u]
                            if u == 0:
                                pe.wait_ge(high_a, 4 * n + 5)
                                pe.wait_ge(high_p, 4 * n + 5)
                                pe.wait_ge(low_ready, 3 * n + 3)
                            pe.wait_ge(scores_taken, 2 * NU * n + NU * h + u + 1)
                            o = ps[:, 2 + u % 2, 0:w]
                            own = k0 + w == P * (i + 1)
                            made = pe.matmul(o, q_split[par][h][:, i * P:(i + 1) * P], k_high[par][h][:, k0:k0 + w],
                                             start=True, stop=not own)
                            if own:
                                made = pe.matmul(o[:, w - P:w], identb[:, :], masks[:, 0, :], start=False, stop=True)
                            made.then_inc(scores_out, 1)
                        elif kind == "sum":
                            prob_sum(m, 0)
                        elif kind == "op" and (h == 0 or prev2):
                            output(m - h, s - 1 - h, h, False)

                step(0, 0, 0, True, False, False)
                step(1, 0, 1, True, True, False)
                with pe.Fori(0, PAIRS // 2 - 1) as r:
                    for k in range(2):
                        step(2 * r + 2 + k, r + 1, k, True, True, True)
                step(PAIRS, 0, 0, False, True, True)
                step(PAIRS + 1, 0, 1, False, False, True)
                part_end(pe, PARTS * b + 3)

                pe.wait_ge(tok_ready, 3 * b + 3)
                for c in range(2):
                    a_bank(18 + c)
                    turn(lambda i: an[:, TPH * c + i, :], c).then_inc(a_out, 1)
                pe.wait_ge(a_taken, b * A_OUTS + 20 + 2)
                for i in range(TILES):
                    made = pe.matmul(ps[:, 6, i * EXPERTS:(i + 1) * EXPERTS], anT[:, i * P:(i + 1) * P], w_router[:, :],
                                     start=True, stop=True)
                made.then_inc(router_out, 1)
                pe.wait_ge(gates_ready, b + 1)
                for c in range(2):
                    a_bank(20 + c)
                    turn(lambda i: gates[:, TPH * c + i, :, :].rearrange("p a e -> p (a e)"), c, 96).then_inc(a_out, 1)
                pe.wait_ge(a_taken, b * A_OUTS + 22 + 2)
                for c in range(2):
                    pe.matmul(ps[:, 4 + c, :], b2_all[:, :], gT32[0:EXPERTS, c * HALF:(c + 1) * HALF], start=True,
                              stop=False, skip_group_check=True)
                pe.wait_ge(g3_ready, b + 1)

                def up(e, turn_of, slot, c):
                    k = HALVES * (b * EXPERTS + e) + c
                    if c == 0:
                        pe.wait_ge(w12_in[slot], 16 * (b * (EXPERTS // SLOTS) + turn_of + 1))
                    pe.wait_ge(hid_ready, k + 1)
                    pe.matmul(ps[:, c, :], w12[slot][:, 0, :], cut(anT, c), start=True, stop=True).then_inc(hid_out, 1)
                    pe.wait_ge(hg_ready, k + 1)
                    pe.matmul(ps[:, 2 + c, :], fold[:, bass.ds(e, 1)].broadcast_to((96, P)), cut(g3, c), start=True,
                              stop=True).then_inc(gate_out, 1)

                def down(e, slot, c):
                    k = HALVES * (b * EXPERTS + e) + c
                    pe.wait_ge(hg_ready, k + 3)
                    pe.matmul(ps[:, 4 + c, :], w12[slot][:, 1, :], hg[:, c, :], start=False, stop=False,
                              skip_group_check=True).then_inc(down_done, 1)

                for c in range(2):
                    up(0, 0, 0, c)
                with pe.Fori(0, EXPERTS // SLOTS - 1) as r:
                    for i in range(SLOTS):
                        for c in range(2):
                            down(SLOTS * r + i, i, c)
                            up(SLOTS * r + i + 1, r + (i + 1) // SLOTS, (i + 1) % SLOTS, c)
                for i in range(SLOTS):
                    for c in range(2):
                        down(EXPERTS - SLOTS + i, i, c)
                        if i < SLOTS - 1:
                            up(EXPERTS - SLOTS + i + 1, EXPERTS // SLOTS - 1, i + 1, c)
                for c in range(2):
                    pe.wait_ge(moe_taken, 2 * b + c + 1)
                    v_bank(4 + c)
                    turn(lambda i: moeT[:, (TPH * c + i) * P:(TPH * c + i + 1) * P], 2 + c).then_inc(v_out, 1)
                part_end(pe, PARTS * b + 4)


def constants():
    eye = np.eye(P, dtype=np.float32)
    q, k = np.arange(P)[:, None], np.arange(P)[None, :]
    masks = np.stack([np.where(k > q, MASKED, 0.0), np.where(k < q, MASKED, 0.0)], 1).astype(np.float32)
    fold = (np.arange(96)[:, None] % 32 == np.arange(32)[None, :]).astype(np.float32)
    resets = (np.arange(TILES * EXPERTS) % EXPERTS != 0).astype(np.float32)[None]
    return dict(c_ident=eye, c_masks=masks, c_fold=fold, c_pos=np.arange(SEQ, dtype=np.float32)[None], c_resets=resets)


def kernel(**inputs):
    import concourse.bacc as bacc
    from concourse.bass_utils import run_bass_kernel_spmd

    x = {k: np.asarray(v) for k, v in inputs.items()}
    m = {k[len("L0_attn_"):]: v for k, v in x.items() if k.startswith("L0_attn_")}
    f = {k[len("L0_ffn_"):]: v for k, v in x.items() if k.startswith("L0_ffn_")}
    f32 = np.float32

    def thrice(w):
        out = np.zeros((w.shape[0], 96), f32)
        for i in range(3):
            out[:, 32 * i:32 * i + w.shape[1]] = w
        return out

    cols = np.zeros((P, NCOLS), f32)
    cols[:, C_B_IN], cols[:, C_CONV_B], cols[:, C_B_D2], cols[:, C_D] = m["b_in"], m["conv_b"], m["b_d2"], m["D"]
    cols[:96, C_B_B], cols[:96, C_B_C] = thrice(m["b_B"][None])[0], thrice(m["b_C"][None])[0]
    cols[:DT_RANK, C_B_D1] = m["b_d1"]
    cols[:, C_THETA] = np.tile(f["theta"], P // f["theta"].shape[0])
    cols[:, C_SIGN] = np.where(np.arange(P) % HD < HD // 2, -1.0, 1.0)
    cols[:, C_ALOG:C_ALOG + STATES] = m["A_log"]
    cols[:, C_B1:C_B1 + ROUTED], cols[:, C_B1 + ROUTED] = f["re_b1"].T, f["sh_b1"]
    order = np.concatenate([np.arange(0, HD, 2), np.arange(1, HD, 2)])
    swapped = np.concatenate([np.arange(1, HD, 2), np.arange(0, HD, 2)])
    pick = [np.concatenate([HD * h + o for h in range(HEADS)]) for o in (order, swapped)]
    w_pairs = np.zeros((PAIRS, P, 4, P), f32)
    for j, name in enumerate("qk"):
        for i in range(2):
            w = f[name + "_w"][:, pick[i]].reshape(DM, PAIRS, P)
            w_pairs[:, :, 2 * j + i, :] = w.transpose(1, 0, 2)
            cols[:, C_QK + 2 * j + i::4] = f[name + "_b"][pick[i]].reshape(PAIRS, P).T
    rows = np.stack([m["b_out"], f["gamma1"], f["gamma2"], f["o_b"]])
    w12 = np.zeros((EXPERTS, P, 2, P), f32)
    w12[:ROUTED, :, 0], w12[ROUTED, :, 0] = f["re_w1"], f["sh_w1"]
    w12[:ROUTED, :, 1], w12[ROUTED, :, 1] = f["re_w2"], f["sh_w2"]
    router_w = np.zeros((DM, EXPERTS), f32)
    router_w[:, :ROUTED] = f["router_w"]
    router_b = np.zeros((1, EXPERTS), f32)
    router_b[0, :ROUTED] = f["router_b"]
    arrays = dict(
        x=m["x"], w_in=m["w_in"].T, conv_w=m["conv_w"].transpose(1, 2, 0), w_b3=thrice(m["w_B"].T),
        w_c3=thrice(m["w_C"].T), w_d1=m["w_d1"].T, w_d2=m["w_d2"].T, w_out=m["w_out"].T, cols=cols, rows=rows,
        w_pairs=w_pairs, v_w=f["v_w"], v_b=f["v_b"][None], o_w=f["o_w"].reshape(PAIRS, P, DM).transpose(1, 0, 2),
        w12=w12, b2=np.concatenate([f["re_b2"], f["sh_b2"][None]]), router_w=router_w, router_b=router_b,
        **constants())
    nc = bacc.Bacc("TRN2", target_bir_lowering=False, num_devices=1)
    arrays = {"in_" + k: np.ascontiguousarray(v) for k, v in arrays.items()}
    ins = {k[3:]: nc.dram_tensor(k, v.shape, mybir.dt.from_np(v.dtype), kind="ExternalInput").ap()
           for k, v in arrays.items()}
    out = nc.dram_tensor("out_0", (BATCH, SEQ, DM), F32, kind="ExternalOutput").ap()
    program(nc, ins, out)
    r = run_bass_kernel_spmd(nc, [arrays], core_ids=[0])
    return r.results[0]["out_0"]
```

```python
from contextlib import ExitStack

import numpy as np

import concourse.bass as bass
from concourse import mybir

ALU = mybir.AluOpType
ACT = mybir.ActivationFunctionType
AX_X = mybir.AxisListType.X
F32 = mybir.dt.float32
F32R = mybir.dt.float32r
BF16 = mybir.dt.bfloat16

P = 128
BATCH, SEQ, DM = 4, 1024, 128
TILES = SEQ // P
HALF = 512
HALVES = SEQ // HALF
TPH = HALF // P
STATES = 16
DT_RANK = 8
HEADS, HD = 16, 64
PAIRS = HEADS // 2
EXPERTS = 32
ROUTED = 31
TOP = 3
SLOTS = 4
SPLITS = PAIRS + 1
UNITS = EXPERTS * HALVES
HG_BUFS = 4
DOWN_LAG = 3
EPS = 1e-5
SCALE = HD ** -0.5
MASKED = -1e30
ENGINES = 5

C_B_IN, C_CONV_B, C_B_D1, C_B_D2, C_D, C_THETA, C_SIGN = range(7)
C_ALOG = 7
C_B1 = C_ALOG + STATES
C_QK = C_B1 + EXPERTS
NCOLS = C_QK + 4 * PAIRS

TWO_PI_A = 6.28125
TWO_PI_B = float(np.float32(np.round((2 * np.pi - TWO_PI_A) * 2.0 ** 17) / 2.0 ** 17))
TWO_PI_C = float(np.float32(2 * np.pi - TWO_PI_A - TWO_PI_B))
ROUNDER = float(1.5 * 2 ** 23)
PI_BELOW = 3.1415925


def st_units():
    return [(c, j, max(P * j, HALF * c)) for c in range(HALVES) for j in range(TPH * (c + 1))]


def max_units():
    out = []
    for i in range(TILES):
        end = P * (i + 1)
        out.append((i, 0, min(end, HALF)))
        if end > HALF:
            out.append((i, HALF, end - HALF))
    return out


ST = st_units()
MX = max_units()
NU = len(ST)


RING = 4
PV_LAG = 2
HALF_START = (0, TPH)
HALF_END = (TPH, NU)


def adds_with(u):
    c, j, _ = ST[u]
    return (1, TPH)[c] + max(j, 1)


ADDS = adds_with(NU - 1)


def slots(do_prev, do_this):
    mx = [("mx", h, u) for h in range(2) for u in range(NU)]
    out = []
    for u in range(NU + PV_LAG):
        def rows():
            return [mx.pop(0)] if do_this and u >= MX_FROM and mx else []

        if do_prev and u < NU:
            out.append(("st", 0, u))
            out += rows()
            out.append(("st", 1, u))
        out += rows()
        if do_prev and u >= PV_LAG:
            out.append(("pv", 0, u - PV_LAG))
        out += rows()
        if do_prev and 1 <= u <= NU:
            out.append(("add", 0, u - 1))
            if not do_this and u - 1 in NORM_AFTER:
                out.append(("input", 0, NORM_AFTER.index(u - 1)))
        if do_this and u == MX_FROM - 1:
            out.append(("low", 0, 0))
        if do_prev:
            out += [(kind, c, i) for kind, c, i, at in LATE if at == u]
    return out + (mx if do_this else [])


NORM_AFTER = (1, 3, 5, 7, 9)
MX_FROM = 4
QUARTER = P // 4
SUMS = HALF // 2
INV_PARTS = 2
PART = SUMS // INV_PARTS
SUM_AFTER = 1
INV_AFTER = (1, 2)
ROWS_AFTER = (4, 6)
LATE = [("spread", 1, 0, 1), ("scale", 1, 0, 2), ("op", 1, 0, 4), ("sum", 0, 0, 6), ("inv", 0, 0, 7), ("inv", 0, 1, 8)]
LATE += [("spread", 0, 0, 9), ("scale", 0, 0, 10), ("op", 0, 0, 11)]


def row_at(m, k, first):
    return 6 * m + k - (0 if first else 1)


def sum_at(m, c):
    return 6 * m + 2 + 2 * c


def op_at(m, c, last):
    return 6 * m + (3 if c == 0 else 5 if last else 7)


def program(nc, ins, out):
    with ExitStack() as ctx:
        def sb(name, shape, dt=F32, where=None):
            return (where or ctx).enter_context(nc.sbuf_tensor(name, shape, dt))

        def sem(name):
            return ctx.enter_context(nc.semaphore(name))

        ident = sb("ident", [P, P])
        identb = sb("identb", [P, P], BF16)
        masks = sb("masks", [P, 2, P], BF16)
        fold32 = sb("fold32", [96, 32])
        fold = sb("fold", [96, 32], BF16)
        mean_of = sb("mean_of", [P, P])
        diag_d = sb("diag_d", [P, P])
        neg_a = sb("neg_a", [P, STATES])
        exp_a = sb("exp_a", [P, STATES])
        neg_half = sb("neg_half", [P, TILES])
        cols = sb("cols", [P, NCOLS])
        cos_t = sb("cos_t", [P, SEQ])
        sin_t = sb("sin_t", [P, SEQ])
        w_in = sb("w_in", [P, P])
        w_conv = sb("w_conv", [P, 3, P])
        w_bc = sb("w_bc", [P, 2 * STATES])
        b_bc = sb("b_bc", [P, 2 * STATES])
        w_d1 = sb("w_d1", [P, DT_RANK])
        w_d2 = sb("w_d2", [DT_RANK, P])
        w_out = sb("w_out", [P, P])
        w_router = sb("w_router", [P, EXPERTS])
        b2_all = sb("b2_all", [96, P])
        rows = sb("rows", [P, 4, P])
        router_b = sb("router_b", [P, EXPERTS])
        v_b = sb("v_b", [P, HEADS * HD])
        v_w = sb("v_w", [P, HEADS * HD])
        o_w = sb("o_w", [P, PAIRS, P])
        resets = sb("resets", [P, TILES * EXPERTS])
        b_out_r, gamma1_r, gamma2_r, o_b_r = (rows[:, i, :] for i in range(4))

        xin = sb("xin", [P, TILES, P])
        resid = sb("resid", [P, TILES, P])
        partial = sb("partial", [P, 2])
        glob = sb("glob", [P, 3])
        stats = sb("stats", [P, TILES, 6])
        mv = sb("mv", [P, TILES, 2])
        ms = sb("ms", [P, TILES])
        rstd = sb("rstd", [P, TILES])
        x0 = sb("x0", [P, TILES, P])
        xa = x0
        xnT_m = sb("xnT_m", [P, SEQ])
        hpad = sb("hpad", [P, SEQ + 2])
        x_scale = sb("x_scale", [P, 1])
        x_shift = sb("x_shift", [P, 1])
        nmb = sb("nmb", [P, TILES])

        acc = sb("acc", [P, TILES, P], F32)
        vals = [sb(f"vals{i}", [P, TILES, 2, HD], F32) for i in range(2)]
        ones = sb("ones", [P, QUARTER])
        pick_quarter = sb("pick_quarter", [P, 4, HD])
        q_max = [[sb(f"q_max{i}{h}", [P, SEQ], F32R) for h in range(2)] for i in range(2)]
        k_low = [[sb(f"k_low{i}{h}", [P, SEQ], F32R) for h in range(2)] for i in range(2)]

        m_ctx = ExitStack()
        gate = sb("gate", [P, SEQ], F32, m_ctx)
        hc = sb("hc", [P, SEQ], F32, m_ctx)
        h_act = sb("h_act", [P, SEQ], F32, m_ctx)
        bc_tok = sb("bc_tok", [P, TILES, 2 * STATES], F32, m_ctx)
        bc_high = sb("bc_high", [P, TILES, 2 * STATES], BF16, m_ctx)
        bc_rest = sb("bc_rest", [P, TILES, 2 * STATES], F32, m_ctx)
        bc_mid = sb("bc_mid", [P, TILES, 2 * STATES], BF16, m_ctx)
        bc_parts = sb("bc_parts", [P, TILES, 3, 2 * STATES], F32, m_ctx)
        bc3 = sb("bc3", [96, SEQ], BF16, m_ctx)
        d1 = sb("d1", [DT_RANK, SEQ], F32, m_ctx)
        z_abs = sb("z_abs", [P, SEQ], F32, m_ctx)
        z = sb("z", [P, SEQ], F32, m_ctx)
        sp_log = sb("sp_log", [P, SEQ], F32, m_ctx)
        delta = sb("delta", [P, SEQ], F32, m_ctx)
        du = sb("du", [P, SEQ], F32, m_ctx)
        decay = sb("decay", [P, 2, SEQ], F32, m_ctx)
        b_rows = sb("b_rows", [P, 2, SEQ], F32, m_ctx)
        bx = sb("bx", [P, 2, SEQ], F32, m_ctx)
        state = sb("state", [P, 2, SEQ], F32, m_ctx)
        cs = sb("cs", [P, 2, SEQ], F32, m_ctx)
        g_tok = sb("g_tok", [P, TILES, P], F32, m_ctx)
        gT = sb("gT", [P, SEQ], F32, m_ctx)
        m_ctx.close()

        a_ctx = ExitStack()
        xnT = sb("xnT", [P, SEQ], F32, a_ctx)
        xn_high = sb("xn_high", [P, SEQ], F32R, a_ctx)
        xn_low = sb("xn_low", [P, SEQ], F32R, a_ctx)
        w_pair_high = [sb(f"w_pair_high{i}", [P, 4, P], F32R, a_ctx) for i in range(2)]
        w_pair_low = [sb(f"w_pair_low{i}", [P, 4, P], F32R, a_ctx) for i in range(2)]
        w_pair = [sb(f"w_pair{i}", [P, 4, P], F32, a_ctx) for i in range(2)]
        turned = sb("turned", [P, 4, SEQ], F32, a_ctx)
        roped = sb("roped", [P, 2, SEQ], F32, a_ctx)
        q_split = [[sb(f"q_split{i}{h}", [P, SEQ], F32R, a_ctx) for h in range(2)] for i in range(2)]
        k_high = [[sb(f"k_high{i}{h}", [P, SEQ], F32R, a_ctx) for h in range(2)] for i in range(2)]
        probs = sb("probs", [P, RING, 2, HALF], F32, a_ctx)
        prob_sums = sb("prob_sums", [P, 2, HALVES, HALF], F32, a_ctx)
        tops = sb("tops", [P, 2, NU], F32, a_ctx)
        top = sb("top", [P, 2, TILES], F32, a_ctx)
        inverse = sb("inverse", [P, SUMS], F32, a_ctx)
        factors = sb("factors", [P, HALF], F32, a_ctx)
        ctxT = sb("ctxT", [P, HALVES, HALF], F32, a_ctx)
        a_ctx.close()

        e_ctx = ExitStack()
        an = sb("an", [P, TILES, P], F32, e_ctx)
        anT = sb("anT", [P, SEQ], F32, e_ctx)
        logits = sb("logits", [P, TILES, EXPERTS], F32, e_ctx)
        aff = sb("aff", [P, TILES, EXPERTS], F32, e_ctx)
        big8 = sb("big8", [P, TILES, 8], F32, e_ctx)
        above = sb("above", [P, TILES, EXPERTS], F32, e_ctx)
        equal = sb("equal", [P, TILES, EXPERTS], F32, e_ctx)
        struck = sb("struck", [P, TILES, EXPERTS], F32, e_ctx)
        gates = sb("gates", [P, TILES, 3, EXPERTS], F32, e_ctx)
        red = sb("red", [P, 2, TILES], F32, e_ctx)
        gT32 = sb("gT32", [96, SEQ], F32, e_ctx)
        g_high = sb("g_high", [P, TILES, EXPERTS], BF16, e_ctx)
        g_rest = sb("g_rest", [P, TILES, EXPERTS], F32, e_ctx)
        g_mid = sb("g_mid", [P, TILES, EXPERTS], BF16, e_ctx)
        g3 = sb("g3", [96, SEQ], BF16, e_ctx)
        w12 = [sb(f"w12_{i}", [P, 2, P], F32, e_ctx) for i in range(SLOTS)]
        w12_high = [sb(f"w12_high{i}", [P, 2, P], F32R, e_ctx) for i in range(SLOTS)]
        w12_low = [sb(f"w12_low{i}", [P, 2, P], F32R, e_ctx) for i in range(SLOTS)]
        an_high = sb("an_high", [P, SEQ], F32R, e_ctx)
        an_low = sb("an_low", [P, SEQ], F32R, e_ctx)
        hid = sb("hid", [P, 2, HALF], F32, e_ctx)
        hg = sb("hg", [P, HG_BUFS, HALF], F32, e_ctx)
        hg_high = sb("hg_high", [P, HG_BUFS, HALF], F32R, e_ctx)
        hg_low = sb("hg_low", [P, HG_BUFS, HALF], F32R, e_ctx)
        moeT = sb("moeT", [P, SEQ], F32, e_ctx)
        e_ctx.close()

        s_ctx = ExitStack()
        pos = sb("pos", [P, SEQ], F32, s_ctx)
        masks32 = sb("masks32", [P, 2, P], F32, s_ctx)
        ang = sb("ang", [P, SEQ], F32, s_ctx)
        turns = sb("turns", [P, 2, SEQ], F32, s_ctx)
        whole = sb("whole", [P, SEQ], F32, s_ctx)
        sin_raw = sb("sin_raw", [P, SEQ], F32, s_ctx)
        s_ctx.close()

        ps = ctx.enter_context(nc.psum_tensor("ps", [P, 8, HALF], F32))

        def banks(a, n=2):
            return ps[:, a:a + n, :].rearrange("p a n -> p (a n)")

        PROJ_BANKS = 4
        MX_BANK = (2, 3, 1)
        passed, part_done, weights_in = sem("passed"), sem("part_done"), sem("weights_in")
        p_setup, v_setup, a_setup = sem("p_setup"), sem("v_setup"), sem("a_setup")
        first_in = sem("first_in")
        x_in = sem("x_in")
        v_step = sem("v_step")
        p_step = sem("p_step")
        a_step = sem("a_step")
        ms_ready, ms_plus, rstd_ready = sem("ms_ready"), sem("ms_plus"), sem("rstd_ready")
        partial_ready, global_sum = sem("partial_ready"), sem("global_sum")
        a_out, a_taken = sem("a_out"), sem("a_taken")
        v_out, v_taken = sem("v_out"), sem("v_taken")
        tok_ready, v_norm, yg_ready = sem("tok_ready"), sem("v_norm"), sem("yg_ready")
        bc_out, bc_ready, delta_ready = sem("bc_out"), sem("bc_ready"), sem("delta_ready")
        b_bcast, b_taken, c_bcast = sem("b_bcast"), sem("b_taken"), sem("c_bcast")
        decay_ready, bx_ready, scanned, cs_ready, cs_used = (
            sem("decay_ready"), sem("bx_ready"), sem("scanned"), sem("cs_ready"), sem("cs_used"))
        w_pair_in = [sem(f"w_pair_in{i}") for i in range(2)]
        xn_high_ready, xn_split = sem("xn_high_ready"), sem("xn_split")
        w_pair_high_ready, w_pair_split = sem("w_pair_high_ready"), sem("w_pair_split")
        proj_out, proj_taken = sem("proj_out"), sem("proj_taken")
        roped_ready, high_a, high_p, low_ready = sem("roped_ready"), sem("high_a"), sem("high_p"), sem("low_ready")
        scores_out, scores_taken = sem("scores_out"), sem("scores_taken")
        blocks_out, blocks_taken = sem("blocks_out"), sem("blocks_taken")
        tops_ready, misc_out, misc_taken = sem("tops_ready"), sem("misc_out"), sem("misc_taken")
        pv_out, v_added, p_added, ctx_ready = sem("pv_out"), sem("v_added"), sem("p_added"), sem("ctx_ready")
        acc_ready, resid_ready = sem("acc_ready"), sem("resid_ready")
        w12_in = [sem(f"w12_in{i}") for i in range(SLOTS)]
        router_out, aff_asked, aff_ready = sem("router_out"), sem("aff_asked"), sem("aff_ready")
        hid_out, hid_ready, gate_out, hg_ready, down_done = (
            sem("hid_out"), sem("hid_ready"), sem("gate_out"), sem("hg_ready"), sem("down_done"))
        an_split, hg_high_ready, hg_low_ready = sem("an_split"), sem("hg_high_ready"), sem("hg_low_ready")
        w12_high_ready, w12_split = sem("w12_high_ready"), sem("w12_split")
        inverted, spread, factors_ready = sem("inverted"), sem("spread"), sem("factors_ready")
        low_p = sem("low_p")
        gates_ready, g3_ready = sem("gates_ready"), sem("g3_ready")
        moe_taken, y_stored = sem("moe_taken"), sem("y_stored")

        DOWN_FREE = HALVES * SLOTS
        CREDITS = [(proj_out, 2 * 10), (y_stored, 16), (a_taken, 2), (v_taken, 2), (scanned, 2), (bx_ready, 2),
                   (cs_used, 2), (b_taken, 1), (cs_ready, 2),
                   (proj_taken, PROJ_BANKS), (scores_taken, 3), (blocks_taken, 2), (pv_out, NU), (v_added, ADDS), (p_added, ADDS),
                   (ctx_ready, 4),
                   (high_a, 1), (high_p, 1), (low_ready, 1), (roped_ready, 1), (inverted, 1), (misc_taken, 1),
                   (hid_ready, 2), (hg_ready, 2), (hg_low_ready, HG_BUFS), (down_done, DOWN_FREE)]

        block = ctx.enter_context(nc.Block())

        class Steps:

            def __init__(self, eng, s, base=0):
                self.eng, self.s, self.base, self.n = eng, s, base, 0

            def did(self, made):
                made.then_inc(self.s, 1)
                self.n += 1

            def wait(self):
                self.eng.wait_ge(self.s, self.base + self.n)

            def link(self, made):
                self.did(made)
                self.wait()

        PARTS, V_ANGLES, V_FIRST, V_STEPS, V_OUTS, A_OUTS, A_STEPS = 3, 14, 23, 118, 6, 20, 7

        CTX_BANK = (0, 6)
        ROW_AT = (HD, 0)
        GATE_BANK = 6

        def part_end(eng, k):
            eng.sem_inc(passed, 1)
            eng.drain().then_inc(part_done, 1)
            eng.wait_ge(part_done, ENGINES * k)
            eng.sem_inc(passed, 1)

        R_CONV, R_GATED, R_BOTH, R_NEXT, R_NEXT_ALL, R_OUT = range(6)
        RSTDS = 6

        def root_at(b, k):
            return 2 + b * RSTDS + k + 1

        def both(t):
            return t.rearrange("p i d -> p (i d)")

        loads = [(ident[:, :], ins["c_ident"]), (masks32[:, :, :], ins["c_masks"]), (fold32[:, :], ins["c_fold"]),
                 (pick_quarter[:, :, :], ins["c_quarters"]),
                 (resets[:, :], ins["c_resets"].broadcast_to((P, TILES * EXPERTS))),
                 (w_in[:, :], ins["w_in"]), (w_conv[:, :, :], ins["conv_w"]), (w_bc[:, :], ins["w_bc"]),
                 (b_bc[:, :], ins["b_bc"].broadcast_to((P, 2 * STATES))), (w_d1[:, :], ins["w_d1"]), (w_d2[:, :], ins["w_d2"]),
                 (w_out[:, :], ins["w_out"]), (w_router[:, :], ins["router_w"]), (b2_all[:, :], ins["b2"]),
                 (v_w[:, :], ins["v_w"]), (o_w[:, :, :], ins["o_w"]),
                 (router_b[:, :], ins["router_b"].broadcast_to((P, EXPERTS))),
                 (v_b[:, :], ins["v_b"].broadcast_to((P, HEADS * HD)))]
        loads += [(rows[:, i, :], ins["rows"][i:i + 1, :].broadcast_to((P, P))) for i in range(4)]
        ALL_IN = 16 * len(loads)
        first_loads = [(cols[:, :], ins["cols"]), (pos[:, :], ins["c_pos"].broadcast_to((P, SEQ)))]

        @block.sync
        def _(sp):
            def load_x(i):
                sp.dma_start(xin[:, :, :], ins["x"][bass.ds(i, 1), :, :].rearrange("o (i p) d -> p (o i) d", p=P)
                             ).then_inc(x_in, 16)

            for dst, src in first_loads:
                sp.dma_start(dst, src).then_inc(first_in, 16)
            load_x(0)
            for dst, src in loads:
                sp.dma_start(dst, src).then_inc(weights_in, 16)
            part_end(sp, 1)
            with sp.Fori(0, BATCH) as b:
                part_end(sp, PARTS * b + 2)
                load_x(b + 1)

                def load_pair(pair, buf):
                    sp.dma_start(w_pair[buf][:, :, :], ins["w_pairs"][bass.ds(pair, 1), :, :, :].rearrange(
                        "o p s n -> p (o s) n")).then_inc(w_pair_in[buf], 16)

                load_pair(0, 0)
                load_pair(1, 1)
                with sp.Fori(0, PAIRS // 2 - 1) as r:
                    for k in range(2):
                        sp.wait_ge(w_pair_split, SPLITS * b + 2 * r + k + 1)
                        sp.sem_inc(passed, 1)
                        load_pair(2 * r + 2 + k, k)
                sp.wait_ge(w_pair_split, SPLITS * b + PAIRS - 1)
                sp.sem_inc(passed, 1)
                load_pair(PAIRS, 0)
                part_end(sp, PARTS * b + 3)
                for k in range(SLOTS):
                    sp.dma_start(w12[k][:, :, :], ins["w12"][k, :, :, :]).then_inc(w12_in[k], 16)
                with sp.Fori(1, EXPERTS // SLOTS) as r:
                    for k in range(SLOTS):
                        sp.wait_ge(w12_split, b * EXPERTS + (r - 1) * SLOTS + k + 1)
                        sp.sem_inc(passed, 1)
                        sp.dma_start(w12[k][:, :, :], ins["w12"][bass.ds(r * SLOTS + k, 1), :, :, :].rearrange(
                            "o p s n -> p (o s) n")).then_inc(w12_in[k], 16)
                sp.wait_ge(v_taken, V_OUTS * (b + 1) + 2)
                sp.dma_start(out[bass.ds(b, 1), :, :].rearrange("o (i p) d -> p (o i) d", p=P), acc[:, :, :]
                             ).then_inc(y_stored, 16)
                part_end(sp, PARTS * b + 4)
            sp.wait_ge(x_in, 16 * (BATCH + 1))
            sp.wait_ge(y_stored, 16 * (BATCH + 1))

        def pool_copy(pool, dst, src):
            return pool.tensor_scalar(dst, src, 1.0, 0.0, ALU.mult, ALU.add)

        P_STEPS = 3

        @block.gpsimd
        def _(pool):
            for s, c in CREDITS:
                pool.sem_inc(s, c)
            pool.memset(nmb[:, :], 0.0)
            pool.memset(neg_half[:, :], -0.5)
            pool.memset(mean_of[:, :], 1.0 / P)
            pool.memset(ones[:, :], 1.0)
            pool.memset(hpad[:, 0:1], 0.0)
            pool.memset(hpad[:, SEQ + 1:SEQ + 2], 0.0)
            for i in range(2):
                pool.memset(q_max[i][1][0:HD, :].bitcast(F32), 0.0)
                pool.memset(k_low[i][1][0:HD, :].bitcast(F32), 0.0).then_inc(p_setup, 1)
            pool.wait_ge(p_setup, 2)
            for i in range(2):
                pool.memset(k_low[i][0][HD:HD + 1, :].bitcast(F32), 1.0)
                pool.memset(k_low[i][1][0:1, :].bitcast(F32), 1.0).then_inc(p_setup, 1)
            pool.wait_ge(p_setup, 4)
            part_end(pool, 1)

            def inverse_root(at, n, eps=EPS):
                pool.wait_ge(ms_ready, at)
                pool.sem_inc(passed, 1)
                pool.tensor_scalar(ms[:, 0:n], ms[:, 0:n], eps, None, ALU.add).then_inc(ms_plus, 1)
                pool.wait_ge(ms_plus, at)
                pool.tensor_tensor(rstd[:, 0:n], ms[:, 0:n], neg_half[:, 0:n], ALU.pow).then_inc(rstd_ready, 1)

            inverse_root(1, TILES)
            inverse_root(2, 1)
            with pool.Fori(0, BATCH) as b:
                steps = Steps(pool, p_step, b * P_STEPS)

                pool.wait_ge(tok_ready, 3 * b + 1)
                steps.link(pool.tensor_tensor(both(resid[:, :, :]), both(xin[:, :, :]), both(x0[:, :, :]), ALU.add))
                steps.link(pool.tensor_tensor(resid[:, :, :], resid[:, :, :],
                                              b_out_r.unsqueeze(1).broadcast_to((P, TILES, P)), ALU.add))
                inverse_root(root_at(b, R_CONV), 1)
                pool.wait_ge(delta_ready, b + 1)
                pool.sem_inc(passed, 1)
                with pool.Fori(0, STATES // 2) as r:
                    for k in range(2):
                        n = b * STATES + 2 * r + k
                        pool.wait_ge(b_taken, n + 2)
                        pool.wait_ge(scanned, n + 1)
                        pool.tensor_tensor(bx[:, k, :], du[:, :], b_rows[:, k, :], ALU.mult).then_inc(bx_ready, 1)
                inverse_root(root_at(b, R_GATED), TILES)
                part_end(pool, PARTS * b + 2)
                inverse_root(root_at(b, R_BOTH), TILES, 0.0)
                pool.wait_ge(y_stored, 16 * b + 16)
                pool.wait_ge(tok_ready, 3 * b + 2)
                pool.tensor_tensor(acc[:, :, :], xa[:, :, :], o_b_r.unsqueeze(1).broadcast_to((P, TILES, P)),
                                   ALU.add).then_inc(acc_ready, 1)

                def split_pair(s, turn_of, par):
                    pool.wait_ge(w_pair_in[par], 16 * (b * (SPLITS // 2 + (1 - par)) + turn_of + 1))
                    pool.wait_ge(proj_out, 10 * (b * PAIRS + s) + 8)
                    pool.sem_inc(passed, 1)
                    pool_copy(pool, w_pair_high[par][:, :, :], w_pair[par][:, :, :]).then_inc(w_pair_high_ready, 1)
                    pool.wait_ge(w_pair_high_ready, SPLITS * b + s + 1)
                    pool.tensor_tensor(w_pair_low[par][:, :, :], w_pair[par][:, :, :],
                                       w_pair_high[par][:, :, :].bitcast(F32), ALU.subtract).then_inc(w_pair_split, 1)
                    pool.wait_ge(w_pair_split, SPLITS * b + s + 1)

                def step(s, par, this, prev, prev2):
                    n = b * PAIRS + s
                    m = n - 1
                    copies = [(q_max[par][0][0:HD, :], roped[0:HD, 0, :]), (q_max[par][1][HD:P, :], roped[HD:P, 0, :]),
                              (k_high[par][0][HD:P, :], roped[0:HD, 1, :]), (k_high[par][1][HD:P, :], roped[HD:P, 1, :])]
                    for k in range(2 if this else 0):
                        pool.wait_ge(proj_taken, 10 * n + 4 * k + 4 + PROJ_BANKS)
                        pool.wait_ge(high_a, 4 * n + 1)
                        pool.wait_ge(low_ready, 3 * n + 1)
                        pool.wait_ge(high_p, 4 * n + 1)
                        pool.tensor_tensor(roped[:, k, :], turned[:, 2 * k, :], turned[:, 2 * k + 1, :], ALU.add
                                           ).then_inc(roped_ready, 1)
                        pool.wait_ge(roped_ready, 2 * n + k + 2)
                        for i in (2 * k, 2 * k + 1):
                            pool.sem_inc(passed, 1)
                            pool_copy(pool, *copies[i]).then_inc(high_p, 1)
                            pool.wait_ge(high_p, 4 * n + i + 2)
                            pool.sem_inc(passed, 1)
                    for kind, _, u in slots(prev, this):
                        if kind == "low":
                            if prev:
                                pool.wait_ge(p_added, ADDS * (m + 1) + adds_with(MX_FROM - 2))
                            pool.tensor_tensor(k_low[par][1][HD:P, :], roped[HD:P, 1, :],
                                               k_high[par][1][HD:P, :].bitcast(F32), ALU.subtract).then_inc(low_p, 1)
                            pool.wait_ge(low_p, n + 1)
                        if kind == "input" and u in (0, 3):
                            pool.wait_ge(p_added, ADDS * (m + 1) + adds_with(NORM_AFTER[u]))
                            pool.sem_inc(passed, 1)
                            inverse_root(root_at(b, R_NEXT if u == 0 else R_NEXT_ALL), TILES if u == 0 else 1)
                            pool.wait_ge(rstd_ready, root_at(b, R_NEXT if u == 0 else R_NEXT_ALL))
                        if kind != "add":
                            continue
                        c, j, q0 = ST[u]
                        at = q0 - HALF * c
                        if u == 0:
                            pool.wait_ge(blocks_taken, 2 * NU * m + 2 + 2)
                            pool.wait_ge(misc_taken, row_at(m, HALVES, not prev2) + 1)
                            pool.sem_inc(passed, 1)
                            pool_copy(pool, prob_sums[:, 1, 0, 0:P], probs[:, 0, 1, 0:P]).then_inc(p_added, 1)
                        if j > 0:
                            pool.wait_ge(blocks_taken, 2 * (NU * m + u + 1) + 2)
                            pool.wait_ge(p_added, ADDS * (m + 1) + adds_with(u) - 1)
                            total = prob_sums[:, 1, c, at:HALF]
                            before = probs[:, (u - 1) % RING, 1, at:HALF] if j == 1 else total
                            pool.tensor_tensor(total, before, probs[:, u % RING, 1, at:HALF], ALU.add).then_inc(p_added, 1)

                split_pair(0, 0, 0)
                split_pair(1, 0, 1)
                step(0, 0, True, False, False)
                step(1, 1, True, True, False)
                split_pair(2, 1, 0)
                pool.sem_inc(passed, 1)
                with pool.Fori(0, PAIRS // 2 - 1) as r:
                    for k in range(2):
                        step(2 * r + 2 + k, k, True, True, True)
                        split_pair(2 * r + 3 + k, r + 1 + k, 1 - k)
                step(PAIRS, 0, False, True, True)
                part_end(pool, PARTS * b + 3)
                inverse_root(root_at(b, R_OUT), TILES)
                pool.wait_ge(ms_ready, root_at(b, R_OUT))
                steps.link(pool.tensor_tensor(both(resid[:, :, :]), both(resid[:, :, :]), both(acc[:, :, :]), ALU.add))
                pool.wait_ge(tok_ready, 3 * b + 4)
                pool.tensor_tensor(both(resid[:, :, :]), both(resid[:, :, :]), both(an[:, :, :]), ALU.add
                                   ).then_inc(resid_ready, 1)
                pool.wait_ge(resid_ready, b + 1)
                pool.sem_inc(passed, 1)
                with pool.Fori(0, EXPERTS // SLOTS) as r:
                    for k in range(SLOTS):
                        e = b * EXPERTS + r * SLOTS + k
                        pool.wait_ge(w12_in[k], 16 * (b * (EXPERTS // SLOTS) + r + 1))
                        pool.wait_ge(down_done, HALVES * (e + 1))
                        pool.sem_inc(passed, 1)
                        pool_copy(pool, w12_high[k][:, :, :], w12[k][:, :, :]).then_inc(w12_high_ready, 1)
                        pool.wait_ge(w12_high_ready, e + 1)
                        pool.tensor_tensor(w12_low[k][:, :, :], w12[k][:, :, :], w12_high[k][:, :, :].bitcast(F32),
                                           ALU.subtract).then_inc(w12_split, 1)
                part_end(pool, PARTS * b + 4)


        @block.scalar
        def _(act):
            act.wait_ge(first_in, 16 * len(first_loads))
            act.activation(exp_a[:, :], cols[:, C_ALOG:C_ALOG + STATES], ACT.Exp).then_inc(a_setup, 1)
            act.wait_ge(v_setup, V_ANGLES)
            act.activation(sin_raw[:, :], turns[:, 0, :], ACT.Sin).then_inc(a_setup, 1)
            act.activation(cos_t[:, :], turns[:, 1, :], ACT.Sin).then_inc(a_setup, 1)
            part_end(act, 1)

            def input_projection(at, normed):
                act.wait_ge(v_norm, normed)
                for c in range(2):
                    act.wait_ge(a_out, at + c + 1)
                    act.activation(xnT_m[:, c * HALF:(c + 1) * HALF], ps[:, c, :], ACT.Identity, bias=x_shift[:, :],
                                   scale=x_scale[:, :]).then_inc(a_taken, 1)
                for c in range(2):
                    act.wait_ge(a_out, at + 2 + c + 1)
                    act.activation(hpad[:, 1 + c * HALF:1 + (c + 1) * HALF], ps[:, c, :], ACT.Identity,
                                   bias=cols[:, C_B_IN:C_B_IN + 1]).then_inc(a_taken, 1)

            input_projection(0, 1)
            with act.Fori(0, BATCH) as b:
                def take(k, n, dst, func, bias=0.0, scale=1.0):
                    act.wait_ge(a_out, b * A_OUTS + k + 1)
                    act.activation(dst, ps[0:n, k % 2, :], func, bias=bias, scale=scale).then_inc(a_taken, 1)

                def col(c, n=P):
                    return cols[0:n, c:c + 1]

                act.wait_ge(a_taken, b * A_OUTS + 4 + 2)
                act.activation(gate[:, :], hpad[:, 1:1 + SEQ], ACT.Silu).then_inc(a_step, 1)
                for c in range(2):
                    take(4 + c, P, hc[:, c * HALF:(c + 1) * HALF], ACT.Identity, col(C_CONV_B))
                act.wait_ge(v_norm, 2 * b + 2)
                act.wait_ge(a_taken, b * A_OUTS + 6 + 2)
                act.activation(h_act[:, :], hc[:, :], ACT.Silu, bias=nmb[:, 0:1], scale=rstd[:, 0:1]).then_inc(a_step, 1)
                act.preload_act_table(ACT.Exp)
                for c in range(2):
                    take(6 + c, DT_RANK, d1[:, c * HALF:(c + 1) * HALF], ACT.Identity, col(C_B_D1, DT_RANK))
                for c in range(2):
                    act.wait_ge(a_out, b * A_OUTS + 8 + c + 1)
                    act.activation(z_abs[:, c * HALF:(c + 1) * HALF], ps[:, c, :], ACT.Abs, bias=col(C_B_D2)
                                   ).then_inc(a_step, 1)
                    take(8 + c, P, z[:, c * HALF:(c + 1) * HALF], ACT.Identity, col(C_B_D2))
                act.wait_ge(a_step, A_STEPS * b + 4)
                act.activation(z_abs[:, :], z_abs[:, :], ACT.Exp, scale=-1.0).then_inc(a_step, 1)
                act.wait_ge(a_step, A_STEPS * b + 5)
                act.activation(sp_log[:, :], z_abs[:, :], ACT.Ln, bias=1.0).then_inc(a_step, 1)
                act.sem_inc(passed, 1)
                act.preload_act_table(ACT.Exp)
                for c in range(2):
                    take(10 + c, 96, bc3[:, c * HALF:(c + 1) * HALF], ACT.Identity)
                with act.Fori(0, STATES // 2) as r:
                    for k in range(2):
                        n = b * STATES + 2 * r + k
                        act.wait_ge(b_bcast, n + 1)
                        act.wait_ge(bx_ready, n + 1)
                        act.activation(b_rows[:, k, :], banks(2), ACT.Copy).then_inc(b_taken, 1)
                        act.wait_ge(delta_ready, b + 1)
                        act.wait_ge(scanned, n + 1)
                        act.sem_inc(passed, 1)
                        act.activation(decay[:, k, :], delta[:, :], ACT.Exp,
                                       scale=neg_a[:, bass.ds(2 * r + k, 1)]).then_inc(decay_ready, 1)
                for c in range(2):
                    take(12 + c, P, gT[:, c * HALF:(c + 1) * HALF], ACT.Identity)
                part_end(act, PARTS * b + 2)
                for c in range(2):
                    take(14 + c, P, xnT[:, c * HALF:(c + 1) * HALF], ACT.Identity)
                act.wait_ge(a_taken, b * A_OUTS + 16 + 2)
                act.activation(xn_high[:, :], xnT[:, :], ACT.Copy).then_inc(xn_high_ready, 1)

                def keep_factors(m, c):
                    act.wait_ge(spread, 2 * m + c + 1)
                    act.wait_ge(ctx_ready, 2 * m + c + 4)
                    act.activation(factors[:, :], ps[:, 7, :], ACT.Copy).then_inc(factors_ready, 1)

                def step(s, par, this, prev, prev2):
                    n = b * PAIRS + s
                    m = n - 1
                    if prev:
                        for c in range(HALVES):
                            act.wait_ge(misc_out, row_at(m, c, not prev2) + 1)
                            for h, at in enumerate(ROW_AT):
                                made = act.activation(q_max[1 - par][h][at:at + 1, c * HALF:(c + 1) * HALF],
                                                      ps[at:at + 1, 7, :], ACT.Copy, scale=-1.0)
                            made.then_inc(misc_taken, 1)

                    def high(k):
                        dst = (q_split, k_high)[k][par]
                        act.wait_ge(roped_ready, 2 * n + k + 2)
                        for h in range(2):
                            act.activation(dst[h][0:HD, :], roped[HD * h:HD * h + HD, k, :], ACT.Copy
                                           ).then_inc(high_a, 1)

                    if this:
                        high(0)
                    if this and not prev:
                        high(1)
                    for kind, h, u in slots(prev, this):
                        if kind == "st":
                            c, j, q0 = ST[u]
                            w = HALF * (c + 1) - q0
                            act.wait_ge(blocks_out, 2 * (NU * m + u) + h + 1)
                            used = u + NU - RING
                            behind = u < RING
                            act.wait_ge(pv_out, NU * (m + 1 - behind) + used % NU + 1)
                            act.wait_ge((v_added, p_added)[h], ADDS * (m + 1 - behind) + adds_with(used % NU))
                            act.activation(probs[:, u % RING, h, q0 - HALF * c:HALF], ps[:, 4 + h, 0:w], ACT.Exp,
                                           scale=SCALE).then_inc(blocks_taken, 1)
                            if this and h == 1 and u == 1:
                                high(1)

                        elif kind == "scale" and (h == 0 or prev2):
                            keep_factors(m - h, h)

                step(0, 0, True, False, False)
                step(1, 1, True, True, False)
                with act.Fori(0, PAIRS // 2 - 1) as r:
                    for k in range(2):
                        step(2 * r + 2 + k, k, True, True, True)
                step(PAIRS, 0, False, True, True)
                keep_factors(b * PAIRS + PAIRS - 1, 1)
                part_end(act, PARTS * b + 3)
                for c in range(2):
                    take(16 + c, P, anT[:, c * HALF:(c + 1) * HALF], ACT.Identity)
                act.wait_ge(a_taken, b * A_OUTS + 18 + 2)
                act.activation(an_high[:, :], anT[:, :], ACT.Copy).then_inc(a_step, 1)
                act.wait_ge(aff_asked, b + 1)
                act.activation(aff[:, :, 0:ROUTED], logits[:, :, 0:ROUTED], ACT.Exp).then_inc(aff_ready, 1)
                input_projection(b * A_OUTS + 18, 2 * b + 3)

                def gelu(e, c):
                    k = HALVES * (b * EXPERTS + e) + c
                    act.wait_ge(hid_out, k + 1)
                    act.wait_ge(hg_ready, k + 1)
                    act.sem_inc(passed, 1)
                    act.activation(hid[:, c, :], ps[:, c, :], ACT.Gelu,
                                   bias=cols[:, bass.ds(C_B1 + e, 1)]).then_inc(hid_ready, 1)

                def high_of_hg(e, buf, c):
                    k = HALVES * (b * EXPERTS + e) + c
                    act.wait_ge(hg_ready, k + 1 + 2)
                    act.wait_ge(down_done, k + 1 + DOWN_FREE - HG_BUFS)
                    act.activation(hg_high[:, buf, :], hg[:, buf, :], ACT.Copy).then_inc(hg_high_ready, 1)

                act.sem_inc(passed, 1)
                act.preload_act_table(ACT.Gelu)
                gelu(0, 0)
                for c in range(2):
                    act.wait_ge(a_out, b * A_OUTS + 22 + c + 1)
                    act.activation(g3[:, c * HALF:(c + 1) * HALF], ps[0:96, GATE_BANK + c, :], ACT.Identity
                                   ).then_inc(g3_ready, 1)
                for c in range(2):
                    act.activation(gT32[:, c * HALF:(c + 1) * HALF], ps[0:96, GATE_BANK + c, :], ACT.Identity
                                   ).then_inc(a_taken, 1)
                with act.Fori(0, EXPERTS // 2 - 1) as r:
                    for u in range(HG_BUFS):
                        gelu(2 * r + (u + 1) // 2, (u + 1) % 2)
                        high_of_hg(2 * r + u // 2, u, u % 2)
                for u in range(HG_BUFS):
                    if u < HG_BUFS - 1:
                        gelu(EXPERTS - 2 + (u + 1) // 2, (u + 1) % 2)
                    high_of_hg(EXPERTS - 2 + u // 2, u, u % 2)
                act.wait_ge(down_done, UNITS * (b + 1) + DOWN_FREE)
                for c in range(2):
                    act.activation(moeT[:, c * HALF:(c + 1) * HALF], ps[:, 4 + c, :], ACT.Identity).then_inc(moe_taken, 1)
                part_end(act, PARTS * b + 4)

        @block.vector
        def _(dve):
            dve.wait_ge(first_in, 16 * len(first_loads))
            su = Steps(dve, v_setup)

            def slink(made):
                su.did(made)
                dve.wait_ge(v_setup, su.n)

            slink(dve.tensor_scalar(ang[:, :], pos[:, :], cols[:, C_THETA:C_THETA + 1], None, ALU.mult))
            for k in range(2):
                slink(dve.tensor_scalar(whole[:, :], ang[:, :], float(1 / (2 * np.pi)), 0.25 * k, ALU.mult, ALU.add))
                slink(dve.tensor_scalar(whole[:, :], whole[:, :], ROUNDER, ROUNDER, ALU.add, ALU.subtract))
                slink(dve.scalar_tensor_tensor(turns[:, k, :], whole[:, :], -TWO_PI_A, ang[:, :], ALU.mult, ALU.add))
                slink(dve.scalar_tensor_tensor(turns[:, k, :], whole[:, :], -TWO_PI_B, turns[:, k, :], ALU.mult, ALU.add))
                slink(dve.scalar_tensor_tensor(turns[:, k, :], whole[:, :], -TWO_PI_C, turns[:, k, :], ALU.mult, ALU.add))
                if k:
                    slink(dve.tensor_scalar(turns[:, k, :], turns[:, k, :], float(np.pi / 2), None, ALU.add))
                slink(dve.tensor_scalar(turns[:, k, :], turns[:, k, :], PI_BELOW, -PI_BELOW, ALU.min, ALU.max))
            assert su.n == V_ANGLES, su.n
            dve.wait_ge(weights_in, ALL_IN)
            dve.tensor_copy(identb[:, :], ident[:, :])
            dve.tensor_copy(masks[:, :, :], masks32[:, :, :])
            dve.tensor_copy(fold[:, :], fold32[:, :])
            dve.tensor_scalar(diag_d[:, :], ident[:, :], cols[:, C_D:C_D + 1], None, ALU.mult)
            dve.wait_ge(a_setup, 1)
            dve.tensor_scalar(neg_a[:, :], exp_a[:, :], -1.0, None, ALU.mult)
            dve.wait_ge(a_setup, 2)
            dve.tensor_scalar(sin_t[:, :], sin_raw[:, :], cols[:, C_SIGN:C_SIGN + 1], None, ALU.mult)
            part_end(dve, 1)
            def root(at, made):
                made.then_inc(ms_ready, 1)
                dve.wait_ge(rstd_ready, at)

            def moments(src, n):
                for i in range(n):
                    st.did(dve.bn_stats(stats[:, i, :], src(i)))
                st.wait()
                dve.sem_inc(passed, 1)
                for i in range(n):
                    st.did(dve.bn_aggr(mv[:, i, :], stats[:, i, :]))
                st.wait()

            def mean_squares(at):
                st.link(dve.tensor_tensor(ms[:, :], mv[:, :, 0], mv[:, :, 0], ALU.mult))
                root(at, dve.tensor_tensor(ms[:, :], ms[:, :], mv[:, :, 1], ALU.add))

            def normed(dst, src, last):
                for i in range(TILES):
                    made = dve.tensor_scalar(dst[:, i, :], src(i), mv[:, i, 0:1], rstd[:, i:i + 1],
                                             ALU.subtract, ALU.mult)
                    last(i, made)

            def signal_last(s):
                return lambda i, made: made.then_inc(s, 1) if i == TILES - 1 else None

            def input_norm(phase, i, at, made_before):
                if phase == 0:
                    dve.wait_ge(x_in, 16 * i + 16)
                    moments(lambda t: xin[:, t, :], TILES)
                    dve.tensor_copy(ms[:, :], mv[:, :, 1]).then_inc(ms_ready, 1)
                elif phase == 1:
                    dve.wait_ge(rstd_ready, at)
                    normed(x0, lambda t: xin[:, t, :], signal_last(tok_ready))
                    dve.wait_ge(tok_ready, made_before + 1)
                elif phase == 2:
                    for c in range(2):
                        st.did(dve.bn_stats(stats[:, c, :], both(x0[:, TPH * c:TPH * (c + 1), :])))
                    st.wait()
                    dve.sem_inc(passed, 1)
                    st.link(dve.bn_aggr(mv[:, 0, :], stats[:, 0:2, :].rearrange("p a b -> p (a b)")))
                    st.link(dve.tensor_copy(partial[:, 0:1], mv[:, 0, 0:1]))
                    dve.scalar_tensor_tensor(partial[:, 1:2], mv[:, 0, 0:1], mv[:, 0, 0:1], mv[:, 0, 1:2], ALU.mult,
                                             ALU.add).then_inc(partial_ready, 1)
                elif phase == 3:
                    dve.wait_ge(global_sum, i + 1)
                    st.link(dve.tensor_copy(glob[:, 0:2], ps[:, 2, 0:2]))
                    st.link(dve.tensor_scalar(glob[:, 2:3], glob[:, 0:1], glob[:, 0:1], -1.0, ALU.mult, ALU.mult))
                    dve.tensor_tensor(ms[:, 0:1], glob[:, 1:2], glob[:, 2:3], ALU.add).then_inc(ms_ready, 1)
                else:
                    dve.wait_ge(rstd_ready, at + 1)
                    st.did(dve.tensor_copy(x_scale[:, :], rstd[:, 0:1]))
                    dve.tensor_scalar(x_shift[:, :], glob[:, 0:1], rstd[:, 0:1], -1.0, ALU.mult, ALU.mult
                                      ).then_inc(v_norm, 1)

            st = Steps(dve, v_step)
            for phase in range(len(NORM_AFTER)):
                input_norm(phase, 0, 1, 0)
            assert st.n == V_FIRST, st.n
            with dve.Fori(0, BATCH) as b:
                st = Steps(dve, v_step, V_FIRST + b * V_STEPS)

                dve.wait_ge(a_taken, b * A_OUTS + 6 + 2)
                for c in range(2):
                    st.did(dve.bn_stats(stats[:, c, :], hc[:, c * HALF:(c + 1) * HALF]))
                st.wait()
                dve.sem_inc(passed, 1)
                st.link(dve.bn_aggr(mv[:, 0, :], stats[:, 0:2, :].rearrange("p a b -> p (a b)")))
                root(root_at(b, R_CONV), dve.tensor_copy(ms[:, 0:1], mv[:, 0, 1:2]))
                dve.tensor_scalar(nmb[:, 0:1], mv[:, 0, 0:1], rstd[:, 0:1], -1.0, ALU.mult, ALU.mult).then_inc(v_norm, 1)

                def three_parts(dst, src, high, rest, mid, last):
                    st.link(dve.tensor_copy(high, src))
                    st.did(dve.tensor_copy(dst[:, :, 0, :], high))
                    st.link(dve.tensor_tensor(rest, src, high, ALU.subtract))
                    st.link(dve.tensor_copy(mid, rest))
                    st.did(dve.tensor_copy(dst[:, :, 1, :], mid))
                    last(dve.tensor_tensor(dst[:, :, 2, :], rest, mid, ALU.subtract))

                dve.wait_ge(bc_out, b + 1)
                st.link(dve.tensor_tensor(bc_tok[:, :, :], ps[:, 4, 0:TILES * 2 * STATES].rearrange("p (i n) -> p i n", i=TILES),
                                          b_bc[:, :].unsqueeze(1).broadcast_to((P, TILES, 2 * STATES)), ALU.add))
                three_parts(bc_parts, bc_tok[:, :, :], bc_high[:, :, :], bc_rest[:, :, :], bc_mid[:, :, :],
                            lambda made: made.then_inc(bc_ready, 1))
                dve.wait_ge(a_step, A_STEPS * b + 6)
                st.link(dve.scalar_tensor_tensor(delta[:, :], z[:, :], 0.0, sp_log[:, :], ALU.max, ALU.add))
                dve.tensor_tensor(du[:, :], delta[:, :], h_act[:, :], ALU.mult).then_inc(delta_ready, 1)
                with dve.Fori(0, STATES // 2) as r:
                    for k in range(2):
                        n = b * STATES + 2 * r + k
                        dve.wait_ge(decay_ready, n + 1)
                        dve.wait_ge(bx_ready, n + 3)
                        dve.wait_ge(cs_ready, n + 1)
                        dve.tensor_tensor_scan(state[:, k, :], decay[:, k, :], bx[:, k, :], 0.0, ALU.mult, ALU.add
                                               ).then_inc(scanned, 1)
                        dve.wait_ge(scanned, n + 3)
                        dve.wait_ge(c_bcast, n + 1)
                        dve.wait_ge(cs_used, n + 1)
                        dve.tensor_tensor(cs[:, k, :], state[:, k, :], banks(4), ALU.mult).then_inc(cs_ready, 1)
                dve.wait_ge(cs_used, STATES * b + STATES + 2)
                dve.tensor_tensor(hc[:, :], banks(6), gate[:, :], ALU.mult).then_inc(yg_ready, 1)
                dve.wait_ge(v_out, V_OUTS * b + 2)
                g_ps = lambda i: ps[:, 2 + i // TPH, (i % TPH) * P:(i % TPH + 1) * P]
                moments(g_ps, TILES)
                root(root_at(b, R_GATED), dve.tensor_copy(ms[:, :], mv[:, :, 1]))
                normed(g_tok, g_ps, lambda i, made: made.then_inc(v_taken, 1) if i % TPH == TPH - 1 else None)
                for c in range(2):
                    dve.wait_ge(v_out, V_OUTS * b + 3 + c)
                    dve.wait_ge(p_step, P_STEPS * b + 2)
                    part = both(resid[:, TPH * c:TPH * (c + 1), :])
                    dve.tensor_tensor(part, part, ps[:, 2 + c, :], ALU.add).then_inc(v_taken, 1)
                part_end(dve, PARTS * b + 2)

                moments(lambda i: resid[:, i, :], TILES)
                root(root_at(b, R_BOTH), dve.tensor_scalar(ms[:, :], mv[:, :, 1], 1.0 + EPS, EPS * EPS, ALU.mult, ALU.add))
                for i in range(TILES):
                    st.did(dve.tensor_scalar(xa[:, i, :], resid[:, i, :], mv[:, i, 0:1], rstd[:, i:i + 1],
                                             ALU.subtract, ALU.mult))
                st.wait()
                made = dve.tensor_tensor(xa[:, :, :], xa[:, :, :], gamma1_r.unsqueeze(1).broadcast_to((P, TILES, P)),
                                         ALU.mult)
                made.then_inc(tok_ready, 1)

                dve.wait_ge(xn_high_ready, b + 1)
                dve.tensor_tensor(xn_low[:, :], xnT[:, :], xn_high[:, :].bitcast(F32), ALU.subtract).then_inc(xn_split, 1)

                def invert(m, c, i):
                    dve.wait_ge(misc_out, sum_at(m, c) + 1)
                    dve.wait_ge(ctx_ready, 2 * m + c + 4)
                    made = dve.reciprocal(inverse[:, i * PART:(i + 1) * PART], ps[:, 7, i * PART:(i + 1) * PART])
                    made.then_inc((inverted, misc_taken)[i == INV_PARTS - 1], 1)

                def scale(m, c):
                    dve.wait_ge(factors_ready, 2 * m + c + 1)
                    dve.wait_ge(pv_out, NU * (m + 1) + HALF_END[c])
                    dve.tensor_tensor(ctxT[:, c, :], ps[:, CTX_BANK[c], :], factors[:, :], ALU.mult).then_inc(ctx_ready, 1)

                def add_output(m, c, last):
                    dve.wait_ge(misc_out, op_at(m, c, last) + 1)
                    dve.wait_ge(acc_ready, b + 1)
                    dve.wait_ge(misc_taken, op_at(m, c, last) + 1)
                    part = both(acc[:, TPH * c:TPH * (c + 1), :])
                    dve.tensor_tensor(part, part, ps[:, 7, :], ALU.add).then_inc(misc_taken, 1)

                def low(k, n, par):
                    dve.wait_ge(high_a, 4 * n + 2 * k + 3)
                    dve.wait_ge(high_p, 4 * n + 2 * k + 3)
                    dst = (q_split, k_low)[k][par]
                    high0 = (q_split, k_high)[k][par][0]
                    high1 = (q_max, k_high)[k][par][1]
                    at0 = (HD, 0)[k]
                    dve.tensor_tensor(dst[0][at0:at0 + HD, :], roped[0:HD, k, :], high0[0:HD, :].bitcast(F32),
                                      ALU.subtract).then_inc(low_ready, 1)
                    if k == 0:
                        dve.tensor_tensor(dst[1][HD:P, :], roped[HD:P, k, :], high1[HD:P, :].bitcast(F32),
                                          ALU.subtract).then_inc(low_ready, 1)

                def step(s, par, this, prev, prev2):
                    n = b * PAIRS + s
                    m = n - 1
                    for k in range(8 if this else 0):
                        j, c = divmod(k, HALVES)
                        dve.wait_ge(proj_out, 10 * n + k + 21)
                        if c == 0 and j % 2 == 0:
                            dve.wait_ge(roped_ready, 2 * n + 1)
                        sl = slice(c * HALF, (c + 1) * HALF)
                        dve.scalar_tensor_tensor(
                            turned[:, j, sl], ps[:, k % PROJ_BANKS, :], cols[:, bass.ds(C_QK + 4 * s + j, 1)],
                            (cos_t, sin_t)[j % 2][:, sl], ALU.add, ALU.mult).then_inc(proj_taken, 1)
                        if prev2 and k in INV_AFTER:
                            invert(n - 2, 1, INV_AFTER.index(k))
                    for i in range(INV_PARTS if prev2 and not this else 0):
                        invert(n - 2, 1, i)
                    if prev2 and not prev:
                        scale(n - 2, 1)
                        add_output(n - 2, 1, True)
                    for c in range(HALVES if this else 0):
                        dve.wait_ge(proj_out, 10 * n + 8 + c + 21)
                        dve.tensor_tensor(
                            vals[par][:, TPH * c:TPH * (c + 1), :, :].rearrange("p i h d -> p i (h d)"),
                            ps[:, c, :].rearrange("p (i n) -> p i n", i=TPH),
                            v_b[:, bass.ds(P * s, P)].unsqueeze(1).broadcast_to((P, TPH, P)), ALU.add
                            ).then_inc(proj_taken, 1)
                    if this:
                        low(0, n, par)
                    for kind, h, u in slots(prev, this):
                        if kind == "mx":
                            i, k0, w = MX[u]
                            dve.wait_ge(scores_out, 2 * NU * n + NU * h + u + 1)
                            dve.tensor_reduce(tops[:, h, u:u + 1], ps[:, MX_BANK[u % 3], 0:w], AX_X, ALU.max
                                              ).then_inc(scores_taken, 1)
                            if u == NU - 1:
                                dve.wait_ge(scores_taken, 2 * NU * n + NU * h + NU + 3)
                                dve.tensor_copy(top[:, h, 0:TPH], tops[:, h, 0:TPH])
                                dve.tensor_tensor(top[:, h, TPH:TILES], tops[:, h, TPH:NU:2], tops[:, h, TPH + 1:NU:2],
                                                  ALU.max).then_inc(tops_ready, 1)
                        elif kind == "input":
                            input_norm(u, b + 1, root_at(b, R_NEXT), 3 * b + 2)
                        elif kind == "low":
                            low(1, n, par)
                        elif kind == "add":
                            c, j, q0 = ST[u]
                            at = q0 - HALF * c
                            if u == 0:
                                dve.wait_ge(blocks_taken, 2 * NU * m + 1 + 2)
                                dve.wait_ge(misc_taken, row_at(m, HALVES, not prev2) + 1)
                                dve.tensor_copy(prob_sums[:, 0, 0, 0:P], probs[:, 0, 0, 0:P]).then_inc(v_added, 1)
                            if j == 0:
                                continue
                            dve.wait_ge(blocks_taken, 2 * (NU * m + u) + 1 + 2)
                            dve.wait_ge(v_added, ADDS * (m + 1) + adds_with(u) - 1)
                            total = prob_sums[:, 0, c, at:HALF]
                            before = probs[:, (u - 1) % RING, 0, at:HALF] if j == 1 else total
                            dve.tensor_tensor(total, before, probs[:, u % RING, 0, at:HALF], ALU.add).then_inc(v_added, 1)
                        elif kind == "inv":
                            invert(m, 0, u)
                        elif kind == "scale" and (h == 0 or prev2):
                            scale(m - h, h)
                        elif kind == "op" and (h == 0 or prev2):
                            add_output(m - h, h, False)

                step(0, 0, True, False, False)
                step(1, 1, True, True, False)
                with dve.Fori(0, PAIRS // 2 - 1) as r:
                    for k in range(2):
                        step(2 * r + 2 + k, k, True, True, True)
                step(PAIRS, 0, False, True, True)
                step(PAIRS + 1, 1, False, False, True)
                dve.wait_ge(misc_taken, 6 * PAIRS * (b + 1) + 1)
                part_end(dve, PARTS * b + 3)

                moments(lambda i: acc[:, i, :], TILES)
                mean_squares(root_at(b, R_OUT))
                for i in range(TILES):
                    made = dve.scalar_tensor_tensor(an[:, i, :], acc[:, i, :], rstd[:, i:i + 1], gamma2_r, ALU.mult, ALU.mult)
                made.then_inc(tok_ready, 1)
                dve.wait_ge(a_step, A_STEPS * b + 7)
                dve.tensor_tensor(an_low[:, :], anT[:, :], an_high[:, :].bitcast(F32), ALU.subtract).then_inc(an_split, 1)
                wide = (P, TILES, ROUTED)
                dve.wait_ge(router_out, b + 1)
                st.link(dve.tensor_tensor(logits[:, :, :], ps[:, 6, 0:TILES * EXPERTS].rearrange("p (i e) -> p i e", i=TILES),
                                          router_b[:, :].unsqueeze(1).broadcast_to((P, TILES, EXPERTS)), ALU.add))
                st.did(dve.memset(aff[:, :, ROUTED:EXPERTS], 0.0))
                st.link(dve.tensor_reduce(red[:, 0, :], logits[:, :, 0:ROUTED], AX_X, ALU.max))
                dve.tensor_tensor(logits[:, :, 0:ROUTED], logits[:, :, 0:ROUTED],
                                  red[:, 0, :].unsqueeze(2).broadcast_to(wide), ALU.subtract).then_inc(aff_asked, 1)
                dve.wait_ge(aff_ready, b + 1)
                st.link(dve.tensor_reduce(red[:, 1, :], aff[:, :, 0:ROUTED], AX_X, ALU.add))
                st.link(dve.reciprocal(red[:, 0, :], red[:, 1, :]))
                st.link(dve.tensor_tensor(aff[:, :, 0:ROUTED], aff[:, :, 0:ROUTED],
                                          red[:, 0, :].unsqueeze(2).broadcast_to(wide), ALU.mult))
                full = (P, TILES, EXPERTS)
                dve.sem_inc(passed, 1)
                for i in range(TILES):
                    st.did(dve.max(big8[:, i, :], aff[:, i, 0:ROUTED]))
                st.wait()
                third = big8[:, :, TOP - 1:TOP].broadcast_to(full)
                st.did(dve.tensor_tensor(above[:, :, :], aff[:, :, :], third, ALU.is_gt))
                st.link(dve.tensor_tensor(equal[:, :, :], aff[:, :, :], third, ALU.is_equal))
                st.did(dve.tensor_reduce(red[:, 1, :], above[:, :, :], AX_X, ALU.add))
                st.link(dve.tensor_tensor_scan(both(struck[:, :, :]), resets[:, :], both(equal[:, :, :]), 0.0,
                                               ALU.mult, ALU.add))
                st.link(dve.tensor_tensor(struck[:, :, :], struck[:, :, :], red[:, 1, :].unsqueeze(2).broadcast_to(full),
                                          ALU.add))
                st.link(dve.scalar_tensor_tensor(both(struck[:, :, :]), both(struck[:, :, :]), TOP + 0.5,
                                                 both(equal[:, :, :]), ALU.is_lt, ALU.mult))
                st.link(dve.tensor_tensor(struck[:, :, :], struck[:, :, :], above[:, :, :], ALU.add))
                st.link(dve.tensor_tensor(struck[:, :, :], struck[:, :, :], aff[:, :, :], ALU.mult))
                st.link(dve.memset(struck[:, :, ROUTED:EXPERTS], 1.0))
                three_parts(gates, struck[:, :, :], g_high[:, :, :], g_rest[:, :, :], g_mid[:, :, :],
                            lambda made: made.then_inc(gates_ready, 1))
                assert st.n == V_STEPS, st.n

                def gated(e, buf, c):
                    k = HALVES * (b * EXPERTS + e) + c
                    dve.wait_ge(hid_ready, k + 3)
                    dve.wait_ge(gate_out, k + 1)
                    dve.wait_ge(hg_low_ready, k + 1)
                    dve.tensor_tensor(hg[:, buf, :], hid[:, c, :], ps[:, 2 + c, :], ALU.mult).then_inc(hg_ready, 1)

                def low_of_hg(e, buf, c):
                    k = HALVES * (b * EXPERTS + e) + c
                    dve.wait_ge(hg_high_ready, k + 1)
                    dve.tensor_tensor(hg_low[:, buf, :], hg[:, buf, :], hg_high[:, buf, :].bitcast(F32), ALU.subtract
                                      ).then_inc(hg_low_ready, 1)

                gated(0, 0, 0)
                with dve.Fori(0, EXPERTS // 2 - 1) as r:
                    for u in range(HG_BUFS):
                        gated(2 * r + (u + 1) // 2, (u + 1) % HG_BUFS, (u + 1) % 2)
                        low_of_hg(2 * r + u // 2, u, u % 2)
                for u in range(HG_BUFS):
                    if u < HG_BUFS - 1:
                        gated(EXPERTS - 2 + (u + 1) // 2, u + 1, (u + 1) % 2)
                    low_of_hg(EXPERTS - 2 + u // 2, u, u % 2)
                for c in range(2):
                    dve.wait_ge(v_out, V_OUTS * b + 5 + c)
                    dve.wait_ge(resid_ready, b + 1)
                    sl = slice(TPH * c, TPH * (c + 1))
                    dve.tensor_tensor(both(acc[:, sl, :]), both(resid[:, sl, :]), ps[:, 2 + c, :], ALU.add
                                      ).then_inc(v_taken, 1)
                part_end(dve, PARTS * b + 4)

        @block.tensor
        def _(pe):
            part_end(pe, 1)

            def global_sums(i):
                pe.wait_ge(partial_ready, i + 1)
                pe.matmul(ps[:, 2, 0:2], mean_of[:, :], partial[:, :], start=True, stop=True).then_inc(global_sum, 1)

            def turn(src, bank, n=P):
                for i in range(TPH):
                    made = pe.transpose(ps[0:n, bank, i * P:(i + 1) * P], src(i), ident[:, :])
                return made

            def cut(t, c, shift=0):
                return t[:, c * HALF + shift:(c + 1) * HALF + shift]

            def parts_product(o, w_high, w_low, x_high, x_low, first, last):
                pe.matmul(o, w_high, x_high, start=first, stop=False, skip_group_check=True)
                pe.matmul(o, w_high, x_low, start=False, stop=False, skip_group_check=True)
                return pe.matmul(o, w_low, x_high, start=False, stop=last, skip_group_check=True)

            def input_projection(at, made):
                pe.wait_ge(tok_ready, made)
                for c in range(2):
                    pe.wait_ge(a_taken, at + c + 1)
                    turn(lambda i: x0[:, TPH * c + i, :], c).then_inc(a_out, 1)
                pe.wait_ge(a_taken, at + 2 + 2)
                for c in range(2):
                    pe.matmul(ps[:, c, :], w_in[:, :], cut(xnT_m, c), start=True, stop=True).then_inc(a_out, 1)

            global_sums(0)
            input_projection(0, 1)
            with pe.Fori(0, BATCH) as b:
                def a_bank(k):
                    pe.wait_ge(a_taken, b * A_OUTS + k + 1)

                def v_bank(k):
                    pe.wait_ge(v_taken, b * V_OUTS + k + 1)

                def halves(k, n, lhs, rhs, taps=1):
                    for c in range(2):
                        a_bank(k + c)
                        for t in range(taps):
                            made = pe.matmul(ps[0:n, c, :], lhs(t), rhs(c, t), start=(t == 0), stop=(t == taps - 1))
                        made.then_inc(a_out, 1)

                pe.wait_ge(a_taken, b * A_OUTS + 4 + 2)
                halves(4, P, lambda t: w_conv[:, t, :], lambda c, t: cut(hpad, c, t), 3)
                pe.wait_ge(a_step, A_STEPS * b + 2)
                halves(6, DT_RANK, lambda t: w_d1[:, :], lambda c, t: cut(h_act, c))
                for c in range(2):
                    pe.matmul(ps[:, 6 + c, :], diag_d[:, :], cut(h_act, c), start=True, stop=False, skip_group_check=True)
                pe.wait_ge(a_taken, b * A_OUTS + 8 + 2)
                halves(8, P, lambda t: w_d2[:, :], lambda c, t: cut(d1, c))
                for i in range(TILES):
                    made = pe.matmul(ps[:, 4, i * 2 * STATES:(i + 1) * 2 * STATES], h_act[:, i * P:(i + 1) * P], w_bc[:, :],
                                     start=True, stop=True)
                made.then_inc(bc_out, 1)
                pe.wait_ge(bc_ready, b + 1)
                for c in range(2):
                    a_bank(10 + c)
                    turn(lambda i: bc_parts[:, TPH * c + i, :, :].rearrange("p a n -> p (a n)"), c, 96).then_inc(a_out, 1)
                pe.wait_ge(a_taken, b * A_OUTS + 12 + 2)
                pe.sem_inc(passed, 1)

                def broadcast_b(i):
                    pe.wait_ge(b_taken, b * STATES + i + 1)
                    for c in range(2):
                        made = pe.matmul(ps[:, 2 + c, :], fold[:, bass.ds(i, 1)].broadcast_to((96, P)),
                                         cut(bc3, c), start=True, stop=True)
                    made.then_inc(b_bcast, 1)

                def broadcast_c(i):
                    pe.wait_ge(cs_ready, b * STATES + i + 2)
                    for c in range(2):
                        made = pe.matmul(ps[:, 4 + c, :], fold[:, bass.ds(STATES + i, 1)].broadcast_to((96, P)),
                                         cut(bc3, c), start=True, stop=True)
                    made.then_inc(c_bcast, 1)

                def add_state(i, k):
                    pe.wait_ge(cs_ready, b * STATES + i + 3)
                    for c in range(2):
                        made = pe.matmul(ps[:, 6 + c, :], ident[:, :], cut(cs[:, k, :], c), start=False, stop=False,
                                         skip_group_check=True)
                    made.then_inc(cs_used, 1)

                broadcast_b(0)
                broadcast_b(1)
                broadcast_c(0)
                with pe.Fori(0, STATES // 2 - 1) as r:
                    for k in range(2):
                        broadcast_b(2 * r + k + 2)
                        broadcast_c(2 * r + k + 1)
                        add_state(2 * r + k, k)
                broadcast_c(STATES - 1)
                add_state(STATES - 2, 0)
                add_state(STATES - 1, 1)
                pe.wait_ge(yg_ready, b + 1)
                for c in range(2):
                    v_bank(c)
                    turn(lambda i: hc[:, (TPH * c + i) * P:(TPH * c + i + 1) * P], 2 + c).then_inc(v_out, 1)
                for c in range(2):
                    pe.wait_ge(v_taken, b * V_OUTS + c + 1 + 2)
                    a_bank(12 + c)
                    turn(lambda i: g_tok[:, TPH * c + i, :], c).then_inc(a_out, 1)
                for c in range(2):
                    pe.wait_ge(a_taken, b * A_OUTS + 12 + c + 1 + 2)
                    v_bank(2 + c)
                    for i in range(TPH):
                        made = pe.matmul(ps[:, 2 + c, i * P:(i + 1) * P], gT[:, (TPH * c + i) * P:(TPH * c + i + 1) * P],
                                         w_out[:, :], start=True, stop=True)
                    made.then_inc(v_out, 1)
                part_end(pe, PARTS * b + 2)

                pe.wait_ge(tok_ready, 3 * b + 2)
                for c in range(2):
                    a_bank(14 + c)
                    turn(lambda i: xa[:, TPH * c + i, :], c).then_inc(a_out, 1)
                pe.wait_ge(xn_split, b + 1)

                def max_rows(m, c, first):
                    if c == 0:
                        pe.wait_ge(tops_ready, 2 * m + 2)
                    pe.wait_ge(misc_taken, row_at(m, c, first) + 1)
                    for i in range(TPH):
                        at = TPH * c + i
                        for h, row in enumerate(ROW_AT):
                            made = pe.matmul(ps[row:row + HD, 7, i * P:(i + 1) * P],
                                             top[:, h, at:at + 1].broadcast_to((P, HD)), ident[:, :],
                                             start=True, stop=True)
                    made.then_inc(misc_out, 1)

                def prob_sum(m, c):
                    done = ADDS * (m + 1) + adds_with(HALF_END[c] - 1)
                    pe.wait_ge(v_added, done)
                    pe.wait_ge(p_added, done)
                    pe.wait_ge(misc_taken, sum_at(m, c) + 1)
                    for g in range(4):
                        at = SUMS * (g % 2)
                        made = pe.matmul(ps[QUARTER * g:QUARTER * (g + 1), 7, 0:SUMS], ones[:, :],
                                         prob_sums[:, g // 2, c, at:at + SUMS], start=True, stop=True)
                    made.then_inc(misc_out, 1)

                def spread_inverses(m, c, last):
                    pe.wait_ge(inverted, 2 * m + c + 2)
                    pe.wait_ge(misc_taken, op_at(m, c, last) + 1)
                    for z in range(2):
                        for h in range(2):
                            made = pe.matmul(ps[HD * h:HD * (h + 1), 7, z * SUMS:(z + 1) * SUMS],
                                             pick_quarter[:, 2 * h + z, :], inverse[:, :], start=True, stop=True)
                    made.then_inc(spread, 1)

                def output(m, pair, c, last):
                    pe.wait_ge(ctx_ready, 2 * m + 4 + c + 1)
                    pe.wait_ge(misc_taken, op_at(m, c, last) + 1)
                    for i in range(TPH):
                        made = pe.matmul(ps[:, 7, i * P:(i + 1) * P], ctxT[:, c, i * P:(i + 1) * P],
                                         o_w[:, bass.ds(pair, 1), :].rearrange("p o n -> p (o n)"), start=True, stop=True)
                    made.then_inc(misc_out, 1)

                def step(s, par, this, prev, prev2):
                    n = b * PAIRS + s
                    m = n - 1
                    if this:
                        pe.wait_ge(w_pair_split, SPLITS * b + s + 1)
                    for k in range(8):
                        j, c = divmod(k, HALVES)
                        if this:
                            pe.wait_ge(proj_taken, 10 * n + k + 1)
                            if k == 0:
                                pe.wait_ge(ctx_ready, 2 * n + 1)
                            if k == 1:
                                pe.wait_ge(scores_taken, 2 * NU * n + 3)
                            parts_product(ps[:, k % PROJ_BANKS, :], w_pair_high[par][:, j, :], w_pair_low[par][:, j, :],
                                          cut(xn_high, c), cut(xn_low, c), True, True).then_inc(proj_out, 1)
                        if prev2 and k == SUM_AFTER:
                            prob_sum(n - 2, 1)
                        if prev and k in ROWS_AFTER:
                            max_rows(m, ROWS_AFTER.index(k), not prev2)
                    if prev2 and not prev:
                        spread_inverses(n - 2, 1, True)
                        output(n - 2, s - 2, 1, True)
                    if this:
                        for c in range(HALVES):
                            pe.wait_ge(proj_taken, 10 * n + 8 + c + 1)
                            for i in range(TPH):
                                at = TPH * c + i
                                made = pe.matmul(ps[:, c, i * P:(i + 1) * P], xnT[:, at * P:(at + 1) * P],
                                                 v_w[:, bass.ds(P * s, P)], start=True, stop=True)
                            made.then_inc(proj_out, 1)
                    for kind, h, u in slots(prev, this):
                        if kind == "st":
                            c, j, q0 = ST[u]
                            w = HALF * (c + 1) - q0
                            if u == 0:
                                pe.wait_ge(misc_taken, row_at(m, HALVES, not prev2) + 1)
                                pe.wait_ge(low_ready, 3 * m + 4)
                                pe.wait_ge(low_p, m + 1)
                            pe.wait_ge(blocks_taken, 2 * (NU * m + u) + h + 1)
                            o = ps[:, 4 + h, 0:w]
                            own = q0 == P * j
                            rows_k = slice(0, HD + 1) if h == 0 else slice(0, P)
                            pe.matmul(o, k_high[1 - par][h][:, j * P:(j + 1) * P], q_split[1 - par][h][:, q0:q0 + w],
                                      start=True, stop=False)
                            made = pe.matmul(o, k_low[1 - par][h][rows_k, j * P:(j + 1) * P],
                                             q_max[1 - par][h][rows_k, q0:q0 + w], start=False, stop=not own)
                            if own:
                                made = pe.matmul(o[:, 0:P], identb[:, :], masks[:, 1, :], start=False, stop=True)
                            made.then_inc(blocks_out, 1)
                        elif kind == "pv":
                            c, j, q0 = ST[u]
                            at = q0 - HALF * c
                            if u == 0:
                                pe.wait_ge(proj_taken, 10 * n + (9 if this else 0) + PROJ_BANKS)
                            if u == HALF_START[1]:
                                pe.wait_ge(ctx_ready, 2 * m + 4)
                            pe.wait_ge(blocks_taken, 2 * (NU * m + u + 1) + 2)
                            for g in range(2):
                                made = pe.matmul(ps[HD * g:HD * (g + 1), CTX_BANK[c], at:HALF], vals[1 - par][:, j, g, :],
                                                 probs[:, u % RING, g, at:HALF], start=(j == 0),
                                                 stop=(u == HALF_END[c] - 1), skip_group_check=True)
                            made.then_inc(pv_out, 1)
                        elif kind == "mx":
                            i, k0, w = MX[u]
                            if u == 0:
                                pe.wait_ge(proj_taken, 10 * n + 10 + PROJ_BANKS)
                                pe.wait_ge(high_a, 4 * n + 5)
                                pe.wait_ge(high_p, 4 * n + 5)
                                pe.wait_ge(low_ready, 3 * n + 3)
                            pe.wait_ge(scores_taken, 2 * NU * n + NU * h + u + 1)
                            o = ps[:, MX_BANK[u % 3], 0:w]
                            own = k0 + w == P * (i + 1)
                            made = pe.matmul(o, q_split[par][h][:, i * P:(i + 1) * P], k_high[par][h][:, k0:k0 + w],
                                             start=True, stop=not own)
                            if own:
                                made = pe.matmul(o[:, w - P:w], identb[:, :], masks[:, 0, :], start=False, stop=True)
                            made.then_inc(scores_out, 1)
                        elif kind == "input" and u == 3:
                            global_sums(b + 1)
                        elif kind == "sum":
                            prob_sum(m, 0)
                        elif kind == "spread" and (h == 0 or prev2):
                            spread_inverses(m - h, h, False)
                        elif kind == "op" and (h == 0 or prev2):
                            output(m - h, s - 1 - h, h, False)

                step(0, 0, True, False, False)
                step(1, 1, True, True, False)
                with pe.Fori(0, PAIRS // 2 - 1) as r:
                    for k in range(2):
                        step(2 * r + 2 + k, k, True, True, True)
                step(PAIRS, 0, False, True, True)
                step(PAIRS + 1, 1, False, False, True)
                part_end(pe, PARTS * b + 3)

                pe.wait_ge(tok_ready, 3 * b + 4)
                for c in range(2):
                    a_bank(16 + c)
                    turn(lambda i: an[:, TPH * c + i, :], c).then_inc(a_out, 1)
                pe.wait_ge(a_taken, b * A_OUTS + 18 + 2)
                for i in range(TILES):
                    made = pe.matmul(ps[:, 6, i * EXPERTS:(i + 1) * EXPERTS], anT[:, i * P:(i + 1) * P], w_router[:, :],
                                     start=True, stop=True)
                made.then_inc(router_out, 1)
                input_projection(b * A_OUTS + 18, 3 * b + 3)
                def hidden(e, slot, c):
                    k = HALVES * (b * EXPERTS + e) + c
                    if c == 0:
                        pe.wait_ge(w12_split, b * EXPERTS + e + 1)
                    pe.wait_ge(hid_ready, k + 1)
                    parts_product(ps[:, c, :], w12_high[slot][:, 0, :], w12_low[slot][:, 0, :], cut(an_high, c),
                                  cut(an_low, c), True, True).then_inc(hid_out, 1)

                def gate_row(e, c):
                    k = HALVES * (b * EXPERTS + e) + c
                    pe.wait_ge(hg_ready, k + 1)
                    pe.matmul(ps[:, 2 + c, :], fold[:, bass.ds(e, 1)].broadcast_to((96, P)), cut(g3, c), start=True,
                              stop=True).then_inc(gate_out, 1)

                def up(e, slot, c):
                    hidden(e, slot, c)
                    gate_row(e, c)

                def down(e, slot, c):
                    k = HALVES * (b * EXPERTS + e) + c
                    buf = (HALVES * slot + c) % HG_BUFS
                    pe.wait_ge(hg_low_ready, k + 1 + HG_BUFS)
                    parts_product(ps[:, 4 + c, :], w12_high[slot][:, 1, :], w12_low[slot][:, 1, :], hg_high[:, buf, :],
                                  hg_low[:, buf, :], False, False).then_inc(down_done, 1)

                pe.wait_ge(an_split, b + 1)
                pe.wait_ge(a_taken, b * A_OUTS + 22 + 2)
                for c in range(HALVES):
                    hidden(0, 0, c)
                pe.wait_ge(gates_ready, b + 1)
                for c in range(2):
                    a_bank(22 + c)
                    turn(lambda i: gates[:, TPH * c + i, :, :].rearrange("p a e -> p (a e)"), GATE_BANK + c, 96
                         ).then_inc(a_out, 1)
                pe.wait_ge(g3_ready, HALVES * (b + 1))
                for c in range(HALVES):
                    gate_row(0, c)
                for k in range(HALVES, DOWN_LAG):
                    up(k // HALVES, k // HALVES, k % HALVES)
                pe.wait_ge(a_taken, b * A_OUTS + 24 + 2)
                for c in range(2):
                    pe.matmul(ps[:, 4 + c, :], b2_all[:, :], gT32[:, c * HALF:(c + 1) * HALF], start=True,
                              stop=False, skip_group_check=True)
                with pe.Fori(0, EXPERTS // SLOTS - 1) as r:
                    for i in range(HALVES * SLOTS):
                        ahead = i + DOWN_LAG
                        up(SLOTS * r + ahead // HALVES, ahead // HALVES % SLOTS, ahead % HALVES)
                        down(SLOTS * r + i // HALVES, i // HALVES, i % HALVES)
                for i in range(HALVES * SLOTS):
                    ahead = i + DOWN_LAG
                    if ahead < HALVES * SLOTS:
                        up(EXPERTS - SLOTS + ahead // HALVES, ahead // HALVES, ahead % HALVES)
                    down(EXPERTS - SLOTS + i // HALVES, i // HALVES, i % HALVES)
                for c in range(2):
                    pe.wait_ge(moe_taken, 2 * b + c + 1)
                    v_bank(4 + c)
                    turn(lambda i: moeT[:, (TPH * c + i) * P:(TPH * c + i + 1) * P], 2 + c).then_inc(v_out, 1)
                part_end(pe, PARTS * b + 4)


def constants():
    eye = np.eye(P, dtype=np.float32)
    q, k = np.arange(P)[:, None], np.arange(P)[None, :]
    masks = np.stack([np.where(k > q, MASKED, 0.0), np.where(k < q, MASKED, 0.0)], 1).astype(np.float32)
    fold = (np.arange(96)[:, None] % 32 == np.arange(32)[None, :]).astype(np.float32)
    quarters = np.zeros((P, 4, HD), np.float32)
    for g in range(4):
        quarters[QUARTER * g, g, :] = 1.0
    resets = (np.arange(TILES * EXPERTS) % EXPERTS != 0).astype(np.float32)[None]
    return dict(c_ident=eye, c_quarters=quarters, c_masks=masks, c_fold=fold,
                c_pos=np.arange(SEQ, dtype=np.float32)[None], c_resets=resets)


def kernel(**inputs):
    import concourse.bacc as bacc
    from concourse.bass_utils import run_bass_kernel_spmd

    x = {k: np.asarray(v) for k, v in inputs.items()}
    m = {k[len("L0_attn_"):]: v for k, v in x.items() if k.startswith("L0_attn_")}
    f = {k[len("L0_ffn_"):]: v for k, v in x.items() if k.startswith("L0_ffn_")}
    f32 = np.float32

    cols = np.zeros((P, NCOLS), f32)
    cols[:, C_B_IN], cols[:, C_CONV_B], cols[:, C_B_D2], cols[:, C_D] = m["b_in"], m["conv_b"], m["b_d2"], m["D"]
    cols[:DT_RANK, C_B_D1] = m["b_d1"]
    cols[:, C_THETA] = np.tile(f["theta"], P // f["theta"].shape[0])
    cols[:, C_SIGN] = np.where(np.arange(P) % HD < HD // 2, -1.0, 1.0)
    cols[:, C_ALOG:C_ALOG + STATES] = m["A_log"]
    cols[:, C_B1:C_B1 + ROUTED], cols[:, C_B1 + ROUTED] = f["re_b1"].T, f["sh_b1"]
    order = np.concatenate([np.arange(0, HD, 2), np.arange(1, HD, 2)])
    swapped = np.concatenate([np.arange(1, HD, 2), np.arange(0, HD, 2)])
    pick = [np.concatenate([HD * h + o for h in range(HEADS)]) for o in (order, swapped)]
    w_pairs = np.zeros((PAIRS, P, 4, P), f32)
    for j, name in enumerate("qk"):
        for i in range(2):
            w = f[name + "_w"][:, pick[i]].reshape(DM, PAIRS, P)
            w_pairs[:, :, 2 * j + i, :] = w.transpose(1, 0, 2)
            cols[:, C_QK + 2 * j + i::4] = f[name + "_b"][pick[i]].reshape(PAIRS, P).T
    rows = np.stack([m["b_out"], f["gamma1"], f["gamma2"], f["o_b"]])
    w12 = np.zeros((EXPERTS, P, 2, P), f32)
    w12[:ROUTED, :, 0], w12[ROUTED, :, 0] = f["re_w1"], f["sh_w1"]
    w12[:ROUTED, :, 1], w12[ROUTED, :, 1] = f["re_w2"], f["sh_w2"]
    router_w = np.zeros((DM, EXPERTS), f32)
    router_w[:, :ROUTED] = f["router_w"]
    router_b = np.zeros((1, EXPERTS), f32)
    router_b[0, :ROUTED] = f["router_b"]
    arrays = dict(
        x=np.concatenate([m["x"], m["x"][:1]]), w_in=m["w_in"].T, conv_w=m["conv_w"].transpose(1, 2, 0),
        w_bc=np.concatenate([m["w_B"].T, m["w_C"].T], 1),
        b_bc=np.concatenate([m["b_B"], m["b_C"]])[None], w_d1=m["w_d1"].T, w_d2=m["w_d2"].T, w_out=m["w_out"].T, cols=cols, rows=rows,
        w_pairs=np.concatenate([w_pairs, w_pairs[:1]]), v_w=f["v_w"], v_b=f["v_b"][None], o_w=f["o_w"].reshape(PAIRS, P, DM).transpose(1, 0, 2),
        w12=w12, b2=np.concatenate([f["re_b2"], f["sh_b2"][None]] * 3), router_w=router_w, router_b=router_b,
        **constants())
    nc = bacc.Bacc("TRN2", target_bir_lowering=False, num_devices=1)
    arrays = {"in_" + k: np.ascontiguousarray(v) for k, v in arrays.items()}
    ins = {k[3:]: nc.dram_tensor(k, v.shape, mybir.dt.from_np(v.dtype), kind="ExternalInput").ap()
           for k, v in arrays.items()}
    out = nc.dram_tensor("out_0", (BATCH, SEQ, DM), F32, kind="ExternalOutput").ap()
    program(nc, ins, out)
    r = run_bass_kernel_spmd(nc, [arrays], core_ids=[0])
    return r.results[0]["out_0"]
```
